# Optimizing a Trainium2 kernel written in Bass

```python
import numpy as np
import jax
import jax.numpy as jnp

def _softmax(x, axis=-1):
    return jax.nn.softmax(x, axis=axis)

def _gelu(x):
    return jax.nn.gelu(x, approximate=True)

def _silu(x):
    return jax.nn.silu(x)

def _sigmoid(x):
    return jax.nn.sigmoid(x)

def _layernorm(x, axis=-1, eps=1e-05):
    m = jnp.mean(x, axis=axis, keepdims=True)
    v = jnp.var(x, axis=axis, keepdims=True)
    return (x - m) / jnp.sqrt(v + eps)

def _scatter_add(tgt, idx, src, axis=0):
    return tgt.at[idx].add(src)

def _segment_sum(src, seg, n):
    return jax.ops.segment_sum(src, seg, n)
kernel_name = 'mk_decoder_postln_d4_seqx_r4_cfebd6'

def setup_inputs(seed: int=0):
    np.random.seed(seed)
    _w = jnp.asarray

    def _rec_inputs():
        import jax
        import jax.numpy as jnp
        _rk = jax.random.key(seed)
        x = -0.0002928 + 1 * jax.random.normal(jax.random.fold_in(_rk, 1), (4, 512, 256), jnp.float32)
        _lenS = 512 - jax.random.randint(jax.random.fold_in(_rk, 7), (4,), 0, max(1, 512 // 4) + 1, jnp.int32)
        _lenS2 = 1601 - jax.random.randint(jax.random.fold_in(_rk, 8), (4,), 0, max(1, 1601 // 4) + 1, jnp.int32)
        _ctx_1024P = jax.random.normal(jax.random.fold_in(_rk, 11), (4, 16, 256), jnp.float32)
        _ctx_1024c = jax.random.dirichlet(jax.random.fold_in(_rk, 511), 0.3 * jnp.ones((16,), jnp.float32), (4, 1601))
        _ctx_1024t = jnp.einsum('bsk,bkd->bsd', _ctx_1024c, _ctx_1024P)
        _ctx_1024t = _ctx_1024t * jax.lax.rsqrt(jnp.mean(jnp.square(_ctx_1024t)) + 1e-12) * 0.953939
        ctx_1024 = -1.39393e-06 + 0.999914 * (_ctx_1024t + 0.3 * jax.random.normal(jax.random.fold_in(_rk, 611), (4, 1601, 256), jnp.float32))
        return (x, ctx_1024)
    x, ctx_1024 = _rec_inputs()

    def _L0_attn_setup():
        import jax, jax.numpy as jnp
        import numpy as np
        B, S, D, H = (2, 512, 256, 16)
        HD = D // H
        FF = 1024
        NUM_ITERS = 8
        DT = 0.1
        LN_EPS = 1e-05

        def _ln(x, g, b):
            m = jnp.mean(x, axis=-1, keepdims=True)
            v = jnp.var(x, axis=-1, keepdims=True)
            return (x - m) * jax.lax.rsqrt(v + LN_EPS) * g + b

        def _forward(x, qkv_w, qkv_b, out_w, out_b, g_attn, b_attn, g1, b1, g2, b2, w_ctx, w_x, b_inl, ff_w1, ff_b1, ff_w2, ff_b2):
            b, s, d = x.shape
            xn = _ln(x, g_attn, b_attn)
            qkv = (xn @ qkv_w + qkv_b).reshape(b, s, 3, H, HD)
            qkv = jnp.transpose(qkv, (2, 0, 3, 1, 4))
            q, k, v = (qkv[0], qkv[1], qkv[2])
            scores = jnp.einsum('bhqd,bhkd->bhqk', q, k) / np.sqrt(HD).astype(np.float32)
            causal = jnp.triu(jnp.ones((s, s), dtype=bool), 1)
            scores = jnp.where(causal[None, None], -jnp.inf, scores)
            attn_w = jax.nn.softmax(scores, axis=-1)
            attn = jnp.einsum('bhqk,bhkd->bhqd', attn_w, v)
            attn = jnp.transpose(attn, (0, 2, 1, 3)).reshape(b, s, d)
            attn = attn @ out_w + out_b
            x = x + attn
            ctx = attn.reshape(b * s, d)
            xs = _ln(x, g1, b1).reshape(b * s, d)
            vs = jnp.zeros_like(xs)

            def step(carry, _):
                xs, vs = carry
                u = jnp.tanh(ctx @ w_ctx + xs @ w_x + b_inl)
                vn = vs + DT * (u - xs - vs)
                xn_ = xs + DT * vn
                return ((xn_, vn), None)
            (xs, vs), _ = jax.lax.scan(step, (xs, vs), None, length=NUM_ITERS)
            x = x + xs.reshape(b, s, d)
            h = _ln(x, g2, b2)
            h = jax.nn.gelu(h @ ff_w1 + ff_b1, approximate=False)
            x = x + (h @ ff_w2 + ff_b2)
            return x
        key = jax.random.key(seed)
        ks = jax.random.split(key, 16)

        def xav(k, shape):
            lim = np.sqrt(6.0 / (shape[0] + shape[1]))
            return jax.random.uniform(k, shape, minval=-lim, maxval=lim, dtype=jnp.float32)
        return {'x': jax.random.normal(ks[0], (B, S, D), dtype=jnp.float32), 'qkv_w': xav(ks[1], (D, 3 * D)), 'qkv_b': jnp.zeros((3 * D,), jnp.float32), 'out_w': xav(ks[2], (D, D)), 'out_b': jnp.zeros((D,), jnp.float32), 'g_attn': jnp.ones((D,), jnp.float32), 'b_attn': jnp.zeros((D,), jnp.float32), 'g1': jnp.ones((D,), jnp.float32), 'b1': jnp.zeros((D,), jnp.float32), 'g2': jnp.ones((D,), jnp.float32), 'b2': jnp.zeros((D,), jnp.float32), 'w_ctx': xav(ks[3], (D, D)), 'w_x': xav(ks[4], (D, D)), 'b_inl': jnp.zeros((D,), jnp.float32), 'ff_w1': xav(ks[5], (D, FF)), 'ff_b1': jnp.zeros((FF,), jnp.float32), 'ff_w2': xav(ks[6], (FF, D)), 'ff_b2': jnp.zeros((D,), jnp.float32)}
    _L0_attn_all = _L0_attn_setup()
    _L0_attn_in = {k: v for k, v in _L0_attn_all.items() if k in ('qkv_w', 'qkv_b', 'out_w', 'out_b', 'g_attn', 'b_attn', 'g1', 'b1', 'g2', 'b2', 'w_ctx', 'w_x', 'b_inl', 'ff_w1', 'ff_b1', 'ff_w2', 'ff_b2')}
    del _L0_attn_all

    def _L0_xattn_setup():
        import jax, jax.numpy as jnp
        import numpy as np
        QUERY_DIM = 256
        CONTEXT_DIM = 256
        HEADS = 8
        DIM_HEAD = 64
        INNER = HEADS * DIM_HEAD
        SCALE = DIM_HEAD ** (-0.5)
        key = jax.random.key(seed)
        ks = jax.random.split(key, 7)
        B, N, M = (2, 512, 512)
        x = jax.random.normal(ks[0], (B, N, QUERY_DIM), dtype=jnp.float32)
        context = jax.random.normal(ks[1], (B, M, CONTEXT_DIM), dtype=jnp.float32)
        Wq = jax.random.normal(ks[2], (QUERY_DIM, INNER), dtype=jnp.float32) * QUERY_DIM ** (-0.5)
        Wk = jax.random.normal(ks[3], (CONTEXT_DIM, INNER), dtype=jnp.float32) * CONTEXT_DIM ** (-0.5)
        Wv = jax.random.normal(ks[4], (CONTEXT_DIM, INNER), dtype=jnp.float32) * CONTEXT_DIM ** (-0.5)
        Wo = jax.random.normal(ks[5], (INNER, QUERY_DIM), dtype=jnp.float32) * INNER ** (-0.5)
        bo = jax.random.normal(ks[6], (QUERY_DIM,), dtype=jnp.float32) * 0.01
        return {'x': x, 'context': context, 'Wq': Wq, 'Wk': Wk, 'Wv': Wv, 'Wo': Wo, 'bo': bo}
    _L0_xattn_all = _L0_xattn_setup()
    _L0_xattn_in = {k: v for k, v in _L0_xattn_all.items() if k in ('Wq', 'Wk', 'Wv', 'Wo', 'bo')}
    del _L0_xattn_all

    def _L0_ffn_setup():
        import jax, jax.numpy as jnp
        import numpy as np
        IN_F = 256
        OUT_F = 256
        B, S = (8, 1024)

        def _pack_ternary(tern):
            enc = (tern + 1.0).astype(jnp.int32).reshape(-1)
            return (enc[0::4] | enc[1::4] << 2 | enc[2::4] << 4 | enc[3::4] << 6).astype(jnp.int32)
        key = jax.random.key(seed)
        kx, kw = jax.random.split(key)
        x = jax.random.normal(kx, (B, S, IN_F), dtype=jnp.float32)
        w = jax.random.normal(kw, (OUT_F, IN_F), dtype=jnp.float32) * 0.02
        scale = jnp.maximum(jnp.mean(jnp.abs(w)), 1e-05)
        wn = w / scale
        tern = jnp.sign(wn) * (jnp.abs(wn) > 0.5).astype(jnp.float32)
        packed = _pack_ternary(tern)
        bias = jnp.zeros((OUT_F,), dtype=jnp.float32)
        return {'x': x, 'packed_weight': packed, 'weight_scale': scale.reshape(1), 'bias': bias}
    _L0_ffn_all = _L0_ffn_setup()
    _L0_ffn_in = {k: v for k, v in _L0_ffn_all.items() if k in ('packed_weight', 'weight_scale', 'bias')}
    del _L0_ffn_all

    def _L1_attn_setup():
        import math
        import jax, jax.numpy as jnp
        import numpy as np
        D_MODEL = 256
        N_HEADS = 16
        D_K = D_MODEL // N_HEADS
        D_C = 64
        B, S = (2, 512)
        key = jax.random.key(seed)
        ks = jax.random.split(key, 7)
        sd = lambda fan_in: 1.0 / math.sqrt(fan_in)
        return {'x': jax.random.normal(ks[0], (B, S, D_MODEL), dtype=jnp.float32), 'W_dq': jax.random.uniform(ks[1], (D_MODEL, D_C), minval=-sd(D_MODEL), maxval=sd(D_MODEL), dtype=jnp.float32), 'W_uq': jax.random.uniform(ks[2], (D_C, N_HEADS * D_K), minval=-sd(D_C), maxval=sd(D_C), dtype=jnp.float32), 'W_dkv': jax.random.uniform(ks[3], (D_MODEL, D_C), minval=-sd(D_MODEL), maxval=sd(D_MODEL), dtype=jnp.float32), 'W_uk': jax.random.uniform(ks[4], (D_C, N_HEADS * D_K), minval=-sd(D_C), maxval=sd(D_C), dtype=jnp.float32), 'W_uv': jax.random.uniform(ks[5], (D_C, N_HEADS * D_K), minval=-sd(D_C), maxval=sd(D_C), dtype=jnp.float32), 'W_o': jax.random.uniform(ks[6], (N_HEADS * D_K, D_MODEL), minval=-sd(N_HEADS * D_K), maxval=sd(N_HEADS * D_K), dtype=jnp.float32)}
    _L1_attn_all = _L1_attn_setup()
    _L1_attn_in = {k: v for k, v in _L1_attn_all.items() if k in ('W_dq', 'W_uq', 'W_dkv', 'W_uk', 'W_uv', 'W_o')}
    del _L1_attn_all

    def _L1_xattn_setup():
        import jax, jax.numpy as jnp
        import numpy as np
        D_MODEL = 256
        N_HEADS = 16
        RANK = 128
        TOPK = 64
        D_HEAD = D_MODEL // N_HEADS
        SCALE = D_HEAD ** (-0.5)
        INIT_SCALE = 0.05

        def _lowrank_proj(x, U, V, b):
            return jnp.einsum('btr,dr->btd', jnp.einsum('btd,dr->btr', x, U), V) + b

        def _heads(x, B, T):
            return x.reshape(B, T, N_HEADS, D_HEAD).transpose(0, 2, 1, 3)

        def _topk_softmax(scores, k):
            B, H, L, S = scores.shape
            flat = scores.reshape(-1, S)
            vals, idx = jax.lax.top_k(flat, k)
            p = jax.nn.softmax(vals, axis=-1)
            rows = jnp.arange(flat.shape[0])[:, None]
            attn = jnp.zeros_like(flat).at[rows, idx].set(p)
            return attn.reshape(B, H, L, S)
        key = jax.random.key(seed)
        ks = jax.random.split(key, 11)
        B, L, S = (2, 512, 512)
        inp = {'q': jax.random.normal(ks[0], (B, L, D_MODEL), jnp.float32), 'k': jax.random.normal(ks[1], (B, S, D_MODEL), jnp.float32), 'v': jax.random.normal(ks[2], (B, S, D_MODEL), jnp.float32)}
        names = ['q', 'k', 'v', 'o']
        for i, n in enumerate(names):
            inp[f'U{n}'] = jax.random.normal(ks[3 + 2 * i], (D_MODEL, RANK), jnp.float32) * INIT_SCALE
            inp[f'V{n}'] = jax.random.normal(ks[4 + 2 * i], (D_MODEL, RANK), jnp.float32) * INIT_SCALE
            inp[f'b{n}'] = jnp.zeros((D_MODEL,), jnp.float32)
        return inp
    _L1_xattn_all = _L1_xattn_setup()
    _L1_xattn_in = {k: v for k, v in _L1_xattn_all.items() if k in ('Uq', 'Vq', 'bq', 'Uk', 'Vk', 'bk', 'Uv', 'Vv', 'bv', 'Uo', 'Vo', 'bo')}
    del _L1_xattn_all

    def _L1_ffn_setup():
        import jax, jax.numpy as jnp
        import numpy as np
        DIM = 256
        NUM_EXPERTS = 6
        TOP_K = 2
        HIDDEN = DIM * 2
        key = jax.random.key(seed)
        ks = jax.random.split(key, 7)
        s_in = 1.0 / np.sqrt(DIM)
        s_h = 1.0 / np.sqrt(HIDDEN)
        x = jax.random.normal(ks[0], (4, 512, DIM), dtype=jnp.float32)
        Wg = jax.random.uniform(ks[1], (DIM, NUM_EXPERTS), jnp.float32, -s_in, s_in)
        bg = jax.random.uniform(ks[2], (NUM_EXPERTS,), jnp.float32, -s_in, s_in)
        W1 = jax.random.uniform(ks[3], (NUM_EXPERTS, DIM, HIDDEN), jnp.float32, -s_in, s_in)
        b1 = jax.random.uniform(ks[4], (NUM_EXPERTS, HIDDEN), jnp.float32, -s_in, s_in)
        W2 = jax.random.uniform(ks[5], (NUM_EXPERTS, HIDDEN, DIM), jnp.float32, -s_h, s_h)
        b2 = jax.random.uniform(ks[6], (NUM_EXPERTS, DIM), jnp.float32, -s_h, s_h)
        return {'x': x, 'Wg': Wg, 'bg': bg, 'W1': W1, 'b1': b1, 'W2': W2, 'b2': b2}
    _L1_ffn_all = _L1_ffn_setup()
    _L1_ffn_in = {k: v for k, v in _L1_ffn_all.items() if k in ('Wg', 'bg', 'W1', 'b1', 'W2', 'b2')}
    del _L1_ffn_all

    def _L2_attn_setup():
        import jax, jax.numpy as jnp
        import numpy as np
        from jax import lax
        key = jax.random.key(seed)
        ks = jax.random.split(key, 7)
        B_, T, H, N = (4, 1024, 256, 64)
        return {'u': jax.random.normal(ks[0], (B_, T, H), dtype=jnp.float32), 'log_A_real': jax.random.normal(ks[1], (N,), dtype=jnp.float32), 'A_imag': jax.random.normal(ks[2], (N,), dtype=jnp.float32), 'B': jax.random.normal(ks[3], (N, H), dtype=jnp.float32), 'C': jax.random.normal(ks[4], (H, N, 2), dtype=jnp.float32), 'D': jax.random.normal(ks[5], (H,), dtype=jnp.float32), 'log_step': jax.random.normal(ks[6], (1,), dtype=jnp.float32)}
    _L2_attn_all = _L2_attn_setup()
    _L2_attn_in = {k: v for k, v in _L2_attn_all.items() if k in ('log_A_real', 'A_imag', 'B', 'C', 'D', 'log_step')}
    del _L2_attn_all

    def _L2_xattn_setup():
        import jax, jax.numpy as jnp
        import numpy as np
        D1, D2, D3 = (256, 256, 256)
        key = jax.random.key(seed)
        k1, k2, kw, kb = jax.random.split(key, 4)
        x1 = jax.random.normal(k1, (8, 512, D1), dtype=jnp.float32)
        x2 = jax.random.normal(k2, (8, 512, D2), dtype=jnp.float32)
        bound = 1.0 / np.sqrt(D1 + D2)
        W = jax.random.uniform(kw, (D3, D1 + D2), minval=-bound, maxval=bound, dtype=jnp.float32)
        b = jax.random.uniform(kb, (D3,), minval=-bound, maxval=bound, dtype=jnp.float32)
        return {'x1': x1, 'x2': x2, 'W': W, 'b': b}
    _L2_xattn_all = _L2_xattn_setup()
    _L2_xattn_in = {k: v for k, v in _L2_xattn_all.items() if k in ('W', 'b')}
    del _L2_xattn_all

    def _L2_ffn_setup():
        import jax, jax.numpy as jnp
        import numpy as np
        B, T, D, R, E = (32, 256, 256, 64, 8)
        key = jax.random.key(seed)
        ks = jax.random.split(key, 12)
        inp = {}
        inp['x'] = jax.random.normal(ks[0], (B, T, D), dtype=jnp.float32)
        inp['base_W'] = jax.random.normal(ks[1], (D, D), dtype=jnp.float32) * (1.0 / np.sqrt(D))
        inp['base_b'] = jax.random.normal(ks[2], (D,), dtype=jnp.float32) * 0.01
        inp['disc_mu'] = jax.random.normal(ks[3], (E, D), dtype=jnp.float32) * 0.5
        inp['disc_sigma'] = jax.random.uniform(ks[4], (E, D), dtype=jnp.float32, minval=0.5, maxval=1.5)
        inp['down_W'] = jax.random.normal(ks[5], (E, D, R), dtype=jnp.float32) * (1.0 / np.sqrt(D))
        inp['down_b'] = jax.random.normal(ks[6], (E, R), dtype=jnp.float32) * 0.01
        inp['up_W'] = jax.random.normal(ks[7], (E, R, D), dtype=jnp.float32) * (1.0 / np.sqrt(R))
        inp['up_b'] = jax.random.normal(ks[8], (E, D), dtype=jnp.float32) * 0.01
        inp['conv_W'] = jax.random.normal(ks[9], (E, D, D), dtype=jnp.float32) * 0.02
        inp['conv_b'] = jax.random.normal(ks[10], (E, D), dtype=jnp.float32) * 0.01
        return inp
    _L2_ffn_all = _L2_ffn_setup()
    _L2_ffn_in = {k: v for k, v in _L2_ffn_all.items() if k in ('base_W', 'base_b', 'disc_mu', 'disc_sigma', 'down_W', 'down_b', 'up_W', 'up_b', 'conv_W', 'conv_b')}
    del _L2_ffn_all

    def _L3_attn_setup():
        import jax, jax.numpy as jnp
        import numpy as np
        D_MODEL = 256
        N_HEADS = 16
        HEAD_DIM = D_MODEL // N_HEADS
        WINDOW = 128
        LOCAL_BLOCK = 64
        LATENT_TOKENS = 64
        LATENT_D = 64
        LATENT_HEADS = 4
        LATENT_HD = LATENT_D // LATENT_HEADS
        NEG = -1000000000.0

        def _local_attention(q, k, v):
            B, H, S, hd = q.shape
            bs = min(S, max(WINDOW, LOCAL_BLOCK))
            nb = S // bs
            w = WINDOW
            L = bs + w - 1
            k_pad = jnp.pad(k, ((0, 0), (0, 0), (w - 1, 0), (0, 0)))
            v_pad = jnp.pad(v, ((0, 0), (0, 0), (w - 1, 0), (0, 0)))
            starts = jnp.arange(nb) * bs
            idx = starts[:, None] + jnp.arange(L)[None, :]
            kb = k_pad[:, :, idx]
            vb = v_pad[:, :, idx]
            qb = q.reshape(B, H, nb, bs, hd)
            q_pos = starts[:, None] + jnp.arange(bs)[None, :]
            k_gpos = starts[:, None] + jnp.arange(L)[None, :] - (w - 1)
            dist = q_pos[:, :, None] - k_gpos[:, None, :]
            allowed = (dist > 0) & (dist <= w) & (k_gpos[:, None, :] >= 0)
            scale = 1.0 / np.sqrt(hd)
            scores = jnp.einsum('bhnqd,bhnkd->bhnqk', qb, kb) * scale
            scores = jnp.where(allowed, scores, NEG)
            attn = jax.nn.softmax(scores, axis=-1)
            attn = jnp.where(allowed.any(-1)[None, None, :, :, None], attn, 0.0)
            out = jnp.einsum('bhnqk,bhnkd->bhnqd', attn, vb)
            return out.reshape(B, H, S, hd)
        key = jax.random.key(seed)
        ks = jax.random.split(key, 14)
        B, S = (2, 1024)
        s = 0.02
        f32 = jnp.float32
        return {'x': jax.random.normal(ks[0], (B, S, D_MODEL), f32), 'qkv_w': jax.random.normal(ks[1], (D_MODEL, 3 * D_MODEL), f32) * s, 'qkv_b': jnp.zeros((3 * D_MODEL,), f32), 'rq_w': jax.random.normal(ks[2], (D_MODEL, LATENT_D), f32) * s, 'rq_b': jnp.zeros((LATENT_D,), f32), 'rkv_w': jax.random.normal(ks[3], (D_MODEL, 2 * LATENT_D), f32) * s, 'rkv_b': jnp.zeros((2 * LATENT_D,), f32), 'rout_w': jax.random.normal(ks[4], (LATENT_D, D_MODEL), f32) * s, 'rout_b': jnp.zeros((D_MODEL,), f32), 'out_w': jax.random.normal(ks[5], (D_MODEL, D_MODEL), f32) * s, 'out_b': jnp.zeros((D_MODEL,), f32), 'gl_w': jax.random.normal(ks[6], (HEAD_DIM, 1), f32) * s, 'gr_w': jax.random.normal(ks[7], (HEAD_DIM, 1), f32) * s}
    _L3_attn_all = _L3_attn_setup()
    _L3_attn_in = {k: v for k, v in _L3_attn_all.items() if k in ('qkv_w', 'qkv_b', 'rq_w', 'rq_b', 'rkv_w', 'rkv_b', 'rout_w', 'rout_b', 'out_w', 'out_b', 'gl_w', 'gr_w')}
    del _L3_attn_all

    def _L3_xattn_setup():
        import jax, jax.numpy as jnp
        import numpy as np
        QUERY_DIM = 256
        KEY_DIM = 256
        NUM_HEADS = 16
        HEAD_DIM = QUERY_DIM // NUM_HEADS
        key = jax.random.key(seed)
        ks = jax.random.split(key, 11)
        B, Sq, Sk = (2, 512, 512)
        s = 0.02
        return {'q': jax.random.normal(ks[0], (B, Sq, QUERY_DIM), jnp.float32), 'k': jax.random.normal(ks[1], (B, Sk, KEY_DIM), jnp.float32), 'v': jax.random.normal(ks[2], (B, Sk, KEY_DIM), jnp.float32), 'Wq': jax.random.normal(ks[3], (QUERY_DIM, QUERY_DIM), jnp.float32) * s, 'bq': jnp.zeros((QUERY_DIM,), jnp.float32), 'Wk': jax.random.normal(ks[4], (KEY_DIM, QUERY_DIM), jnp.float32) * s, 'bk': jnp.zeros((QUERY_DIM,), jnp.float32), 'Wv': jax.random.normal(ks[5], (KEY_DIM, QUERY_DIM), jnp.float32) * s, 'bv': jnp.zeros((QUERY_DIM,), jnp.float32), 'Wo': jax.random.normal(ks[6], (QUERY_DIM, QUERY_DIM), jnp.float32) * s, 'bo': jnp.zeros((QUERY_DIM,), jnp.float32)}
    _L3_xattn_all = _L3_xattn_setup()
    _L3_xattn_in = {k: v for k, v in _L3_xattn_all.items() if k in ('Wq', 'bq', 'Wk', 'bk', 'Wv', 'bv', 'Wo', 'bo')}
    del _L3_xattn_all

    def _L3_ffn_setup():
        import jax, jax.numpy as jnp
        import numpy as np
        N_EMBD = 256
        N_STATE = 1024
        key = jax.random.key(seed)
        k_x, k_w1, k_b1, k_w2, k_b2 = jax.random.split(key, 5)
        x = jax.random.normal(k_x, (4, 512, N_EMBD), dtype=jnp.float32)
        w1 = jax.random.normal(k_w1, (N_EMBD, N_STATE), dtype=jnp.float32) * (1.0 / np.sqrt(N_EMBD))
        b1 = jax.random.normal(k_b1, (N_STATE,), dtype=jnp.float32) * 0.02
        w2 = jax.random.normal(k_w2, (N_STATE, N_EMBD), dtype=jnp.float32) * (1.0 / np.sqrt(N_STATE))
        b2 = jax.random.normal(k_b2, (N_EMBD,), dtype=jnp.float32) * 0.02
        return {'x': x, 'w1': w1, 'b1': b1, 'w2': w2, 'b2': b2}
    _L3_ffn_all = _L3_ffn_setup()
    _L3_ffn_in = {k: v for k, v in _L3_ffn_all.items() if k in ('w1', 'b1', 'w2', 'b2')}
    del _L3_ffn_all
    return {'x': x, 'ctx_1024': ctx_1024, 'L0_attn_qkv_w': _L0_attn_in['qkv_w'], 'L0_attn_qkv_b': _L0_attn_in['qkv_b'], 'L0_attn_out_w': _L0_attn_in['out_w'], 'L0_attn_out_b': _L0_attn_in['out_b'], 'L0_attn_g_attn': _L0_attn_in['g_attn'], 'L0_attn_b_attn': _L0_attn_in['b_attn'], 'L0_attn_g1': _L0_attn_in['g1'], 'L0_attn_b1': _L0_attn_in['b1'], 'L0_attn_g2': _L0_attn_in['g2'], 'L0_attn_b2': _L0_attn_in['b2'], 'L0_attn_w_ctx': _L0_attn_in['w_ctx'], 'L0_attn_w_x': _L0_attn_in['w_x'], 'L0_attn_b_inl': _L0_attn_in['b_inl'], 'L0_attn_ff_w1': _L0_attn_in['ff_w1'], 'L0_attn_ff_b1': _L0_attn_in['ff_b1'], 'L0_attn_ff_w2': _L0_attn_in['ff_w2'], 'L0_attn_ff_b2': _L0_attn_in['ff_b2'], 'L0_xattn_Wq': _L0_xattn_in['Wq'], 'L0_xattn_Wk': _L0_xattn_in['Wk'], 'L0_xattn_Wv': _L0_xattn_in['Wv'], 'L0_xattn_Wo': _L0_xattn_in['Wo'], 'L0_xattn_bo': _L0_xattn_in['bo'], 'L0_ffn_packed_weight': _L0_ffn_in['packed_weight'], 'L0_ffn_weight_scale': _L0_ffn_in['weight_scale'], 'L0_ffn_bias': _L0_ffn_in['bias'], 'L1_attn_W_dq': _L1_attn_in['W_dq'], 'L1_attn_W_uq': _L1_attn_in['W_uq'], 'L1_attn_W_dkv': _L1_attn_in['W_dkv'], 'L1_attn_W_uk': _L1_attn_in['W_uk'], 'L1_attn_W_uv': _L1_attn_in['W_uv'], 'L1_attn_W_o': _L1_attn_in['W_o'], 'L1_xattn_Uq': _L1_xattn_in['Uq'], 'L1_xattn_Vq': _L1_xattn_in['Vq'], 'L1_xattn_bq': _L1_xattn_in['bq'], 'L1_xattn_Uk': _L1_xattn_in['Uk'], 'L1_xattn_Vk': _L1_xattn_in['Vk'], 'L1_xattn_bk': _L1_xattn_in['bk'], 'L1_xattn_Uv': _L1_xattn_in['Uv'], 'L1_xattn_Vv': _L1_xattn_in['Vv'], 'L1_xattn_bv': _L1_xattn_in['bv'], 'L1_xattn_Uo': _L1_xattn_in['Uo'], 'L1_xattn_Vo': _L1_xattn_in['Vo'], 'L1_xattn_bo': _L1_xattn_in['bo'], 'L1_ffn_Wg': _L1_ffn_in['Wg'], 'L1_ffn_bg': _L1_ffn_in['bg'], 'L1_ffn_W1': _L1_ffn_in['W1'], 'L1_ffn_b1': _L1_ffn_in['b1'], 'L1_ffn_W2': _L1_ffn_in['W2'], 'L1_ffn_b2': _L1_ffn_in['b2'], 'L2_attn_log_A_real': _L2_attn_in['log_A_real'], 'L2_attn_A_imag': _L2_attn_in['A_imag'], 'L2_attn_B': _L2_attn_in['B'], 'L2_attn_C': _L2_attn_in['C'], 'L2_attn_D': _L2_attn_in['D'], 'L2_attn_log_step': _L2_attn_in['log_step'], 'L2_xattn_W': _L2_xattn_in['W'], 'L2_xattn_b': _L2_xattn_in['b'], 'L2_ffn_base_W': _L2_ffn_in['base_W'], 'L2_ffn_base_b': _L2_ffn_in['base_b'], 'L2_ffn_disc_mu': _L2_ffn_in['disc_mu'], 'L2_ffn_disc_sigma': _L2_ffn_in['disc_sigma'], 'L2_ffn_down_W': _L2_ffn_in['down_W'], 'L2_ffn_down_b': _L2_ffn_in['down_b'], 'L2_ffn_up_W': _L2_ffn_in['up_W'], 'L2_ffn_up_b': _L2_ffn_in['up_b'], 'L2_ffn_conv_W': _L2_ffn_in['conv_W'], 'L2_ffn_conv_b': _L2_ffn_in['conv_b'], 'L3_attn_qkv_w': _L3_attn_in['qkv_w'], 'L3_attn_qkv_b': _L3_attn_in['qkv_b'], 'L3_attn_rq_w': _L3_attn_in['rq_w'], 'L3_attn_rq_b': _L3_attn_in['rq_b'], 'L3_attn_rkv_w': _L3_attn_in['rkv_w'], 'L3_attn_rkv_b': _L3_attn_in['rkv_b'], 'L3_attn_rout_w': _L3_attn_in['rout_w'], 'L3_attn_rout_b': _L3_attn_in['rout_b'], 'L3_attn_out_w': _L3_attn_in['out_w'], 'L3_attn_out_b': _L3_attn_in['out_b'], 'L3_attn_gl_w': _L3_attn_in['gl_w'], 'L3_attn_gr_w': _L3_attn_in['gr_w'], 'L3_xattn_Wq': _L3_xattn_in['Wq'], 'L3_xattn_bq': _L3_xattn_in['bq'], 'L3_xattn_Wk': _L3_xattn_in['Wk'], 'L3_xattn_bk': _L3_xattn_in['bk'], 'L3_xattn_Wv': _L3_xattn_in['Wv'], 'L3_xattn_bv': _L3_xattn_in['bv'], 'L3_xattn_Wo': _L3_xattn_in['Wo'], 'L3_xattn_bo': _L3_xattn_in['bo'], 'L3_ffn_w1': _L3_ffn_in['w1'], 'L3_ffn_b1': _L3_ffn_in['b1'], 'L3_ffn_w2': _L3_ffn_in['w2'], 'L3_ffn_b2': _L3_ffn_in['b2']}

def reference(x, ctx_1024, L0_attn_qkv_w, L0_attn_qkv_b, L0_attn_out_w, L0_attn_out_b, L0_attn_g_attn, L0_attn_b_attn, L0_attn_g1, L0_attn_b1, L0_attn_g2, L0_attn_b2, L0_attn_w_ctx, L0_attn_w_x, L0_attn_b_inl, L0_attn_ff_w1, L0_attn_ff_b1, L0_attn_ff_w2, L0_attn_ff_b2, L0_xattn_Wq, L0_xattn_Wk, L0_xattn_Wv, L0_xattn_Wo, L0_xattn_bo, L0_ffn_packed_weight, L0_ffn_weight_scale, L0_ffn_bias, L1_attn_W_dq, L1_attn_W_uq, L1_attn_W_dkv, L1_attn_W_uk, L1_attn_W_uv, L1_attn_W_o, L1_xattn_Uq, L1_xattn_Vq, L1_xattn_bq, L1_xattn_Uk, L1_xattn_Vk, L1_xattn_bk, L1_xattn_Uv, L1_xattn_Vv, L1_xattn_bv, L1_xattn_Uo, L1_xattn_Vo, L1_xattn_bo, L1_ffn_Wg, L1_ffn_bg, L1_ffn_W1, L1_ffn_b1, L1_ffn_W2, L1_ffn_b2, L2_attn_log_A_real, L2_attn_A_imag, L2_attn_B, L2_attn_C, L2_attn_D, L2_attn_log_step, L2_xattn_W, L2_xattn_b, L2_ffn_base_W, L2_ffn_base_b, L2_ffn_disc_mu, L2_ffn_disc_sigma, L2_ffn_down_W, L2_ffn_down_b, L2_ffn_up_W, L2_ffn_up_b, L2_ffn_conv_W, L2_ffn_conv_b, L3_attn_qkv_w, L3_attn_qkv_b, L3_attn_rq_w, L3_attn_rq_b, L3_attn_rkv_w, L3_attn_rkv_b, L3_attn_rout_w, L3_attn_rout_b, L3_attn_out_w, L3_attn_out_b, L3_attn_gl_w, L3_attn_gr_w, L3_xattn_Wq, L3_xattn_bq, L3_xattn_Wk, L3_xattn_bk, L3_xattn_Wv, L3_xattn_bv, L3_xattn_Wo, L3_xattn_bo, L3_ffn_w1, L3_ffn_b1, L3_ffn_w2, L3_ffn_b2):
    import jax
    import jax.numpy as jnp

    def _L0_attn_ref(x, qkv_w, qkv_b, out_w, out_b, g_attn, b_attn, g1, b1, g2, b2, w_ctx, w_x, b_inl, ff_w1, ff_b1, ff_w2, ff_b2):
        import jax, jax.numpy as jnp
        import numpy as np
        B, S, D, H = (2, 512, 256, 16)
        HD = D // H
        FF = 1024
        NUM_ITERS = 8
        DT = 0.1
        LN_EPS = 1e-05

        def _ln(x, g, b):
            m = jnp.mean(x, axis=-1, keepdims=True)
            v = jnp.var(x, axis=-1, keepdims=True)
            return (x - m) * jax.lax.rsqrt(v + LN_EPS) * g + b

        def _forward(x, qkv_w, qkv_b, out_w, out_b, g_attn, b_attn, g1, b1, g2, b2, w_ctx, w_x, b_inl, ff_w1, ff_b1, ff_w2, ff_b2):
            b, s, d = x.shape
            xn = _ln(x, g_attn, b_attn)
            qkv = (xn @ qkv_w + qkv_b).reshape(b, s, 3, H, HD)
            qkv = jnp.transpose(qkv, (2, 0, 3, 1, 4))
            q, k, v = (qkv[0], qkv[1], qkv[2])
            scores = jnp.einsum('bhqd,bhkd->bhqk', q, k) / np.sqrt(HD).astype(np.float32)
            causal = jnp.triu(jnp.ones((s, s), dtype=bool), 1)
            scores = jnp.where(causal[None, None], -jnp.inf, scores)
            attn_w = jax.nn.softmax(scores, axis=-1)
            attn = jnp.einsum('bhqk,bhkd->bhqd', attn_w, v)
            attn = jnp.transpose(attn, (0, 2, 1, 3)).reshape(b, s, d)
            attn = attn @ out_w + out_b
            x = x + attn
            ctx = attn.reshape(b * s, d)
            xs = _ln(x, g1, b1).reshape(b * s, d)
            vs = jnp.zeros_like(xs)

            def step(carry, _):
                xs, vs = carry
                u = jnp.tanh(ctx @ w_ctx + xs @ w_x + b_inl)
                vn = vs + DT * (u - xs - vs)
                xn_ = xs + DT * vn
                return ((xn_, vn), None)
            (xs, vs), _ = jax.lax.scan(step, (xs, vs), None, length=NUM_ITERS)
            x = x + xs.reshape(b, s, d)
            h = _ln(x, g2, b2)
            h = jax.nn.gelu(h @ ff_w1 + ff_b1, approximate=False)
            x = x + (h @ ff_w2 + ff_b2)
            return x
        return _forward(x, qkv_w, qkv_b, out_w, out_b, g_attn, b_attn, g1, b1, g2, b2, w_ctx, w_x, b_inl, ff_w1, ff_b1, ff_w2, ff_b2)

    def _L0_xattn_ref(x, context, Wq, Wk, Wv, Wo, bo):
        import jax, jax.numpy as jnp
        import numpy as np
        QUERY_DIM = 256
        CONTEXT_DIM = 256
        HEADS = 8
        DIM_HEAD = 64
        INNER = HEADS * DIM_HEAD
        SCALE = DIM_HEAD ** (-0.5)
        B, N, _ = x.shape
        M = context.shape[1]
        q = (x @ Wq).reshape(B, N, HEADS, DIM_HEAD)
        k = (context @ Wk).reshape(B, M, HEADS, DIM_HEAD)
        v = (context @ Wv).reshape(B, M, HEADS, DIM_HEAD)
        sim = jnp.einsum('bihd,bjhd->bhij', q.astype(jnp.float32), k.astype(jnp.float32)) * SCALE
        attn = jax.nn.softmax(sim, axis=-1).astype(v.dtype)
        out = jnp.einsum('bhij,bjhd->bihd', attn, v).reshape(B, N, INNER)
        return out @ Wo + bo

    def _L0_ffn_ref(x, packed_weight, weight_scale, bias):
        import jax, jax.numpy as jnp
        import numpy as np
        IN_F = 256
        OUT_F = 256
        B, S = (8, 1024)

        def _pack_ternary(tern):
            enc = (tern + 1.0).astype(jnp.int32).reshape(-1)
            return (enc[0::4] | enc[1::4] << 2 | enc[2::4] << 4 | enc[3::4] << 6).astype(jnp.int32)
        n = OUT_F * IN_F
        shifts = jnp.array([0, 2, 4, 6], dtype=jnp.int32)
        enc = (packed_weight[None, :] >> shifts[:, None] & 3).reshape(-1)[:n]
        w = (enc.astype(jnp.float32) - 1.0).reshape(OUT_F, IN_F) * weight_scale
        act_scale = 127.0 / jnp.maximum(jnp.max(jnp.abs(x), axis=-1, keepdims=True), 1e-05)
        x_dq = jnp.clip(jnp.round(x * act_scale), -128.0, 127.0) / act_scale
        return jnp.einsum('bsi,oi->bso', x_dq, w) + bias

    def _L1_attn_ref(x, W_dq, W_uq, W_dkv, W_uk, W_uv, W_o):
        import math
        import jax, jax.numpy as jnp
        import numpy as np
        D_MODEL = 256
        N_HEADS = 16
        D_K = D_MODEL // N_HEADS
        D_C = 64
        B, S = (2, 512)
        Bx, Sx, _ = x.shape
        c_q = x @ W_dq
        Q = (c_q @ W_uq).reshape(Bx, Sx, N_HEADS, D_K)
        c_kv = x @ W_dkv
        K = (c_kv @ W_uk).reshape(Bx, Sx, N_HEADS, D_K)
        V = (c_kv @ W_uv).reshape(Bx, Sx, N_HEADS, D_K)
        scores = jnp.einsum('bqhd,bkhd->bhqk', Q, K) / math.sqrt(D_K)
        causal = jnp.tril(jnp.ones((Sx, Sx), dtype=bool))
        scores = jnp.where(causal, scores, -jnp.inf)
        attn = jax.nn.softmax(scores, axis=-1)
        out = jnp.einsum('bhqk,bkhd->bqhd', attn, V).reshape(Bx, Sx, N_HEADS * D_K)
        return out @ W_o

    def _L1_xattn_ref(q, k, v, Uq, Vq, bq, Uk, Vk, bk, Uv, Vv, bv, Uo, Vo, bo):
        import jax, jax.numpy as jnp
        import numpy as np
        D_MODEL = 256
        N_HEADS = 16
        RANK = 128
        TOPK = 64
        D_HEAD = D_MODEL // N_HEADS
        SCALE = D_HEAD ** (-0.5)
        INIT_SCALE = 0.05

        def _lowrank_proj(x, U, V, b):
            return jnp.einsum('btr,dr->btd', jnp.einsum('btd,dr->btr', x, U), V) + b

        def _heads(x, B, T):
            return x.reshape(B, T, N_HEADS, D_HEAD).transpose(0, 2, 1, 3)

        def _topk_softmax(scores, k):
            B, H, L, S = scores.shape
            flat = scores.reshape(-1, S)
            vals, idx = jax.lax.top_k(flat, k)
            p = jax.nn.softmax(vals, axis=-1)
            rows = jnp.arange(flat.shape[0])[:, None]
            attn = jnp.zeros_like(flat).at[rows, idx].set(p)
            return attn.reshape(B, H, L, S)
        B, L, _ = q.shape
        S = k.shape[1]
        qh = _heads(_lowrank_proj(q, Uq, Vq, bq), B, L)
        kh = _heads(_lowrank_proj(k, Uk, Vk, bk), B, S)
        vh = _heads(_lowrank_proj(v, Uv, Vv, bv), B, S)
        scores = jnp.einsum('bhld,bhsd->bhls', qh, kh) * SCALE
        dyn_k = min(TOPK, S)
        attn = _topk_softmax(scores, dyn_k)
        out = jnp.einsum('bhls,bhsd->bhld', attn, vh)
        out = out.transpose(0, 2, 1, 3).reshape(B, L, D_MODEL)
        return _lowrank_proj(out, Uo, Vo, bo)

    def _L1_ffn_ref(x, Wg, bg, W1, b1, W2, b2):
        import jax, jax.numpy as jnp
        import numpy as np
        DIM = 256
        NUM_EXPERTS = 6
        TOP_K = 2
        HIDDEN = DIM * 2
        gate_logits = jnp.einsum('bsd,de->bse', x, Wg) + bg
        topk_w, topk_idx = jax.lax.top_k(gate_logits, TOP_K)
        topk_w = jax.nn.softmax(topk_w, axis=-1)
        combine = jnp.sum(jax.nn.one_hot(topk_idx, NUM_EXPERTS, dtype=x.dtype) * topk_w[..., None], axis=-2)
        h = jnp.einsum('bsd,edh->ebsh', x, W1) + b1[:, None, None, :]
        h = jax.nn.gelu(h, approximate=False)
        y = jnp.einsum('ebsh,ehd->ebsd', h, W2) + b2[:, None, None, :]
        out = jnp.einsum('ebsd,bse->bsd', y, combine)
        return out

    def _L2_attn_ref(u, log_A_real, A_imag, B, C, D, log_step):
        import jax, jax.numpy as jnp
        import numpy as np
        from jax import lax
        step = jnp.exp(log_step)
        A = (-jnp.exp(log_A_real)).astype(jnp.complex64) + 1j * A_imag.astype(jnp.complex64)
        A_bar = jnp.exp(A * step.astype(jnp.complex64))
        B_bar = ((A_bar - 1.0) / A)[:, None] * B.astype(jnp.complex64)
        C_complex = (C[..., 0] + 1j * C[..., 1]).astype(jnp.complex64)
        Bu = jnp.einsum('bth,nh->tbn', u, B_bar)

        def scan_step(x, bu_t):
            x = A_bar[None, :] * x + bu_t
            return (x, x)
        x0 = jnp.zeros((u.shape[0], A_bar.shape[0]), dtype=jnp.complex64)
        _, xs = lax.scan(scan_step, x0, Bu)
        y = jnp.real(jnp.einsum('tbn,hn->tbh', xs, C_complex))
        y = jnp.transpose(y, (1, 0, 2)) + D[None, None, :] * u
        return y

    def _L2_xattn_ref(x1, x2, W, b):
        import jax, jax.numpy as jnp
        import numpy as np
        D1, D2, D3 = (256, 256, 256)
        d1 = x1.shape[-1]
        W1 = W[:, :d1]
        W2 = W[:, d1:]
        part1 = jnp.einsum('bld,ed->ble', x1, W1)
        part2 = jnp.einsum('bld,ed->be', x2, W2) / x2.shape[1]
        return part1 + part2[:, None, :] + b

    def _L2_ffn_ref(x, base_W, base_b, disc_mu, disc_sigma, down_W, down_b, up_W, up_b, conv_W, conv_b):
        import jax, jax.numpy as jnp
        import numpy as np
        B, T, D, R, E = (32, 256, 256, 64, 8)
        base = jnp.einsum('btd,od->bto', x, base_W) + base_b
        m1 = x.mean(axis=1)
        m2 = (x * x).mean(axis=1)
        inv_var = 1.0 / (disc_sigma * disc_sigma)
        losses = (jnp.einsum('bd,ed->eb', m2, inv_var) - 2.0 * jnp.einsum('bd,ed->eb', m1, disc_mu * inv_var) + jnp.sum(disc_mu * disc_mu * inv_var, axis=1)[:, None]) / D
        idx = jnp.argmin(losses, axis=0)
        Wd, bd = (down_W[idx], down_b[idx])
        Wu, bu = (up_W[idx], up_b[idx])
        Wc, bc = (conv_W[idx], conv_b[idx])
        h = jax.nn.relu(jnp.einsum('btd,bdr->btr', x, Wd) + bd[:, None, :])
        a = jnp.einsum('btr,brd->btd', h, Wu) + bu[:, None, :]
        y = jnp.einsum('btd,bod->bto', a, Wc) + bc[:, None, :]
        return base + y

    def _L3_attn_ref(x, qkv_w, qkv_b, rq_w, rq_b, rkv_w, rkv_b, rout_w, rout_b, out_w, out_b, gl_w, gr_w):
        import jax, jax.numpy as jnp
        import numpy as np
        D_MODEL = 256
        N_HEADS = 16
        HEAD_DIM = D_MODEL // N_HEADS
        WINDOW = 128
        LOCAL_BLOCK = 64
        LATENT_TOKENS = 64
        LATENT_D = 64
        LATENT_HEADS = 4
        LATENT_HD = LATENT_D // LATENT_HEADS
        NEG = -1000000000.0

        def _local_attention(q, k, v):
            B, H, S, hd = q.shape
            bs = min(S, max(WINDOW, LOCAL_BLOCK))
            nb = S // bs
            w = WINDOW
            L = bs + w - 1
            k_pad = jnp.pad(k, ((0, 0), (0, 0), (w - 1, 0), (0, 0)))
            v_pad = jnp.pad(v, ((0, 0), (0, 0), (w - 1, 0), (0, 0)))
            starts = jnp.arange(nb) * bs
            idx = starts[:, None] + jnp.arange(L)[None, :]
            kb = k_pad[:, :, idx]
            vb = v_pad[:, :, idx]
            qb = q.reshape(B, H, nb, bs, hd)
            q_pos = starts[:, None] + jnp.arange(bs)[None, :]
            k_gpos = starts[:, None] + jnp.arange(L)[None, :] - (w - 1)
            dist = q_pos[:, :, None] - k_gpos[:, None, :]
            allowed = (dist > 0) & (dist <= w) & (k_gpos[:, None, :] >= 0)
            scale = 1.0 / np.sqrt(hd)
            scores = jnp.einsum('bhnqd,bhnkd->bhnqk', qb, kb) * scale
            scores = jnp.where(allowed, scores, NEG)
            attn = jax.nn.softmax(scores, axis=-1)
            attn = jnp.where(allowed.any(-1)[None, None, :, :, None], attn, 0.0)
            out = jnp.einsum('bhnqk,bhnkd->bhnqd', attn, vb)
            return out.reshape(B, H, S, hd)
        B, S, D = x.shape
        qkv = x @ qkv_w + qkv_b
        q, k, v = jnp.split(qkv, 3, axis=-1)

        def heads(t):
            return t.reshape(B, S, N_HEADS, HEAD_DIM).transpose(0, 2, 1, 3)
        local = _local_attention(heads(q), heads(k), heads(v))
        chunk = -(-S // min(LATENT_TOKENS, S))
        nlat = S // chunk
        pooled = x.reshape(B, nlat, chunk, D).mean(axis=2)
        chunk_ids = jnp.arange(S) // chunk
        rq = (x @ rq_w + rq_b).reshape(B, S, LATENT_HEADS, LATENT_HD).transpose(0, 2, 1, 3)
        rkv = pooled @ rkv_w + rkv_b
        rk, rv = jnp.split(rkv, 2, axis=-1)
        rk = rk.reshape(B, nlat, LATENT_HEADS, LATENT_HD).transpose(0, 2, 1, 3)
        rv = rv.reshape(B, nlat, LATENT_HEADS, LATENT_HD).transpose(0, 2, 1, 3)
        lscale = 1.0 / np.sqrt(LATENT_HD)
        lscores = jnp.einsum('bhsd,bhld->bhsl', rq, rk) * lscale
        lat_allowed = jnp.arange(nlat)[None, :] < chunk_ids[:, None]
        lscores = jnp.where(lat_allowed[None, None], lscores, NEG)
        lattn = jax.nn.softmax(lscores, axis=-1)
        lattn = jnp.where(lat_allowed.any(-1)[None, None, :, None], lattn, 0.0)
        lat_out = jnp.einsum('bhsl,bhld->bhsd', lattn, rv)
        lat_out = lat_out.transpose(0, 2, 1, 3).reshape(B, S, LATENT_D)
        remote = lat_out @ rout_w + rout_b
        remote_h = remote.reshape(B, S, N_HEADS, HEAD_DIM).transpose(0, 2, 1, 3)
        gate = jax.nn.sigmoid(local @ gl_w + remote_h @ gr_w)
        mixed = gate * local + (1.0 - gate) * remote_h
        mixed = mixed.transpose(0, 2, 1, 3).reshape(B, S, D)
        return mixed @ out_w + out_b

    def _L3_xattn_ref(q, k, v, Wq, bq, Wk, bk, Wv, bv, Wo, bo):
        import jax, jax.numpy as jnp
        import numpy as np
        QUERY_DIM = 256
        KEY_DIM = 256
        NUM_HEADS = 16
        HEAD_DIM = QUERY_DIM // NUM_HEADS
        B, Sq, _ = q.shape
        Sk = k.shape[1]
        scale = HEAD_DIM ** (-0.5)
        qh = (q @ Wq + bq).reshape(B, Sq, NUM_HEADS, HEAD_DIM).transpose(0, 2, 1, 3)
        kh = (k @ Wk + bk).reshape(B, Sk, NUM_HEADS, HEAD_DIM).transpose(0, 2, 1, 3)
        vh = (v @ Wv + bv).reshape(B, Sk, NUM_HEADS, HEAD_DIM).transpose(0, 2, 1, 3)
        scores = jnp.einsum('bhqd,bhkd->bhqk', qh, kh) * scale
        attn = jax.nn.softmax(scores, axis=-1)
        out = jnp.einsum('bhqk,bhkd->bhqd', attn, vh)
        out = out.transpose(0, 2, 1, 3).reshape(B, Sq, QUERY_DIM)
        return out @ Wo + bo

    def _L3_ffn_ref(x, w1, b1, w2, b2):
        import jax, jax.numpy as jnp
        import numpy as np
        N_EMBD = 256
        N_STATE = 1024
        h = jax.nn.gelu(jnp.einsum('bse,eh->bsh', x, w1) + b1, approximate=False)
        return jnp.einsum('bsh,he->bse', h, w2) + b2
    x = _layernorm(x + _L0_attn_ref(x, L0_attn_qkv_w, L0_attn_qkv_b, L0_attn_out_w, L0_attn_out_b, L0_attn_g_attn, L0_attn_b_attn, L0_attn_g1, L0_attn_b1, L0_attn_g2, L0_attn_b2, L0_attn_w_ctx, L0_attn_w_x, L0_attn_b_inl, L0_attn_ff_w1, L0_attn_ff_b1, L0_attn_ff_w2, L0_attn_ff_b2), axis=-1)
    x = _layernorm(x + _L0_xattn_ref(x, ctx_1024, L0_xattn_Wq, L0_xattn_Wk, L0_xattn_Wv, L0_xattn_Wo, L0_xattn_bo), axis=-1)
    x = _layernorm(x + _L0_ffn_ref(x, L0_ffn_packed_weight, L0_ffn_weight_scale, L0_ffn_bias), axis=-1)
    x = _layernorm(x + _L1_attn_ref(x, L1_attn_W_dq, L1_attn_W_uq, L1_attn_W_dkv, L1_attn_W_uk, L1_attn_W_uv, L1_attn_W_o), axis=-1)
    x = _layernorm(x + _L1_xattn_ref(x, ctx_1024, ctx_1024, L1_xattn_Uq, L1_xattn_Vq, L1_xattn_bq, L1_xattn_Uk, L1_xattn_Vk, L1_xattn_bk, L1_xattn_Uv, L1_xattn_Vv, L1_xattn_bv, L1_xattn_Uo, L1_xattn_Vo, L1_xattn_bo), axis=-1)
    x = _layernorm(x + _L1_ffn_ref(x, L1_ffn_Wg, L1_ffn_bg, L1_ffn_W1, L1_ffn_b1, L1_ffn_W2, L1_ffn_b2), axis=-1)
    x = _layernorm(x + _L2_attn_ref(x, L2_attn_log_A_real, L2_attn_A_imag, L2_attn_B, L2_attn_C, L2_attn_D, L2_attn_log_step), axis=-1)
    x = _layernorm(x + _L2_xattn_ref(x, ctx_1024, L2_xattn_W, L2_xattn_b), axis=-1)
    x = _layernorm(x + _L2_ffn_ref(x, L2_ffn_base_W, L2_ffn_base_b, L2_ffn_disc_mu, L2_ffn_disc_sigma, L2_ffn_down_W, L2_ffn_down_b, L2_ffn_up_W, L2_ffn_up_b, L2_ffn_conv_W, L2_ffn_conv_b), axis=-1)
    x = _layernorm(x + _L3_attn_ref(x, L3_attn_qkv_w, L3_attn_qkv_b, L3_attn_rq_w, L3_attn_rq_b, L3_attn_rkv_w, L3_attn_rkv_b, L3_attn_rout_w, L3_attn_rout_b, L3_attn_out_w, L3_attn_out_b, L3_attn_gl_w, L3_attn_gr_w), axis=-1)
    x = _layernorm(x + _L3_xattn_ref(x, ctx_1024, ctx_1024, L3_xattn_Wq, L3_xattn_bq, L3_xattn_Wk, L3_xattn_bk, L3_xattn_Wv, L3_xattn_bv, L3_xattn_Wo, L3_xattn_bo), axis=-1)
    x = _layernorm(x + _L3_ffn_ref(x, L3_ffn_w1, L3_ffn_b1, L3_ffn_w2, L3_ffn_b2), axis=-1)
    return x

_drawn_inputs = setup_inputs


def setup_inputs(seed=0):
    import zlib

    import numpy as np

    out = dict(_drawn_inputs(seed))
    spreads = {'L0_attn_qkv_b': (0.0, 0.1),
     'L0_attn_out_b': (0.0, 0.1),
     'L0_attn_g_attn': (1.0, 0.6),
     'L0_attn_b_attn': (0.0, 0.1),
     'L0_attn_g1': (1.0, 0.2),
     'L0_attn_b1': (0.0, 0.1),
     'L0_attn_g2': (1.0, 0.2),
     'L0_attn_b2': (0.0, 0.339),
     'L0_attn_b_inl': (0.0, 0.646),
     'L0_attn_ff_b1': (0.0, 0.1),
     'L0_attn_ff_b2': (0.0, 0.1),
     'L0_ffn_bias': (0.0, 0.1),
     'L1_xattn_bq': (0.0, 0.1),
     'L1_xattn_bk': (0.0, 2.0),
     'L1_xattn_bv': (0.0, 0.1),
     'L1_xattn_bo': (0.0, 0.1),
     'L3_attn_qkv_b': (0.0, 0.48),
     'L3_attn_rq_b': (0.0, 0.8),
     'L3_attn_rkv_b': (0.0, 0.8),
     'L3_attn_rout_b': (0.0, 0.554),
     'L3_attn_out_b': (0.0, 0.1),
     'L3_xattn_bq': (0.0, 0.8),
     'L3_xattn_bk': (0.0, 2.0),
     'L3_xattn_bv': (0.0, 0.1),
     'L3_xattn_bo': (0.0, 0.1)}
    factors = {'L0_attn_w_ctx': 3.771,
     'L0_xattn_bo': 4.437,
     'L1_attn_W_dq': 8.0,
     'L1_attn_W_uq': 8.0,
     'L1_attn_W_uk': 8.0,
     'L1_ffn_b1': 5.693,
     'L1_ffn_b2': 2.762,
     'L2_attn_D': 8.0,
     'L2_xattn_b': 2.716,
     'L2_ffn_base_b': 7.963,
     'L2_ffn_down_b': 35.616,
     'L2_ffn_up_b': 24.565,
     'L2_ffn_conv_b': 8.0,
     'L3_attn_rq_w': 8.0,
     'L3_attn_rkv_w': 8.0,
     'L3_attn_rout_w': 8.0,
     'L3_attn_gl_w': 8.0,
     'L3_attn_gr_w': 8.0,
     'L3_xattn_Wq': 8.0,
     'L3_xattn_Wk': 8.0,
     'L3_ffn_b1': 5.041,
     'L3_ffn_b2': 3.502}
    for name, (base, spread) in spreads.items():
        noise = np.random.default_rng([zlib.crc32(name.encode()), seed]).standard_normal(out[name].shape)
        drawn = base * np.exp(spread * noise) if base else spread * noise
        out[name] = jnp.asarray(drawn.astype(out[name].dtype))
    for name, factor in factors.items():
        out[name] = (out[name] * factor).astype(out[name].dtype)
    return out
```

```python
from contextlib import ExitStack, contextmanager
from dataclasses import dataclass

import concourse.bass as bass
from concourse import mybir

F32 = mybir.dt.float32
I32 = mybir.dt.int32
ALU = mybir.AluOpType
ACT = mybir.ActivationFunctionType
AX = mybir.AxisListType

P = 128
B, S, D = 4, 512, 256
M = 1601
TT = S // P
DT = D // P
MT = (M + P - 1) // P
BANK = 512
BANKS = 8
EPS = 1e-5
MASKED = -1e30
TAKEN = -3e38
ROUND = 12582912.0


def kt_rows(n, t):
    return min(P, n - t * P)


@contextmanager
def stage(nc, *signals):
    with ExitStack() as held:
        sems = [held.enter_context(nc.semaphore(s)) for s in signals]
        with nc.Block() as block:
            yield (block, *sems)
        with nc.Block() as clearing:
            @clearing.sync
            def _(sp):
                for s in sems:
                    sp.sem_clear(s)


def stepper(engine, sem):
    done = [0]

    def step(instruction):
        done[0] += 1
        instruction.then_inc(sem, 1)
        engine.wait_ge(sem, done[0])

    return step


@dataclass
class Job:
    multiply: object
    engine: str
    evacuate: object


class Core:

    def __init__(self, nc, ctx):
        self.nc = nc
        self.sublayer, self.tensors = "", 0
        sb = lambda name, shape: ctx.enter_context(nc.sbuf_tensor(name, shape, F32))
        self.psum = ctx.enter_context(nc.psum_tensor("psum", [P, BANKS * BANK], F32))
        self.x_all = sb("x_all", [P, B, TT, D])
        self.x = sb("x", [P, TT, D])
        self.xT = sb("xT", [P, DT, S])
        self.delta = sb("delta", [P, TT, D])
        self.ident = sb("ident", [P, P])
        self.ones = sb("ones", [P, BANK])
        self.causal = sb("causal", [P, P])
        self.stats = sb("stats", [P, TT, 6])
        self.moments = sb("moments", [P, TT, 2])
        self.spread = sb("spread", [P, TT])
        self.rstd = sb("rstd", [P, TT])

    def named(self, name):
        self.tensors += 1
        return f"{self.sublayer}_{name}_{self.tensors}"

    def bank(self, j):
        return self.psum[:, (j % BANKS) * BANK:(j % BANKS + 1) * BANK]


def constants_stage(core, x):
    nc = core.nc
    with stage(nc, "filled", "x_loaded") as (block, filled, x_loaded):
        @block.gpsimd
        def _(pool):
            pool.memset(core.ident[:], 0.0).then_inc(filled, 1)
            pool.memset(core.causal[:], 0.0).then_inc(filled, 1)
            pool.memset(core.ones[:], 1.0).then_inc(filled, 1)
            pool.wait_ge(filled, 3)
            pool.affine_select(out=core.ident[:], in_=core.ident[:], compare_op=ALU.not_equal, fill=1.0,
                               base=0, pattern=[[-1, P]], channel_multiplier=1).then_inc(filled, 1)
            pool.affine_select(out=core.causal[:], in_=core.causal[:], compare_op=ALU.is_ge, fill=MASKED,
                               base=0, pattern=[[-1, P]], channel_multiplier=1).then_inc(filled, 1)
            pool.wait_ge(filled, 5)

        @block.sync
        def _(sp):
            for b in range(B):
                sp.dma_start(core.x_all[:, b], x[b].rearrange("(t p) d -> p t d", p=P)).then_inc(x_loaded, 16)
            sp.wait_ge(x_loaded, 16 * B)


def load_stage(core, loads, zeroed=()):
    nc = core.nc
    with stage(nc, "padding_zeroed", "loaded_by_sp", "loaded_by_act") as (block, padding_zeroed, by_sp, by_act):
        @block.gpsimd
        def _(pool):
            for z in zeroed:
                pool.memset(z, 0.0).then_inc(padding_zeroed, 1)

        @block.sync
        def _(sp):
            if zeroed:
                sp.wait_ge(padding_zeroed, len(zeroed))
            with nc.allow_non_contiguous_dma("biases and small tables, a value per partition"):
                for to, of in loads[0::2]:
                    sp.dma_start(to, of).then_inc(by_sp, 16)
            sp.wait_ge(by_sp, 16 * len(loads[0::2]))

        @block.scalar
        def _(act):
            if zeroed:
                act.wait_ge(padding_zeroed, len(zeroed))
            with nc.allow_non_contiguous_dma("biases and small tables, a value per partition"):
                for to, of in loads[1::2]:
                    act.dma_start(to, of).then_inc(by_act, 16)
            if loads[1::2]:
                act.wait_ge(by_act, 16 * len(loads[1::2]))


def take_stage(core, b):
    nc = core.nc
    with stage(nc, "taken") as (block, taken):
        @block.vector
        def _(dve):
            nc.vector.tensor_copy(core.x[:], core.x_all[:, bass.ds(b, 1)].rearrange("p o t d -> p (o t) d")).then_inc(taken, 1)
            dve.wait_ge(taken, 1)


def product_stage(core, jobs):
    nc = core.nc

    def emptied_before(j, engine):
        return sum(job.engine == engine for job in jobs[:j])

    with stage(nc, "products_ready", "emptied_by_act", "emptied_by_dve", "dve_step") as (
            block, products_ready, emptied_by_act, emptied_by_dve, dve_step):
        @block.tensor
        def _(pe):
            for j, job in enumerate(jobs):
                if j >= BANKS:
                    last = jobs[j - BANKS].engine
                    pe.wait_ge(emptied_by_act if last == "act" else emptied_by_dve,
                               emptied_before(j - BANKS + 1, last))
                job.multiply(core.bank(j)).then_inc(products_ready, 1)

        @block.scalar
        def _(act):
            for j, job in enumerate(jobs):
                if job.engine == "act":
                    act.wait_ge(products_ready, j + 1)
                    job.evacuate(core.bank(j)).then_inc(emptied_by_act, 1)

        @block.vector
        def _(dve):
            step = stepper(dve, dve_step)
            for j, job in enumerate(jobs):
                if job.engine == "dve":
                    dve.wait_ge(products_ready, j + 1)
                    step(job.evacuate(core.bank(j)))
                    nc.vector.sem_inc(emptied_by_dve, 1)


def norm_stage(core, source, out, add=None, total=None):
    nc = core.nc
    with stage(nc, "dve_step", "variance_ready", "root_ready") as (block, dve_step, variance_ready, root_ready):
        @block.vector
        def _(dve):
            step = stepper(dve, dve_step)
            y = source
            if add is not None:
                y = total
                step(nc.vector.tensor_tensor(total, source, add, ALU.add))
            for t in range(TT):
                step(nc.vector.bn_stats(core.stats[:, t], y[:, t]))
            for t in range(TT):
                step(nc.vector.bn_aggr(core.moments[:, t], core.stats[:, t]))
            nc.vector.tensor_scalar(core.spread[:], core.moments[:, :, 1], EPS, None, ALU.add).then_inc(variance_ready, 1)
            dve.wait_ge(root_ready, 1)
            step(nc.vector.reciprocal(core.rstd[:], core.rstd[:]))
            for t in range(TT):
                step(nc.vector.tensor_scalar(out(t), y[:, t], core.moments[:, t, 0:1], core.rstd[:, t:t + 1],
                                             ALU.subtract, ALU.mult))

        @block.scalar
        def _(act):
            act.wait_ge(variance_ready, 1)
            nc.scalar.activation(core.rstd[:], core.spread[:], ACT.Sqrt).then_inc(root_ready, 1)


def residual_norm(core, b, delta=None):
    delta = core.delta if delta is None else delta
    norm_stage(core, core.x[:], lambda t: core.x_all[:, bass.ds(b, 1), t].rearrange("p o d -> p (o d)"), add=delta[:], total=delta[:])



def out_of_bank(core, engine, to, scale=None, bias=None, func=None):
    nc = core.nc
    rows, cols = to.shape[0], to.shape[-1]

    def evacuate(bank):
        held = bank[0:rows, 0:cols]
        if engine == "act":
            if bias is None and scale is None:
                return nc.scalar.activation(to, held, func or ACT.Copy)
            return nc.scalar.activation(to, held, func or ACT.Identity, bias=0.0 if bias is None else bias,
                                        scale=1.0 if scale is None else scale)
        if scale is not None:
            return nc.vector.tensor_scalar(to, held, scale, bias, ALU.mult, ALU.add)
        if bias is not None:
            return nc.vector.tensor_scalar(to, held, bias, None, ALU.add)
        return nc.vector.tensor_copy(to, held)

    return evacuate


def accumulate(nc, out, terms):
    for i, (lhsT, rhs) in enumerate(terms):
        last = nc.tensor.matmul(out, lhsT, rhs, start=(i == 0), stop=(i == len(terms) - 1))
    return last


def turned(core, source, to, rows=S, scale=None, bias=None, features=DT):
    nc = core.nc
    jobs = []
    for f in range(features):
        for c in range(0, rows, BANK):
            width = min(BANK, rows - c)

            def multiply(bank, f=f, c=c, width=width):
                for o in range(0, width, P):
                    n = min(P, width - o)
                    last = nc.tensor.transpose(bank[:, o:o + n], source[0:n, (c + o) // P, f * P:(f + 1) * P],
                                               core.ident[0:n, 0:n])
                return last

            engine = ("act", "dve")[len(jobs) % 2]
            jobs.append(Job(multiply, engine, out_of_bank(
                core, engine, to[:, f, c:c + width],
                None if scale is None else scale[:, f:f + 1], None if bias is None else bias[:, f:f + 1])))
    return jobs


def turned_back(core, source, evacuations, features=DT):
    nc = core.nc
    jobs = []
    for t in range(TT):
        def multiply(bank, t=t):
            for f in range(features):
                last = nc.tensor.transpose(bank[:, f * P:(f + 1) * P], source[:, f, t * P:(t + 1) * P], core.ident[:])
            return last

        jobs.append(Job(multiply, *evacuations(t)))
    return jobs


def columns_out(core, weight, xT, to, n, m=P, bias=None, func=None, engines=("act", "dve")):
    nc = core.nc
    kts = weight.shape[1]
    jobs = []
    for o in range(weight.shape[2] // m):
        for c in range(0, n, BANK):
            w = min(BANK, n - c)
            engine = engines[len(jobs) % len(engines)]

            def multiply(bank, o=o, c=c, w=w):
                return accumulate(nc, bank[0:m, 0:w],
                                  [(weight[:, k, o * m:(o + 1) * m], xT[:, k, c:c + w]) for k in range(kts)])

            jobs.append(Job(multiply, engine, out_of_bank(core, engine, to[0:m, o, c:c + w],
                                                          bias=None if bias is None else bias[0:m, o:o + 1], func=func)))
    return jobs


def rows_out(core, xT, weight, n, cols, evacuation, bias_row=None):
    nc = core.nc
    jobs = []
    for t in range((n + P - 1) // P):
        r = kt_rows(n, t)

        def multiply(bank, t=t, r=r):
            terms = [(xT[:, k, t * P:t * P + r], weight[:, k, 0:cols]) for k in range(weight.shape[1])]
            if bias_row is not None:
                terms.append((core.ones[0:1, 0:r], bias_row))
            return accumulate(nc, bank[0:r, 0:cols], terms)

        jobs.append(Job(multiply, *evacuation(t, r)))
    return jobs


def into(core, to):
    def evacuation(t, r=P):
        engine = ("act", "dve")[t % 2]
        return engine, out_of_bank(core, engine, to[0:r, t])
    return evacuation


def added_to(core, other, to):
    def evacuation(t, r=P):
        return "dve", lambda bank: core.nc.vector.tensor_tensor(to[0:r, t], bank[0:r, 0:to.shape[2]], other[0:r, t], ALU.add)
    return evacuation


def columned(v, p=P):
    return v.rearrange("(t p) -> p t", p=p)


def rowed(v):
    return v.rearrange("(a n) -> a n", a=1)


def spread_over(v):
    return v.partition_broadcast(P)


def slotted_weight(padded, w):
    pv = padded[:].rearrange("p k (h s) -> p k h s", s=32)
    wv = w.rearrange("(k p) (h s) -> p k h s", p=padded.shape[0], s=16)
    return [(pv[:, k, :, 0:16], wv[:, k]) for k in range(padded.shape[1])]


def slotted_bias(padded, v):
    view = v.rearrange("(g h s) -> h s g", h=4, s=16)
    return [(padded[32 * h:32 * h + 16, :], view[h]) for h in range(4)]



@dataclass
class Heads:
    qT: object
    kT: object
    v: object
    out: object
    groups: int
    heads: int
    dh: int
    keys: int
    scale: float
    blocks: object
    valid: object = None
    top: int = 0


def attention_stage(core, a, g, bufs):
    nc = core.nc
    slot = P // a.heads
    tiles = [(h, q) for q in range(TT) for h in range(a.heads)]
    N = len(tiles)
    KT = (a.keys + P - 1) // P
    qg, kg, vg, og = bufs.qg, bufs.kg, bufs.vg, bufs.og
    top = a.top
    psT = core.psum[:, 4 * BANK:6 * BANK]
    psO = core.psum[:, 6 * BANK:8 * BANK]

    def span(q):
        bl = a.blocks(q)
        k0 = bl[0][0] * P
        return bl, k0, min(a.keys, (bl[-1][0] + 1) * P) - k0

    chunks = []
    first_chunk = []
    for n, (h, q) in enumerate(tiles):
        bl, k0, width = span(q)
        first_chunk.append(len(chunks))
        i = 0
        while i < len(bl):
            rows = kt_rows(a.keys, bl[i][0])
            m = 1
            while i + m < len(bl) and m < 4 and kt_rows(a.keys, bl[i + m][0]) == rows:
                m += 1
            chunks.append((n, i, m, rows))
            i += m
    first_chunk.append(len(chunks))

    with stage(nc, "q_copied", "k_copied", "v_copied", "scores_ready", "scores_copied", "max_ready", "exp_ready",
               "probs_ready", "turned_ready", "turned_copied", "out_ready", "out_kept", "dve_step") as (
            block, q_copied, k_copied, v_copied, scores_ready, scores_copied, max_ready, exp_ready, probs_ready,
            turned_ready, turned_copied, out_ready, out_kept, dve_step):
        probs_done = probs_ready if top else exp_ready

        @block.tensor
        def _(pe):
            pe.wait_ge(q_copied, 1)
            pe.wait_ge(k_copied, 1)
            pe.wait_ge(v_copied, 1)

            def scores(n):
                h, q = tiles[n]
                bl, k0, width = span(q)
                if n >= 1:
                    pe.wait_ge(scores_copied if top else exp_ready, n)
                lo = h * slot
                for c in range(0, width, BANK):
                    w = min(BANK, width - c)
                    masks = [(kt, mask) for kt, mask in bl if mask is not None and c <= kt * P - k0 < c + w]
                    last = nc.tensor.matmul(core.psum[:, c:c + w], qg[lo:lo + a.dh, q * P:(q + 1) * P],
                                            kg[lo:lo + a.dh, k0 + c:k0 + c + w], start=True, stop=not masks)
                    for i, (kt, mask) in enumerate(masks):
                        o = kt * P - k0
                        r = kt_rows(a.keys, kt)
                        last = nc.tensor.matmul(core.psum[:, o:o + r], core.ident[:], mask[:, 0:r],
                                                start=False, stop=(i == len(masks) - 1))
                last.then_inc(scores_ready, 1)

            def values(n):
                h, q = tiles[n]
                bl, k0, width = span(q)
                pe.wait_ge(probs_done, n + 1)
                for c in range(first_chunk[n], first_chunk[n + 1]):
                    _, i, m, rows = chunks[c]
                    if c >= 2:
                        pe.wait_ge(turned_copied, c - 1)
                    for j in range(m):
                        last = nc.tensor.transpose(psT[0:rows, (c % 2) * BANK + j * P:(c % 2) * BANK + (j + 1) * P],
                                                   bufs.probs[:, n % 2, (i + j) * P:(i + j) * P + rows], core.ident[:])
                    last.then_inc(turned_ready, 1)
                if n >= 2:
                    pe.wait_ge(out_kept, n - 1)
                pe.wait_ge(turned_copied, first_chunk[n + 1])
                for i, (kt, _) in enumerate(bl):
                    rows = kt_rows(a.keys, kt)
                    last = nc.tensor.matmul(psO[:, (n % 2) * BANK:(n % 2) * BANK + a.dh],
                                            bufs.pT[0:rows, n % 2, i * P:(i + 1) * P],
                                            vg[0:rows, kt, h * a.dh:(h + 1) * a.dh],
                                            start=(i == 0), stop=(i == len(bl) - 1))
                last.then_inc(out_ready, 1)

            for n in range(N + 1):
                if n < N:
                    scores(n)
                if n >= 1:
                    values(n - 1)

        def copy_turned(engine, copy, n):
            for c in range(first_chunk[n], first_chunk[n + 1]):
                _, i, m, rows = chunks[c]
                engine.wait_ge(turned_ready, c + 1)
                if n >= 2 and c == first_chunk[n]:
                    engine.wait_ge(out_ready, n - 1)
                copy(bufs.pT[0:rows, n % 2, i * P:(i + m) * P],
                     psT[0:rows, (c % 2) * BANK:(c % 2) * BANK + m * P]).then_inc(turned_copied, 1)

        @block.scalar
        def _(act):
            nc.scalar.copy(qg[:], a.qT[:, bass.ds(g, 1), :].rearrange("p o n -> p (o n)")).then_inc(q_copied, 1)
            nc.scalar.copy(kg[:, 0:a.keys], a.kT[:, bass.ds(g, 1), :].rearrange("p o n -> p (o n)")).then_inc(k_copied, 1)

            def exponentials(n):
                h, q = tiles[n]
                _, _, width = span(q)
                if top:
                    act.wait_ge(scores_ready, n + 1)
                    if n >= 2:
                        act.wait_ge(probs_ready, n - 1)
                    nc.scalar.copy(bufs.raw[:, n % 2, 0:width], core.psum[:, 0:width]).then_inc(scores_copied, 1)
                    act.wait_ge(scores_copied, n + 1)
                act.wait_ge(max_ready, n + 1)
                source = bufs.raw[:, n % 2, 0:width] if top else core.psum[:, 0:width]
                to = bufs.exps[:, n % 2, 0:width] if top else bufs.probs[:, n % 2, 0:width]
                if n >= 2 and not top:
                    act.wait_ge(out_ready, n - 1)
                nc.scalar.activation(to, source, ACT.Exp, bias=bufs.negmax[:, n:n + 1], scale=a.scale,
                                     accum_out=(bufs.unused if top else bufs.total)[:, n:n + 1]).then_inc(exp_ready, 1)

            for n in range(N + 1):
                if n < N:
                    exponentials(n)
                if n >= 1 and top:
                    copy_turned(act, nc.scalar.copy, n - 1)

        @block.vector
        def _(dve):
            step = stepper(dve, dve_step)
            full = KT if kt_rows(a.keys, KT - 1) == P else KT - 1
            if full:
                step(nc.vector.tensor_copy(vg[:, 0:full, :], a.v[:, 0:full, bass.ds(g * (a.heads * a.dh), a.heads * a.dh)]))
            if full < KT:
                r = kt_rows(a.keys, KT - 1)
                step(nc.vector.tensor_copy(vg[0:r, full, :], a.v[0:r, full, bass.ds(g * (a.heads * a.dh), a.heads * a.dh)]))
            dve.sem_inc(v_copied, 1)

            def maximum(n):
                h, q = tiles[n]
                _, _, width = span(q)
                dve.wait_ge(scores_ready, n + 1)
                step(nc.vector.reduce_max(bufs.negmax[:, n:n + 1], core.psum[:, 0:width], AX.X))
                nc.vector.tensor_scalar(bufs.negmax[:, n:n + 1], bufs.negmax[:, n:n + 1], -a.scale, None,
                                        ALU.mult).then_inc(max_ready, 1)

            def keep_top(n):
                h, q = tiles[n]
                _, _, width = span(q)
                raw = bufs.raw[:, n % 2, 0:width]
                left = bufs.left[:, 0:width]
                dve.wait_ge(scores_copied, n + 1)
                source = raw
                for i in range(top // 8):
                    step(nc.vector.max(bufs.best[:], source))
                    if i == 0:
                        nc.vector.tensor_scalar(bufs.negmax[:, n:n + 1], bufs.best[:, 0:1], -a.scale, None,
                                                ALU.mult).then_inc(max_ready, 1)
                    step(nc.vector.match_replace(left, bufs.best[:], source, TAKEN))
                    source = left
                dve.wait_ge(exp_ready, n + 1)
                if n >= 2:
                    dve.wait_ge(out_ready, n - 1)
                nc.vector.scalar_tensor_tensor(out=bufs.probs[:, n % 2, 0:width], in0=left, scalar=TAKEN / 2,
                                               in1=bufs.exps[:, n % 2, 0:width], op0=ALU.is_lt, op1=ALU.mult,
                                               accum_out=bufs.total[:, n:n + 1]).then_inc(probs_ready, 1)

            def keep_out(n):
                h, q = tiles[n]
                dve.wait_ge(probs_done, n + 1)
                step(nc.vector.reciprocal(bufs.share[:, n:n + 1], bufs.total[:, n:n + 1]))
                if a.valid is not None:
                    step(nc.vector.tensor_tensor(bufs.share[:, n:n + 1], bufs.share[:, n:n + 1], a.valid[:, q:q + 1], ALU.mult))
                dve.wait_ge(out_ready, n + 1)
                nc.vector.tensor_scalar(og[:, q, h * a.dh:(h + 1) * a.dh], psO[:, (n % 2) * BANK:(n % 2) * BANK + a.dh],
                                        bufs.share[:, n:n + 1], None, ALU.mult).then_inc(out_kept, 1)

            if top:
                for n in range(N + 1):
                    if n < N:
                        keep_top(n)
                    if n >= 2:
                        keep_out(n - 2)
                keep_out(N - 1)
            else:
                for n in range(N + 2):
                    if n < N:
                        maximum(n)
                    if n >= 2:
                        keep_out(n - 2)
                    if 1 <= n <= N:
                        copy_turned(dve, nc.vector.tensor_copy, n - 1)
            dve.wait_ge(out_kept, N)
            step(nc.vector.tensor_copy(a.out[:, :, bass.ds(g * (a.heads * a.dh), a.heads * a.dh)], og[:]))


@dataclass
class Buffers:
    qg: object
    kg: object
    vg: object
    og: object
    probs: object
    pT: object
    negmax: object
    total: object
    share: object
    raw: object = None
    left: object = None
    exps: object = None
    best: object = None
    unused: object = None


def attention_groups(core, a):
    nc = core.nc
    KT = (a.keys + P - 1) // P
    with ExitStack() as ctx:
        sb = lambda name, shape: ctx.enter_context(nc.sbuf_tensor(core.named(name), shape, F32))
        n = a.heads * TT
        bufs = Buffers(qg=sb("qg", [P, S]), kg=sb("kg", [P, a.keys]), vg=sb("vg", [P, KT, a.heads * a.dh]),
                       og=sb("og", [P, TT, a.heads * a.dh]), probs=sb("probs", [P, 2, a.keys]),
                       pT=sb("pT", [P, 2, KT * P]), negmax=sb("negmax", [P, n]), total=sb("total", [P, n]),
                       share=sb("share", [P, n]))
        if a.top:
            bufs.raw, bufs.exps = sb("raw", [P, 2, a.keys]), sb("exps", [P, 2, a.keys])
            bufs.left, bufs.best, bufs.unused = sb("left", [P, a.keys]), sb("best", [P, 8]), sb("unused", [P, n])
        with nc.Fori(0, a.groups) as g:
            attention_stage(core, a, g, bufs)


def all_blocks(keys):
    return lambda q: [(kt, None) for kt in range((keys + P - 1) // P)]


def causal_blocks(core):
    return lambda q: [(kt, None) for kt in range(q)] + [(q, core.causal)]


def context_columns(core, ctx_in, b, ctxT):
    nc = core.nc
    with ExitStack() as held:
        rows = held.enter_context(nc.sbuf_tensor(core.named("ctx_rows"), [P, MT, D], F32))
        context_load(core, ctx_in, b, rows)
        product_stage(core, turned(core, rows, ctxT, rows=M))


def context_load(core, ctx_in, b, rows):
    nc = core.nc
    full = M // P
    with stage(nc, "context_loaded") as (block, context_loaded):
        @block.sync
        def _(sp):
            here = ctx_in[bass.ds(b, 1)]
            sp.dma_start(rows[:, 0:full], here[:, 0:full * P].rearrange("o (t p) d -> p (o t) d", p=P)).then_inc(context_loaded, 16)
            sp.dma_start(rows[0:M - full * P, full], here[:, full * P:M].rearrange("o p d -> p (o d)")).then_inc(context_loaded, 16)
            sp.wait_ge(context_loaded, 32)


def head_weights(sb, name, kts=DT):
    return sb(name, [P, kts, 512])



def matrix(w, p=P):
    return w.rearrange("(k p) n -> p k n", p=p)


def l0_attn(core, w):
    nc = core.nc
    FF = w["L0_attn_ff_w1"].shape[1]
    STEPS, STEP = 8, 0.1
    with ExitStack() as ctx:
        sb = lambda name, shape: ctx.enter_context(nc.sbuf_tensor(core.named(name), shape, F32))
        wq, wk, wv = sb("wq", [P, DT, 512]), sb("wk", [P, DT, 512]), sb("wv", [P, DT, D])
        bq, bk, bv = sb("bq", [P, 4]), sb("bk", [P, 4]), sb("bv", [1, D])
        wo, bo_col, bo_row = sb("wo", [P, DT, D]), sb("bo_col", [P, DT]), sb("bo_row", [1, D])
        gains = {k: sb(k, [P, DT]) for k in ("g_attn", "b_attn", "g1", "b1", "g2", "b2", "b_inl")}
        w_ctx, w_x = sb("w_ctx", [P, DT, D]), sb("w_x", [P, DT, D])
        ff1, ff1_b = sb("ff1", [P, DT, FF]), sb("ff1_b", [P, FF // P])
        ff2, ff2_b = sb("ff2", [P, FF // P, D]), sb("ff2_b", [1, D])
        qkv, qkv_b = w["L0_attn_qkv_w"], w["L0_attn_qkv_b"]
        load_stage(core, [
            *slotted_weight(wq, qkv[:, 0:D]), *slotted_weight(wk, qkv[:, D:2 * D]), (wv[:], matrix(qkv[:, 2 * D:3 * D])),
            *slotted_bias(bq, qkv_b[0:D]), *slotted_bias(bk, qkv_b[D:2 * D]), (bv[:], rowed(qkv_b[2 * D:3 * D])),
            (wo[:], matrix(w["L0_attn_out_w"])), (bo_col[:], columned(w["L0_attn_out_b"])), (bo_row[:], rowed(w["L0_attn_out_b"])),
            *[(t[:], columned(w["L0_attn_" + k])) for k, t in gains.items()],
            (w_ctx[:], matrix(w["L0_attn_w_ctx"])), (w_x[:], matrix(w["L0_attn_w_x"])),
            (ff1[:], matrix(w["L0_attn_ff_w1"])), (ff1_b[:], columned(w["L0_attn_ff_b1"])),
            (ff2[:], matrix(w["L0_attn_ff_w2"])), (ff2_b[:], rowed(w["L0_attn_ff_b2"])),
        ], zeroed=[wq[:], wk[:], bq[:], bk[:]])

        y = sb("y", [P, TT, D])
        qT, kT = sb("qT", [P, 4, S]), sb("kT", [P, 4, S])
        v, o, oT = sb("v", [P, TT, D]), sb("o", [P, TT, D]), sb("oT", [P, DT, S])
        attnT, drive = sb("attnT", [P, DT, S]), sb("drive", [P, DT, S])
        state, speed, u = sb("state", [P, DT, S]), sb("speed", [P, DT, S]), sb("u", [P, DT, S])
        hT = sb("hT", [P, FF // P, S])
        with nc.Fori(0, B) as b:
            take_stage(core, b)
            norm_stage(core, core.x[:], lambda t: y[:, t])
            product_stage(core, turned(core, y, core.xT, scale=gains["g_attn"], bias=gains["b_attn"]))
            product_stage(core, [
                *columns_out(core, wq, core.xT, qT, S, bias=bq), *columns_out(core, wk, core.xT, kT, S, bias=bk),
                *rows_out(core, core.xT, wv, S, D, into(core, v), bias_row=bv[:])])
            attention_groups(core, Heads(qT, kT, v, o, 4, 4, 16, S, 0.25, causal_blocks(core)))
            product_stage(core, turned(core, o, oT))
            product_stage(core, [
                *columns_out(core, wo, oT, attnT, S, bias=bo_col),
                *rows_out(core, oT, wo, S, D, added_to(core, core.x, core.delta), bias_row=bo_row[:])])
            norm_stage(core, core.delta[:], lambda t: y[:, t])
            product_stage(core, [
                *turned(core, y, state, scale=gains["g1"], bias=gains["b1"]),
                *columns_out(core, w_ctx, attnT, drive, S, bias=gains["b_inl"])])
            with stage(nc, "speed_zeroed") as (block, speed_zeroed):
                @block.gpsimd
                def _(pool):
                    pool.memset(speed[:], 0.0).then_inc(speed_zeroed, 1)
                    pool.wait_ge(speed_zeroed, 1)
            with nc.Fori(0, STEPS) as _i:
                recurrence_stage(core, w_x, drive, state, speed, u, STEP)
            product_stage(core, turned_back(core, state, added_to(core, core.delta, core.delta)))
            norm_stage(core, core.delta[:], lambda t: y[:, t])
            product_stage(core, turned(core, y, core.xT, scale=gains["g2"], bias=gains["b2"]))
            product_stage(core, columns_out(core, ff1, core.xT, hT, S, bias=ff1_b, func=ACT.Gelu, engines=("act",)))
            product_stage(core, rows_out(core, hT, ff2, S, D, added_to(core, core.delta, core.delta), bias_row=ff2_b[:]))
            residual_norm(core, b)


def recurrence_stage(core, w_x, drive, state, speed, u, step_size):
    nc = core.nc
    with stage(nc, "products_ready", "summed", "tanh_ready", "dve_step") as (block, products_ready, summed, tanh_ready, dve_step):
        @block.tensor
        def _(pe):
            for f in range(DT):
                accumulate(nc, core.bank(f), [(w_x[:, k, f * P:(f + 1) * P], state[:, k]) for k in range(DT)]
                           ).then_inc(products_ready, 1)

        @block.vector
        def _(dve):
            step = stepper(dve, dve_step)
            for f in range(DT):
                dve.wait_ge(products_ready, f + 1)
                nc.vector.tensor_tensor(u[:, f], core.bank(f), drive[:, f], ALU.add).then_inc(summed, 1)
            for f in range(DT):
                dve.wait_ge(tanh_ready, f + 1)
                dve.wait_ge(products_ready, DT)
                step(nc.vector.tensor_tensor(u[:, f], u[:, f], state[:, f], ALU.subtract))
                step(nc.vector.scalar_tensor_tensor(out=speed[:, f], in0=speed[:, f], scalar=1.0 - step_size, in1=u[:, f],
                                                    op0=ALU.mult, op1=ALU.add))
                step(nc.vector.scalar_tensor_tensor(out=state[:, f], in0=speed[:, f], scalar=step_size * step_size,
                                                    in1=state[:, f], op0=ALU.mult, op1=ALU.add))

        @block.scalar
        def _(act):
            for f in range(DT):
                act.wait_ge(summed, f + 1)
                nc.scalar.activation(u[:, f], u[:, f], ACT.Tanh).then_inc(tanh_ready, 1)


def l0_xattn(core, w, ctx_in):
    nc = core.nc
    INNER = w["L0_xattn_Wq"].shape[1]
    with ExitStack() as ctx:
        sb = lambda name, shape: ctx.enter_context(nc.sbuf_tensor(core.named(name), shape, F32))
        wq, wk, wv = (sb(n, [P, DT, INNER]) for n in ("wq", "wk", "wv"))
        wo, bo = sb("wo", [P, INNER // P, D]), sb("bo", [1, D])
        load_stage(core, [(wq[:], matrix(w["L0_xattn_Wq"])), (wk[:], matrix(w["L0_xattn_Wk"])),
                          (wv[:], matrix(w["L0_xattn_Wv"])), (wo[:], matrix(w["L0_xattn_Wo"])),
                          (bo[:], rowed(w["L0_xattn_bo"]))])
        qT, kT = sb("qT", [P, 4, S]), sb("kT", [P, 4, M])
        v, o = sb("v", [P, MT, INNER]), sb("o", [P, TT, INNER])
        with nc.Fori(0, B) as b:
            take_stage(core, b)
            product_stage(core, turned(core, core.x, core.xT))
            with ExitStack() as early:
                ctxT = early.enter_context(nc.sbuf_tensor(core.named("ctxT"), [P, DT, M], F32))
                context_columns(core, ctx_in, b, ctxT)
                product_stage(core, [
                    *columns_out(core, wq, core.xT, qT, S), *columns_out(core, wk, ctxT, kT, M),
                    *rows_out(core, ctxT, wv, M, INNER, into(core, v))])
            attention_groups(core, Heads(qT, kT, v, o, 4, 2, 64, M, 64 ** -0.5, all_blocks(M)))
            with ExitStack() as late:
                oT = late.enter_context(nc.sbuf_tensor(core.named("oT"), [P, INNER // P, S], F32))
                product_stage(core, turned(core, o, oT, features=INNER // P))
                product_stage(core, rows_out(core, oT, wo, S, D, into(core, core.delta), bias_row=bo[:]))
            residual_norm(core, b)


def l0_ffn(core, w):
    nc = core.nc
    with ExitStack() as ctx:
        sb = lambda name, shape, dt=F32: ctx.enter_context(nc.sbuf_tensor(core.named(name), shape, dt))
        packed, codes = sb("packed", [64, D], I32), sb("codes", [64, 4, D], I32)
        ternary, wT = sb("ternary", [64, 4, D]), sb("wT", [P, DT, D])
        scale, bias = sb("scale", [P, 1]), sb("bias", [P, D])
        load_stage(core, [(packed[:], w["L0_ffn_packed_weight"].rearrange("(r c) -> r c", c=D)),
                          (scale[:], spread_over(w["L0_ffn_weight_scale"])), (bias[:], spread_over(w["L0_ffn_bias"]))])
        with stage(nc, "dve_step") as (block, dve_step):
            @block.vector
            def _(dve):
                step = stepper(dve, dve_step)
                for s in range(4):
                    step(nc.vector.tensor_scalar(codes[:, s], packed[:], 2 * s, 3, ALU.logical_shift_right, ALU.bitwise_and))
                step(nc.vector.tensor_copy(ternary[:], codes[:]))
                step(nc.vector.tensor_scalar(ternary[:], ternary[:], 1.0, None, ALU.subtract))

        def turn(f):
            def multiply(bank):
                for s in range(4):
                    last = nc.tensor.transpose(bank[:, 64 * s:64 * s + 64], ternary[:, s, f * P:(f + 1) * P], core.ident[0:64, 0:64])
                return last
            return multiply

        product_stage(core, [Job(turn(f), "dve", out_of_bank(core, "dve", wT[:, f])) for f in range(DT)])
        xq = sb("xq", [P, TT, D])
        peak, gain, back = sb("peak", [P, TT]), sb("gain", [P, TT]), sb("back", [P, TT])
        with nc.Fori(0, B) as b:
            take_stage(core, b)
            with stage(nc, "dve_step") as (block, dve_step):
                @block.vector
                def _(dve):
                    step = stepper(dve, dve_step)
                    step(nc.vector.tensor_reduce(peak[:], core.x[:], AX.X, ALU.max, apply_absolute_value=True))
                    step(nc.vector.tensor_scalar(peak[:], peak[:], 1e-5, None, ALU.max))
                    step(nc.vector.reciprocal(gain[:], peak[:]))
                    step(nc.vector.tensor_scalar(gain[:], gain[:], 127.0, None, ALU.mult))
                    step(nc.vector.reciprocal(back[:], gain[:]))
                    for t in range(TT):
                        step(nc.vector.tensor_scalar(xq[:, t], core.x[:, t], gain[:, t:t + 1], None, ALU.mult))
                    step(nc.vector.tensor_scalar(xq[:], xq[:], ROUND, None, ALU.add))
                    step(nc.vector.tensor_scalar(xq[:], xq[:], ROUND, None, ALU.subtract))
                    step(nc.vector.tensor_scalar(xq[:], xq[:], -128.0, 127.0, ALU.max, ALU.min))
                    for t in range(TT):
                        step(nc.vector.tensor_scalar(xq[:, t], xq[:, t], back[:, t:t + 1], None, ALU.mult))
            product_stage(core, turned(core, xq, core.xT))
            product_stage(core, rows_out(core, core.xT, wT, S, D, lambda t, r: ("dve", lambda bank: (
                nc.vector.scalar_tensor_tensor(out=core.delta[:, t], in0=bank[:, 0:D], scalar=scale[:, 0:1], in1=bias[:],
                                               op0=ALU.mult, op1=ALU.add)))))
            residual_norm(core, b)


def l1_attn(core, w):
    nc = core.nc
    C = w["L1_attn_W_dq"].shape[1]
    with ExitStack() as ctx:
        sb = lambda name, shape: ctx.enter_context(nc.sbuf_tensor(core.named(name), shape, F32))
        w_dq, w_dkv = sb("w_dq", [P, DT, C]), sb("w_dkv", [P, DT, C])
        w_uq, w_uk, w_uv = sb("w_uq", [C, 1, 512]), sb("w_uk", [C, 1, 512]), sb("w_uv", [C, 1, D])
        wo = sb("wo", [P, DT, D])
        load_stage(core, [
            (w_dq[:], matrix(w["L1_attn_W_dq"])), (w_dkv[:], matrix(w["L1_attn_W_dkv"])),
            *slotted_weight(w_uq, w["L1_attn_W_uq"]), *slotted_weight(w_uk, w["L1_attn_W_uk"]),
            (w_uv[:], matrix(w["L1_attn_W_uv"], C)), (wo[:], matrix(w["L1_attn_W_o"])),
        ], zeroed=[w_uq[:], w_uk[:]])
        cqT, ckvT = sb("cqT", [C, 1, S]), sb("ckvT", [C, 1, S])
        qT, kT = sb("qT", [P, 4, S]), sb("kT", [P, 4, S])
        v, o, oT = sb("v", [P, TT, D]), sb("o", [P, TT, D]), sb("oT", [P, DT, S])
        with nc.Fori(0, B) as b:
            take_stage(core, b)
            product_stage(core, turned(core, core.x, core.xT))
            product_stage(core, [*columns_out(core, w_dq, core.xT, cqT, S, m=C), *columns_out(core, w_dkv, core.xT, ckvT, S, m=C)])
            product_stage(core, [*columns_out(core, w_uq, cqT, qT, S), *columns_out(core, w_uk, ckvT, kT, S),
                                 *rows_out(core, ckvT, w_uv, S, D, into(core, v))])
            attention_groups(core, Heads(qT, kT, v, o, 4, 4, 16, S, 0.25, causal_blocks(core)))
            product_stage(core, turned(core, o, oT))
            product_stage(core, rows_out(core, oT, wo, S, D, into(core, core.delta)))
            residual_norm(core, b)


def l1_xattn(core, w, ctx_in):
    nc = core.nc
    R = w["L1_xattn_Uq"].shape[1]
    assert R == P
    with ExitStack() as ctx:
        sb = lambda name, shape: ctx.enter_context(nc.sbuf_tensor(core.named(name), shape, F32))
        up = {k: sb("up_" + k, [P, DT, R]) for k in "qkvo"}
        down = {k: sb("down_" + k, [R, 1, 512 if k in "qk" else D]) for k in "qkvo"}
        bq, bk, bv, bo = sb("bq", [P, 4]), sb("bk", [P, 4]), sb("bv", [1, D]), sb("bo", [1, D])
        with ExitStack() as early:
            V = {k: early.enter_context(nc.sbuf_tensor(core.named("V" + k), [P, DT, R], F32)) for k in "qkvo"}
            load_stage(core, [
                *[(up[k][:], matrix(w["L1_xattn_U" + k])) for k in "qkvo"], *[(V[k][:], matrix(w["L1_xattn_V" + k])) for k in "qkvo"],
                *slotted_bias(bq, w["L1_xattn_bq"]), *slotted_bias(bk, w["L1_xattn_bk"]),
                (bv[:], rowed(w["L1_xattn_bv"])), (bo[:], rowed(w["L1_xattn_bo"])),
            ], zeroed=[down["q"][:], down["k"][:], bq[:], bk[:]])

            def turn(k):
                def multiply(bank):
                    for f in range(DT):
                        last = nc.tensor.transpose(bank[:, f * P:(f + 1) * P], V[k][:, f], core.ident[:])
                    return last

                def evacuate(bank):
                    if k in "vo":
                        return nc.vector.tensor_copy(down[k][:, 0], bank[:, 0:D])
                    slots = down[k][:, 0].rearrange("p (h s) -> p h s", s=32)[:, :, 0:16]
                    return nc.vector.tensor_copy(slots, bank[:, 0:D].rearrange("p (h s) -> p h s", s=16))
                return Job(multiply, "dve", evacuate)

            product_stage(core, [turn(k) for k in "qkvo"])
        qT, kT = sb("qT", [P, 4, S]), sb("kT", [P, 4, M])
        v, o = sb("v", [P, MT, D]), sb("o", [P, TT, D])
        with nc.Fori(0, B) as b:
            take_stage(core, b)
            product_stage(core, turned(core, core.x, core.xT))
            with ExitStack() as early:
                ctxT = early.enter_context(nc.sbuf_tensor(core.named("ctxT"), [P, DT, M], F32))
                low_q, low_k, low_v = (early.enter_context(nc.sbuf_tensor(core.named("low_" + k), [P, 1, S if k == "q" else M], F32)) for k in "qkv")
                context_columns(core, ctx_in, b, ctxT)
                product_stage(core, [*columns_out(core, up["q"], core.xT, low_q, S),
                                     *columns_out(core, up["k"], ctxT, low_k, M), *columns_out(core, up["v"], ctxT, low_v, M)])
                product_stage(core, [*columns_out(core, down["q"], low_q, qT, S, bias=bq), *columns_out(core, down["k"], low_k, kT, M, bias=bk),
                                     *rows_out(core, low_v, down["v"], M, D, into(core, v), bias_row=bv[:])])
            attention_groups(core, Heads(qT, kT, v, o, 4, 4, 16, M, 0.25, all_blocks(M), top=64))
            with ExitStack() as late:
                oT, low_o = (late.enter_context(nc.sbuf_tensor(core.named(n), [P, k, S], F32)) for n, k in (("oT", DT), ("low_o", 1)))
                product_stage(core, turned(core, o, oT))
                product_stage(core, columns_out(core, up["o"], oT, low_o, S))
                product_stage(core, rows_out(core, low_o, down["o"], S, D, into(core, core.delta), bias_row=bo[:]))
            residual_norm(core, b)


def first_of_equal(nc, step, onehot, values, best, ties, counted, ones):
    rows, n = values.shape[1], values.shape[2]
    step(nc.vector.tensor_tensor(ties, values, best.unsqueeze(2).to_broadcast([values.shape[0], rows, n]), ALU.is_equal))
    for t in range(rows):
        step(nc.vector.tensor_tensor_scan(counted[:, t], ties[:, t], ones, 0.0, ALU.add, ALU.mult))
    step(nc.vector.scalar_tensor_tensor(out=onehot, in0=counted, scalar=1.0, in1=ties, op0=ALU.is_equal, op1=ALU.mult))


def l1_ffn(core, w):
    nc = core.nc
    E, _, H = w["L1_ffn_W1"].shape
    HT = H // P
    with ExitStack() as ctx:
        sb = lambda name, shape: ctx.enter_context(nc.sbuf_tensor(core.named(name), shape, F32))
        wg, bg = sb("wg", [P, DT, E]), sb("bg", [1, E])
        w1, b1 = sb("w1", [P, E, DT, H]), sb("b1", [P, E, HT])
        w2, b2 = sb("w2", [P, E, HT, D]), sb("b2", [E, D])
        load_stage(core, [
            (wg[:], matrix(w["L1_ffn_Wg"])), (bg[:], rowed(w["L1_ffn_bg"])), (b2[:], w["L1_ffn_b2"]),
            *[(w1[:, e], matrix(w["L1_ffn_W1"][e])) for e in range(E)], *[(w2[:, e], matrix(w["L1_ffn_W2"][e])) for e in range(E)],
            *[(b1[:, e], columned(w["L1_ffn_b1"][e])) for e in range(E)]])
        logits, ties, counted = (sb(n, [P, TT, E]) for n in ("logits", "ties", "counted"))
        first, second, mix = (sb(n, [P, TT, E]) for n in ("first", "second", "mix"))
        top1, top2, ratio = (sb(n, [P, TT]) for n in ("top1", "top2", "ratio"))
        mixT, hT = sb("mixT", [E, S]), sb("hT", [P, 2, HT, S])
        with nc.Fori(0, B) as b:
            take_stage(core, b)
            product_stage(core, turned(core, core.x, core.xT))
            product_stage(core, rows_out(core, core.xT, wg, S, E, into(core, logits), bias_row=bg[:]))
            with stage(nc, "dve_step", "gap_ready", "ratio_ready") as (block, dve_step, gap_ready, ratio_ready):
                @block.vector
                def _(dve):
                    step = stepper(dve, dve_step)
                    step(nc.vector.reduce_max(top1[:], logits[:], AX.X))
                    first_of_equal(nc, step, first[:], logits[:], top1[:], ties[:], counted[:], core.ones[:, 0:E])
                    step(nc.vector.scalar_tensor_tensor(out=logits[:], in0=first[:], scalar=MASKED, in1=logits[:], op0=ALU.mult, op1=ALU.add))
                    step(nc.vector.reduce_max(top2[:], logits[:], AX.X))
                    first_of_equal(nc, step, second[:], logits[:], top2[:], ties[:], counted[:], core.ones[:, 0:E])
                    nc.vector.tensor_tensor(ratio[:], top2[:], top1[:], ALU.subtract).then_inc(gap_ready, 1)
                    dve.wait_ge(ratio_ready, 1)
                    step(nc.vector.tensor_scalar(top1[:], ratio[:], 1.0, None, ALU.add))
                    step(nc.vector.reciprocal(top1[:], top1[:]))
                    step(nc.vector.tensor_tensor(top2[:], ratio[:], top1[:], ALU.mult))
                    step(nc.vector.tensor_tensor(first[:], first[:], top1[:].unsqueeze(2).to_broadcast([P, TT, E]), ALU.mult))
                    step(nc.vector.tensor_tensor(second[:], second[:], top2[:].unsqueeze(2).to_broadcast([P, TT, E]), ALU.mult))
                    step(nc.vector.tensor_tensor(mix[:], first[:], second[:], ALU.add))

                @block.scalar
                def _(act):
                    act.wait_ge(gap_ready, 1)
                    nc.scalar.activation(ratio[:], ratio[:], ACT.Exp).then_inc(ratio_ready, 1)

            def turn_mix(bank):
                for t in range(TT):
                    last = nc.tensor.transpose(bank[0:E, t * P:(t + 1) * P], mix[:, t], core.ident[:])
                return last

            product_stage(core, [Job(turn_mix, "dve", out_of_bank(core, "dve", mixT[:]))])
            experts_stage(core, w1, b1, w2, b2, mix, mixT, hT)
            residual_norm(core, b)


def experts_stage(core, w1, b1, w2, b2, mix, mixT, hT):
    nc = core.nc
    E, HT = w1.shape[1], hT.shape[2]
    with stage(nc, "hidden_products", "hidden_ready", "out_products", "summed") as (
            block, hidden_products, hidden_ready, out_products, summed):
        @block.tensor
        def _(pe):
            for t in range(TT):
                nc.tensor.matmul(core.bank(4 + t)[:, 0:D], mixT[:, t * P:(t + 1) * P], b2[:], start=True, stop=True).then_inc(out_products, 1)

            def hidden(e):
                for h in range(HT):
                    if e >= 1:
                        pe.wait_ge(hidden_ready, HT * (e - 1) + h + 1)
                    accumulate(nc, core.bank(h), [(w1[:, e, k, h * P:(h + 1) * P], core.xT[:, k]) for k in range(DT)]
                               ).then_inc(hidden_products, 1)

            def output(e):
                pe.wait_ge(hidden_ready, HT * (e + 1))
                for t in range(TT):
                    pe.wait_ge(summed, TT * e + t + 1)
                    accumulate(nc, core.bank(4 + t)[:, 0:D], [(hT[:, e % 2, h, t * P:(t + 1) * P], w2[:, e, h]) for h in range(HT)]
                               ).then_inc(out_products, 1)

            hidden(0)
            for e in range(E):
                if e + 1 < E:
                    hidden(e + 1)
                output(e)

        @block.scalar
        def _(act):
            for e in range(E):
                for h in range(HT):
                    act.wait_ge(hidden_products, HT * e + h + 1)
                    if e >= 2:
                        act.wait_ge(out_products, TT * e)
                    nc.scalar.activation(hT[:, e % 2, h], core.bank(h), ACT.Gelu, bias=b1[:, e, h:h + 1]).then_inc(hidden_ready, 1)

        @block.vector
        def _(dve):
            for t in range(TT):
                dve.wait_ge(out_products, t + 1)
                nc.vector.tensor_copy(core.delta[:, t], core.bank(4 + t)[:, 0:D]).then_inc(summed, 1)
            for e in range(E):
                for t in range(TT):
                    dve.wait_ge(out_products, TT * (e + 1) + t + 1)
                    dve.wait_ge(summed, TT * e + t + 1)
                    nc.vector.scalar_tensor_tensor(out=core.delta[:, t], in0=core.bank(4 + t)[:, 0:D], scalar=mix[:, t, e:e + 1],
                                                   in1=core.delta[:, t], op0=ALU.mult, op1=ALU.add).then_inc(summed, 1)


def l2_attn(core, w):
    nc = core.nc
    NS = w["L2_attn_B"].shape[0]
    K = 9
    TWO_PI_HI, TWO_PI_MID, TWO_PI_LO = 6.28125, 0.0019350051879882812, 3.0199159819567e-07
    with ExitStack() as ctx:
        sb = lambda name, shape: ctx.enter_context(nc.sbuf_tensor(core.named(name), shape, F32))
        cosT, sinT, drive, decay = (sb(n, [P, S]) for n in ("cosT", "sinT", "drive", "decay"))
        inT, outP, outQ = sb("inT", [P, DT, P]), sb("outP", [P, D]), sb("outQ", [P, D])
        skip = sb("skip", [P, D])
        with ExitStack() as early:
            eb = lambda name, shape: early.enter_context(nc.sbuf_tensor(core.named(name), shape, F32))
            lar, aim, ls = eb("lar", [P, 1]), eb("aim", [P, 1]), eb("ls", [P, 1])
            b_rows, c_rows, c_sorted = eb("b_rows", [NS, D]), eb("c_rows", [P, DT, NS, 2]), eb("c_sorted", [P, DT, 2, P])
            la, ai = w["L2_attn_log_A_real"].rearrange("(n o) -> n o", o=1), w["L2_attn_A_imag"].rearrange("(n o) -> n o", o=1)
            load_stage(core, [
                (lar[0:NS], la), (lar[NS:P], la), (aim[0:NS], ai), (aim[NS:P], ai), (ls[:], spread_over(w["L2_attn_log_step"])),
                (b_rows[:], w["L2_attn_B"]), (skip[:], spread_over(w["L2_attn_D"])),
                *[(c_rows[:, t], w["L2_attn_C"][t * P:(t + 1) * P]) for t in range(DT)]])
            dt_, are, r, angle, turns, half = eb("dt", [P, 1]), eb("are", [P, 1]), eb("r", [P, 1]), eb("angle", [P, K]), eb("turns", [P, K]), eb("half", [P, K])
            cosK, sinK = eb("cosK", [P, K]), eb("sinK", [P, K])
            nr, ni, den, cr, ci, t0, ga, gb = (eb(n, [P, 1]) for n in ("nr", "ni", "den", "cr", "ci", "t0", "ga", "gb"))
            tmp = eb("tmp", [P, S])
            with stage(nc, "dve_step", "act_step", "product_ready", "angle_ready", "sines_ready") as (
                    block, dve_step, act_step, product_ready, angle_ready, sines_ready):
                @block.scalar
                def _(act):
                    step = stepper(act, act_step)
                    step(nc.scalar.activation(dt_[:], ls[:], ACT.Exp))
                    step(nc.scalar.activation(are[:], lar[:], ACT.Exp))
                    act.wait_ge(product_ready, 1)
                    nc.scalar.activation(r[:], r[:], ACT.Exp).then_inc(sines_ready, 1)
                    act.wait_ge(angle_ready, 1)
                    nc.scalar.activation(sinK[:], angle[:], ACT.Sin).then_inc(sines_ready, 1)
                    nc.scalar.activation(half[:], half[:], ACT.Sin).then_inc(sines_ready, 1)

                @block.vector
                def _(dve):
                    v = nc.vector
                    step = stepper(dve, dve_step)
                    dve.wait_ge(act_step, 2)
                    step(v.tensor_scalar(are[:], are[:], -1.0, None, ALU.mult))
                    v.tensor_tensor(r[:], are[:], dt_[:], ALU.mult).then_inc(product_ready, 1)
                    step(v.tensor_tensor(angle[:, 0:1], aim[:], dt_[:], ALU.mult))
                    for k in range(1, K):
                        step(v.tensor_scalar(angle[:, k:k + 1], angle[:, k - 1:k], 2.0, None, ALU.mult))
                    step(v.tensor_scalar(turns[:], angle[:], 0.15915494309189535, None, ALU.mult))
                    step(v.tensor_scalar(turns[:], turns[:], ROUND, None, ALU.add))
                    step(v.tensor_scalar(turns[:], turns[:], ROUND, None, ALU.subtract))
                    for part in (TWO_PI_HI, TWO_PI_MID, TWO_PI_LO):
                        step(v.scalar_tensor_tensor(out=angle[:], in0=turns[:], scalar=-part, in1=angle[:], op0=ALU.mult, op1=ALU.add))
                    step(v.tensor_scalar(angle[:], angle[:], -3.1415925, 3.1415925, ALU.max, ALU.min))
                    v.tensor_scalar(half[:], angle[:], 0.5, None, ALU.mult).then_inc(angle_ready, 1)
                    dve.wait_ge(sines_ready, 3)
                    step(v.tensor_tensor(cosK[:], half[:], half[:], ALU.mult))
                    step(v.tensor_scalar(cosK[:], cosK[:], -2.0, 1.0, ALU.mult, ALU.add))
                    step(v.tensor_tensor(nr[:], r[:], cosK[:, 0:1], ALU.mult))
                    step(v.tensor_scalar(nr[:], nr[:], -1.0, None, ALU.add))
                    step(v.tensor_tensor(ni[:], r[:], sinK[:, 0:1], ALU.mult))
                    step(v.tensor_tensor(den[:], are[:], are[:], ALU.mult))
                    step(v.tensor_tensor(t0[:], aim[:], aim[:], ALU.mult))
                    step(v.tensor_tensor(den[:], den[:], t0[:], ALU.add))
                    step(v.reciprocal(den[:], den[:]))
                    step(v.tensor_tensor(cr[:], nr[:], are[:], ALU.mult))
                    step(v.scalar_tensor_tensor(out=cr[:], in0=ni[:], scalar=aim[:, 0:1], in1=cr[:], op0=ALU.mult, op1=ALU.add))
                    step(v.tensor_tensor(cr[:], cr[:], den[:], ALU.mult))
                    step(v.tensor_tensor(t0[:], nr[:], aim[:], ALU.mult))
                    step(v.scalar_tensor_tensor(out=ci[:], in0=ni[:], scalar=are[:, 0:1], in1=t0[:], op0=ALU.mult, op1=ALU.subtract))
                    step(v.tensor_tensor(ci[:], ci[:], den[:], ALU.mult))
                    step(v.memset(cosT[:, 0:1], 1.0))
                    step(v.memset(sinT[:, 0:1], 0.0))
                    for k in range(K):
                        n = 1 << k
                        for to, a, bb, op in ((cosT, cosT, sinT, ALU.subtract), (sinT, sinT, cosT, ALU.add)):
                            step(v.tensor_scalar(tmp[:, 0:n], bb[:, 0:n], sinK[:, k:k + 1], None, ALU.mult))
                            step(v.scalar_tensor_tensor(out=to[:, n:2 * n], in0=a[:, 0:n], scalar=cosK[:, k:k + 1], in1=tmp[:, 0:n],
                                                        op0=ALU.mult, op1=op))
                    step(v.tensor_copy(ga[0:NS], cr[0:NS]))
                    step(v.tensor_copy(ga[NS:P], ci[NS:P]))
                    step(v.tensor_copy(gb[0:NS], ci[0:NS]))
                    step(v.tensor_scalar(gb[NS:P], cr[NS:P], -1.0, None, ALU.mult))
                    step(v.tensor_scalar(tmp[:], sinT[:], gb[:, 0:1], None, ALU.mult))
                    step(v.scalar_tensor_tensor(out=drive[:], in0=cosT[:], scalar=ga[:, 0:1], in1=tmp[:], op0=ALU.mult, op1=ALU.add))
                    step(v.tensor_scalar(decay[:], core.ones[:], r[:, 0:1], None, ALU.mult))
                    for t in range(DT):
                        step(v.tensor_copy(c_sorted[:, t, 0, 0:NS], c_rows[:, t, :, 0]))
                        step(v.tensor_scalar(c_sorted[:, t, 0, NS:P], c_rows[:, t, :, 1], -1.0, None, ALU.mult))
                        step(v.tensor_scalar(c_sorted[:, t, 1, 0:NS], c_rows[:, t, :, 1], -1.0, None, ALU.mult))
                        step(v.tensor_scalar(c_sorted[:, t, 1, NS:P], c_rows[:, t, :, 0], -1.0, None, ALU.mult))

            def turn_b(bank):
                for f in range(DT):
                    for half_ in range(2):
                        last = nc.tensor.transpose(bank[:, f * P + half_ * NS:f * P + half_ * NS + NS], b_rows[:, f * P:(f + 1) * P], core.ident[0:NS, 0:NS])
                return last

            def turn_c(i):
                def multiply(bank):
                    for t in range(DT):
                        last = nc.tensor.transpose(bank[:, t * P:(t + 1) * P], c_sorted[:, t, i], core.ident[:])
                    return last
                return multiply

            product_stage(core, [Job(turn_b, "dve", out_of_bank(core, "dve", inT[:].rearrange("p k n -> p (k n)"))),
                                 Job(turn_c(0), "act", out_of_bank(core, "act", outP[:])), Job(turn_c(1), "dve", out_of_bank(core, "dve", outQ[:]))])
        z, zc, zs = sb("z", [P, S]), sb("zc", [P, S]), sb("zs", [P, S])
        with nc.Fori(0, B) as b:
            take_stage(core, b)
            product_stage(core, turned(core, core.x, core.xT))
            with stage(nc, "drive_product", "dve_step", "state_ready", "out_products") as (
                    block, drive_product, dve_step, state_ready, out_products):
                @block.tensor
                def _(pe):
                    accumulate(nc, core.bank(0), [(inT[:, k], core.xT[:, k]) for k in range(DT)]).then_inc(drive_product, 1)
                    pe.wait_ge(state_ready, 1)
                    for t in range(TT):
                        cut = slice(t * P, (t + 1) * P)
                        accumulate(nc, core.bank(1 + t)[:, 0:D], [(zc[:, cut], outP[:]), (zs[:, cut], outQ[:])]).then_inc(out_products, 1)

                @block.vector
                def _(dve):
                    v = nc.vector
                    step = stepper(dve, dve_step)
                    dve.wait_ge(drive_product, 1)
                    step(v.tensor_tensor(zc[:], core.bank(0), drive[:], ALU.mult))
                    step(v.tensor_tensor_scan(z[:], decay[:], zc[:], 0.0, ALU.mult, ALU.add))
                    step(v.tensor_tensor(zc[:], z[:], cosT[:], ALU.mult))
                    v.tensor_tensor(zs[:], z[:], sinT[:], ALU.mult).then_inc(state_ready, 1)
                    for t in range(TT):
                        step(v.tensor_tensor(core.delta[:, t], core.x[:, t], skip[:], ALU.mult))
                    for t in range(TT):
                        dve.wait_ge(out_products, t + 1)
                        step(v.tensor_tensor(core.delta[:, t], core.bank(1 + t)[:, 0:D], core.delta[:, t], ALU.add))
            residual_norm(core, b)


def turn_square(core, source, to, rows_tiles, cols_tiles):
    nc = core.nc
    jobs = []
    for c in range(cols_tiles):
        def multiply(bank, c=c):
            for r in range(rows_tiles):
                last = nc.tensor.transpose(bank[:, r * P:(r + 1) * P], source[:, r, c * P:(c + 1) * P], core.ident[:])
            return last
        jobs.append(Job(multiply, "dve", out_of_bank(core, "dve", to[:, c, 0:rows_tiles * P])))
    return jobs


def l2_xattn(core, w, ctx_in):
    nc = core.nc
    with ExitStack() as ctx:
        sb = lambda name, shape: ctx.enter_context(nc.sbuf_tensor(core.named(name), shape, F32))
        wr, wT, bias = sb("wr", [P, DT, 2 * D]), sb("wT", [P, 2 * DT, D]), sb("bias", [1, D])
        load_stage(core, [(wr[:], matrix(w["L2_xattn_W"])), (bias[:], rowed(w["L2_xattn_b"]))])
        product_stage(core, turn_square(core, wr, wT, DT, 2 * DT))
        rows, mean, pooled = sb("rows", [P, MT, D]), sb("mean", [P, DT]), sb("pooled", [1, D])
        with nc.Fori(0, B) as b:
            take_stage(core, b)
            context_load(core, ctx_in, b, rows)

            def sums(bank):
                for f in range(DT):
                    last = accumulate(nc, bank[:, f:f + 1], [(rows[0:kt_rows(M, t), t, f * P:(f + 1) * P], core.ones[0:kt_rows(M, t), 0:1]) for t in range(MT)])
                return last

            product_stage(core, [*turned(core, core.x, core.xT), Job(sums, "dve", lambda bank: nc.vector.tensor_scalar(
                mean[:], bank[:, 0:DT], 1.0 / M, None, ALU.mult))])
            product_stage(core, [Job(lambda bank: accumulate(nc, bank[0:1, 0:D], [(mean[:, k:k + 1], wT[:, DT + k]) for k in range(DT)]), "dve",
                                     lambda bank: nc.vector.tensor_tensor(pooled[:], bank[0:1, 0:D], bias[:], ALU.add))])
            product_stage(core, rows_out(core, core.xT, wT[:, 0:DT], S, D, into(core, core.delta), bias_row=pooled[:]))
            residual_norm(core, b)


def l2_ffn(core, w):
    nc = core.nc
    E, _, R = w["L2_ffn_down_W"].shape
    with ExitStack() as ctx:
        sb = lambda name, shape: ctx.enter_context(nc.sbuf_tensor(core.named(name), shape, F32))
        base, baseT, base_b = sb("base", [P, DT, D]), sb("baseT", [P, DT, D]), sb("base_b", [1, D])
        mu, iv, muiv, mu2iv = (sb(n, [P, DT, E]) for n in ("mu", "iv", "muiv", "mu2iv"))
        down, up, conv = sb("down", [P, E, DT, R]), sb("up", [R, E, D]), sb("conv", [P, E, DT, D])
        down_b, up_b, conv_b = sb("down_b", [E, R]), sb("up_b", [E, D]), sb("conv_b", [E, D])
        by_feature = lambda v: v.rearrange("e (k p) -> p k e", p=P)
        with nc.allow_non_contiguous_dma("small tables of the experts' statistics"):
            load_stage(core, [
                (base[:], matrix(w["L2_ffn_base_W"])), (base_b[:], rowed(w["L2_ffn_base_b"])),
                *[(mu[:, k], by_feature(w["L2_ffn_disc_mu"])[:, k]) for k in range(DT)],
                *[(iv[:, k], by_feature(w["L2_ffn_disc_sigma"])[:, k]) for k in range(DT)],
                *[(down[:, e], matrix(w["L2_ffn_down_W"][e])) for e in range(E)], (up[:], w["L2_ffn_up_W"].rearrange("e r d -> r e d")),
                *[(conv[:, e], matrix(w["L2_ffn_conv_W"][e])) for e in range(E)],
                (down_b[:], w["L2_ffn_down_b"]), (up_b[:], w["L2_ffn_up_b"]), (conv_b[:], w["L2_ffn_conv_b"])])
        with stage(nc, "dve_step") as (block, dve_step):
            @block.vector
            def _(dve):
                v = nc.vector
                step = stepper(dve, dve_step)
                step(v.tensor_tensor(iv[:], iv[:], iv[:], ALU.mult))
                step(v.reciprocal(iv[:], iv[:]))
                step(v.tensor_tensor(muiv[:], mu[:], iv[:], ALU.mult))
                step(v.tensor_tensor(mu2iv[:], mu[:], muiv[:], ALU.mult))
                step(v.tensor_scalar(muiv[:], muiv[:], -2.0, None, ALU.mult))
        product_stage(core, turn_square(core, base, baseT, DT, DT))
        m1, m2, square = sb("m1", [P, DT]), sb("m2", [P, DT]), sb("square", [P, DT, S])
        loss, least, ties, counted, pick = sb("loss", [1, 1, E]), sb("least", [1, 1]), sb("ties", [1, 1, E]), sb("counted", [1, 1, E]), sb("pick", [1, 1, E])
        everywhere, picked = sb("everywhere", [P, E]), sb("picked", [E, 1])
        wd, wu, wc, wcT = sb("wd", [P, DT, R]), sb("wu", [R, 1, D]), sb("wc", [P, DT, D]), sb("wcT", [P, DT, D])
        bd, bu, bc = sb("bd", [R, 1]), sb("bu", [P, DT]), sb("bc", [1, D])
        hT, aT = sb("hT", [R, 1, S]), sb("aT", [P, DT, S])
        with nc.Fori(0, B) as b:
            take_stage(core, b)
            product_stage(core, turned(core, core.x, core.xT))
            with stage(nc, "dve_step", "act_step") as (block, dve_step, act_step):
                @block.vector
                def _(dve):
                    step = stepper(dve, dve_step)
                    step(nc.vector.reduce_sum(m1[:], core.xT[:], AX.X))
                    step(nc.vector.tensor_scalar(m1[:], m1[:], 1.0 / S, None, ALU.mult))
                    dve.wait_ge(act_step, DT)
                    step(nc.vector.tensor_scalar(m2[:], m2[:], 1.0 / S, None, ALU.mult))

                @block.scalar
                def _(act):
                    step = stepper(act, act_step)
                    for f in range(DT):
                        step(nc.scalar.activation(square[:, f], core.xT[:, f], ACT.Square, accum_out=m2[:, f:f + 1]))

            def losses(bank):
                terms = []
                for k in range(DT):
                    terms += [(m2[:, k:k + 1], iv[:, k]), (m1[:, k:k + 1], muiv[:, k]), (core.ones[:, 0:1], mu2iv[:, k])]
                return accumulate(nc, bank[0:1, 0:E], terms)

            product_stage(core, [Job(losses, "dve", lambda bank: nc.vector.tensor_scalar(loss[:, 0], bank[0:1, 0:E], -1.0 / D, None, ALU.mult))])
            with stage(nc, "dve_step") as (block, dve_step):
                @block.vector
                def _(dve):
                    step = stepper(dve, dve_step)
                    step(nc.vector.reduce_max(least[:], loss[:], AX.X))
                    first_of_equal(nc, step, pick[:], loss[:], least[:], ties[:], counted[:], core.ones[0:1, 0:E])
            product_stage(core, [
                Job(lambda bank: nc.tensor.matmul(bank[:, 0:E], core.ones[0:1, 0:P], pick[:, 0], start=True, stop=True), "dve",
                    out_of_bank(core, "dve", everywhere[:])),
                Job(lambda bank: nc.tensor.matmul(bank[0:E, 0:1], pick[:, 0], core.ones[0:1, 0:1], start=True, stop=True), "dve",
                    out_of_bank(core, "dve", picked[:]))])
            with stage(nc, "dve_step") as (block, dve_step):
                @block.vector
                def _(dve):
                    step = stepper(dve, dve_step)
                    for e in range(E):
                        for to, of, p in ((wd[:], down[:, e], P), (wu[:, 0], up[:, e], R), (wc[:], conv[:, e], P)):
                            if e == 0:
                                step(nc.vector.tensor_scalar(to, of, everywhere[0:p, 0:1], None, ALU.mult))
                            else:
                                step(nc.vector.scalar_tensor_tensor(out=to, in0=of, scalar=everywhere[0:p, e:e + 1], in1=to, op0=ALU.mult, op1=ALU.add))

            def column(bias, cut, rows):
                return lambda bank: nc.tensor.matmul(bank[0:rows, 0:1], bias[:, cut], picked[:], start=True, stop=True)

            product_stage(core, [
                *turn_square(core, wc, wcT, DT, DT),
                Job(column(down_b, slice(0, R), R), "dve", out_of_bank(core, "dve", bd[:])),
                *[Job(column(up_b, slice(f * P, (f + 1) * P), P), "dve", out_of_bank(core, "dve", bu[:, f:f + 1])) for f in range(DT)],
                Job(lambda bank: nc.tensor.matmul(bank[0:1, 0:D], picked[:], conv_b[:], start=True, stop=True), "dve", out_of_bank(core, "dve", bc[:]))])
            product_stage(core, columns_out(core, wd, core.xT, hT, S, m=R, bias=bd, func=ACT.Relu, engines=("act",)))
            product_stage(core, columns_out(core, wu, hT, aT, S, bias=bu))

            def both(t):
                cut = slice(t * P, (t + 1) * P)
                terms = [(core.xT[:, k, cut], baseT[:, k]) for k in range(DT)] + [(aT[:, k, cut], wcT[:, k]) for k in range(DT)]
                terms += [(core.ones[0:1, 0:P], base_b[:]), (core.ones[0:1, 0:P], bc[:])]
                return lambda bank: accumulate(nc, bank[:, 0:D], terms)

            product_stage(core, [Job(both(t), *into(core, core.delta)(t)) for t in range(TT)])
            residual_norm(core, b)


def l3_attn(core, w):
    nc = core.nc
    L, CH, HD = 64, S // 64, 16
    with ExitStack() as ctx:
        sb = lambda name, shape: ctx.enter_context(nc.sbuf_tensor(core.named(name), shape, F32))
        wq, wk, wv = sb("wq", [P, DT, 512]), sb("wk", [P, DT, 512]), sb("wv", [P, DT, D])
        bq, bk, bv = sb("bq", [P, 4]), sb("bk", [P, 4]), sb("bv", [1, D])
        rq, rk, rv = sb("rq", [P, DT, P]), sb("rk", [P, DT, P]), sb("rv", [P, DT, L])
        rbq, rbk, rbv = sb("rbq", [P, 1]), sb("rbk", [P, 1]), sb("rbv", [1, L])
        rout, rout_b = sb("rout", [L, 1, D]), sb("rout_b", [1, D])
        wo, bo = sb("wo", [P, DT, D]), sb("bo", [1, D])
        gl, gr = sb("gl", [P, HD]), sb("gr", [P, HD])
        before, after, chunks, some_key, some_chunk = sb("before", [P, P]), sb("after", [P, P]), sb("chunks", [P, TT, L]), sb("some_key", [P, TT]), sb("some_chunk", [P, TT])
        qkv, qkv_b = w["L3_attn_qkv_w"], w["L3_attn_qkv_b"]
        load_stage(core, [
            *slotted_weight(wq, qkv[:, 0:D]), *slotted_weight(wk, qkv[:, D:2 * D]), (wv[:], matrix(qkv[:, 2 * D:3 * D])),
            *slotted_bias(bq, qkv_b[0:D]), *slotted_bias(bk, qkv_b[D:2 * D]), (bv[:], rowed(qkv_b[2 * D:3 * D])),
            *slotted_weight(rq, w["L3_attn_rq_w"]), *slotted_weight(rk, w["L3_attn_rkv_w"][:, 0:L]), (rv[:], matrix(w["L3_attn_rkv_w"][:, L:2 * L])),
            *slotted_bias(rbq, w["L3_attn_rq_b"]), *slotted_bias(rbk, w["L3_attn_rkv_b"][0:L]), (rbv[:], rowed(w["L3_attn_rkv_b"][L:2 * L])),
            (rout[:], matrix(w["L3_attn_rout_w"], L)), (rout_b[:], rowed(w["L3_attn_rout_b"])),
            (wo[:], matrix(w["L3_attn_out_w"])), (bo[:], rowed(w["L3_attn_out_b"])),
            (gl[:], spread_over(w["L3_attn_gl_w"].rearrange("a b -> (a b)"))), (gr[:], spread_over(w["L3_attn_gr_w"].rearrange("a b -> (a b)"))),
        ], zeroed=[wq[:], wk[:], bq[:], bk[:], rq[:], rk[:], rbq[:], rbk[:], before[:], after[:], chunks[:]])
        with stage(nc, "filled") as (block, filled):
            @block.gpsimd
            def _(pool):
                pool.memset(some_key[:], 1.0).then_inc(filled, 1)
                pool.memset(some_chunk[:], 1.0).then_inc(filled, 1)
                pool.wait_ge(filled, 2)
                pool.affine_select(out=before[:], in_=before[:], compare_op=ALU.is_gt, fill=MASKED, base=0, pattern=[[-1, P]], channel_multiplier=1).then_inc(filled, 1)
                pool.affine_select(out=after[:], in_=after[:], compare_op=ALU.is_ge, fill=MASKED, base=0, pattern=[[1, P]], channel_multiplier=-1).then_inc(filled, 1)
                for q in range(TT):
                    pool.affine_select(out=chunks[:, q], in_=chunks[:, q], compare_op=ALU.is_ge, fill=MASKED, base=q * P - CH, pattern=[[-CH, L]], channel_multiplier=1).then_inc(filled, 1)
                pool.affine_select(out=some_key[:, 0:1], in_=some_key[:, 0:1], compare_op=ALU.is_gt, fill=0.0, base=0, pattern=[[0, 1]], channel_multiplier=1).then_inc(filled, 1)
                pool.affine_select(out=some_chunk[:, 0:1], in_=some_chunk[:, 0:1], compare_op=ALU.is_ge, fill=0.0, base=-CH, pattern=[[0, 1]], channel_multiplier=1).then_inc(filled, 1)
                pool.wait_ge(filled, 6 + TT)

        def local_blocks(q):
            return ([(q - 1, after)] if q else []) + [(q, before)]

        qT, kT = sb("qT", [P, 4, S]), sb("kT", [P, 4, S])
        v, o, oT = sb("v", [P, TT, D]), sb("o", [P, TT, D]), sb("oT", [P, DT, S])
        pooledT, rqT, rkT, rvr = sb("pooledT", [P, DT, L]), sb("rqT", [P, 1, S]), sb("rkT", [P, 1, L]), sb("rvr", [L, 1, L])
        lat, latT, remote = sb("lat", [P, TT, L]), sb("latT", [L, 1, S]), sb("remote", [P, TT, D])
        gated, gate, gate2 = sb("gated", [P, TT * 16, HD]), sb("gate", [P, TT * 16]), sb("gate2", [P, TT * 16])
        with nc.Fori(0, B) as b:
            take_stage(core, b)
            product_stage(core, turned(core, core.x, core.xT))
            with stage(nc, "dve_step") as (block, dve_step):
                @block.vector
                def _(dve):
                    step = stepper(dve, dve_step)
                    for k in range(DT):
                        step(nc.vector.reduce_sum(pooledT[:, k], core.xT[:, k].rearrange("p (l c) -> p l c", c=CH), AX.X))
                    step(nc.vector.tensor_scalar(pooledT[:], pooledT[:], 1.0 / CH, None, ALU.mult))
            product_stage(core, [
                *columns_out(core, wq, core.xT, qT, S, bias=bq), *columns_out(core, wk, core.xT, kT, S, bias=bk),
                *rows_out(core, core.xT, wv, S, D, into(core, v), bias_row=bv[:]),
                *columns_out(core, rq, core.xT, rqT, S, bias=rbq), *columns_out(core, rk, pooledT, rkT, L, bias=rbk),
                *rows_out(core, pooledT, rv, L, L, into(core, rvr), bias_row=rbv[:])])
            attention_groups(core, Heads(qT, kT, v, o, 4, 4, 16, S, 0.25, local_blocks, valid=some_key))
            attention_groups(core, Heads(rqT, rkT, rvr, lat, 1, 4, 16, L, 0.25, lambda q: [(0, chunks[:, q])], valid=some_chunk))

            def turn_lat(bank):
                for t in range(TT):
                    last = nc.tensor.transpose(bank[0:L, t * P:(t + 1) * P], lat[:, t], core.ident[:])
                return last

            product_stage(core, [Job(turn_lat, "dve", out_of_bank(core, "dve", latT[:, 0]))])
            product_stage(core, rows_out(core, latT, rout, S, D, into(core, remote), bias_row=rout_b[:]))
            with stage(nc, "dve_step", "logit_ready", "gate_ready") as (block, dve_step, logit_ready, gate_ready):
                by_head = lambda t: t[:].rearrange("p t (h s) -> p (t h) s", s=HD)
                wide = lambda t: t[:].unsqueeze(1).to_broadcast([P, TT * 16, HD])

                @block.vector
                def _(dve):
                    v_ = nc.vector
                    step = stepper(dve, dve_step)
                    step(v_.tensor_tensor(gated[:], by_head(o), wide(gl), ALU.mult))
                    step(v_.reduce_sum(gate[:], gated[:], AX.X))
                    step(v_.tensor_tensor(gated[:], by_head(remote), wide(gr), ALU.mult))
                    step(v_.reduce_sum(gate2[:], gated[:], AX.X))
                    v_.tensor_tensor(gate[:], gate[:], gate2[:], ALU.add).then_inc(logit_ready, 1)
                    step(v_.tensor_tensor(gated[:], by_head(o), by_head(remote), ALU.subtract))
                    dve.wait_ge(gate_ready, 1)
                    step(v_.tensor_tensor(gated[:], gated[:], gate[:].unsqueeze(2).to_broadcast([P, TT * 16, HD]), ALU.mult))
                    step(v_.tensor_tensor(by_head(o), gated[:], by_head(remote), ALU.add))

                @block.scalar
                def _(act):
                    act.wait_ge(logit_ready, 1)
                    nc.scalar.activation(gate[:], gate[:], ACT.Sigmoid).then_inc(gate_ready, 1)
            product_stage(core, turned(core, o, oT))
            product_stage(core, rows_out(core, oT, wo, S, D, into(core, core.delta), bias_row=bo[:]))
            residual_norm(core, b)


def l3_xattn(core, w, ctx_in):
    nc = core.nc
    with ExitStack() as ctx:
        sb = lambda name, shape: ctx.enter_context(nc.sbuf_tensor(core.named(name), shape, F32))
        wq, wk, wv = sb("wq", [P, DT, 512]), sb("wk", [P, DT, 512]), sb("wv", [P, DT, D])
        bq, bk, bv = sb("bq", [P, 4]), sb("bk", [P, 4]), sb("bv", [1, D])
        wo, bo = sb("wo", [P, DT, D]), sb("bo", [1, D])
        load_stage(core, [
            *slotted_weight(wq, w["L3_xattn_Wq"]), *slotted_weight(wk, w["L3_xattn_Wk"]), (wv[:], matrix(w["L3_xattn_Wv"])),
            *slotted_bias(bq, w["L3_xattn_bq"]), *slotted_bias(bk, w["L3_xattn_bk"]), (bv[:], rowed(w["L3_xattn_bv"])),
            (wo[:], matrix(w["L3_xattn_Wo"])), (bo[:], rowed(w["L3_xattn_bo"])),
        ], zeroed=[wq[:], wk[:], bq[:], bk[:]])
        qT, kT = sb("qT", [P, 4, S]), sb("kT", [P, 4, M])
        v, o, oT = sb("v", [P, MT, D]), sb("o", [P, TT, D]), sb("oT", [P, DT, S])
        with nc.Fori(0, B) as b:
            take_stage(core, b)
            product_stage(core, turned(core, core.x, core.xT))
            with ExitStack() as early:
                ctxT = early.enter_context(nc.sbuf_tensor(core.named("ctxT"), [P, DT, M], F32))
                context_columns(core, ctx_in, b, ctxT)
                product_stage(core, [
                    *columns_out(core, wq, core.xT, qT, S, bias=bq), *columns_out(core, wk, ctxT, kT, M, bias=bk),
                    *rows_out(core, ctxT, wv, M, D, into(core, v), bias_row=bv[:])])
            attention_groups(core, Heads(qT, kT, v, o, 4, 4, 16, M, 0.25, all_blocks(M)))
            product_stage(core, turned(core, o, oT))
            product_stage(core, rows_out(core, oT, wo, S, D, into(core, core.delta), bias_row=bo[:]))
            residual_norm(core, b)


def l3_ffn(core, w):
    nc = core.nc
    FF = w["L3_ffn_w1"].shape[1]
    with ExitStack() as ctx:
        sb = lambda name, shape: ctx.enter_context(nc.sbuf_tensor(core.named(name), shape, F32))
        w1, b1 = sb("w1", [P, DT, FF]), sb("b1", [P, FF // P])
        w2, b2 = sb("w2", [P, FF // P, D]), sb("b2", [1, D])
        load_stage(core, [(w1[:], matrix(w["L3_ffn_w1"])), (b1[:], columned(w["L3_ffn_b1"])),
                          (w2[:], matrix(w["L3_ffn_w2"])), (b2[:], rowed(w["L3_ffn_b2"]))])
        hT = sb("hT", [P, FF // P, S])
        with nc.Fori(0, B) as b:
            take_stage(core, b)
            product_stage(core, turned(core, core.x, core.xT))
            product_stage(core, columns_out(core, w1, core.xT, hT, S, bias=b1, func=ACT.Gelu, engines=("act",)))
            product_stage(core, rows_out(core, hT, w2, S, D, into(core, core.delta), bias_row=b2[:]))
            residual_norm(core, b)


def decoder(nc, w, out, layers=range(12)):
    with ExitStack() as ctx:
        core = Core(nc, ctx)
        constants_stage(core, w["x"])
        context = w["ctx_1024"]
        sublayers = [lambda: l0_attn(core, w), lambda: l0_xattn(core, w, context), lambda: l0_ffn(core, w),
                     lambda: l1_attn(core, w), lambda: l1_xattn(core, w, context), lambda: l1_ffn(core, w),
                     lambda: l2_attn(core, w), lambda: l2_xattn(core, w, context), lambda: l2_ffn(core, w),
                     lambda: l3_attn(core, w), lambda: l3_xattn(core, w, context), lambda: l3_ffn(core, w)]
        for n in layers:
            core.sublayer = f"l{n // 3}_{n % 3}"
            sublayers[n]()
        with stage(nc, "stored") as (block, stored):
            @block.sync
            def _(sp):
                for b in range(B):
                    sp.dma_start(out[b].rearrange("(t p) d -> p t d", p=P), core.x_all[:, b]).then_inc(stored, 16)
                sp.wait_ge(stored, 16 * B)


def kernel(**inputs):
    import numpy as _np
    import concourse.bacc as _bacc
    from concourse import mybir as _mybir
    from concourse.bass_utils import run_bass_kernel_spmd as _run

    nc = _bacc.Bacc("TRN2", target_bir_lowering=False, num_devices=1)
    arrays, args = {}, {}
    for name, value in inputs.items():
        a = _np.ascontiguousarray(value)
        arrays[name + "_dram"] = a
        args[name] = nc.dram_tensor(name + "_dram", a.shape, _mybir.dt.from_np(a.dtype), kind="ExternalInput").ap()
    out = nc.dram_tensor("out_dram", (B, S, D), F32, kind="ExternalOutput").ap()
    decoder(nc, args, out)
    return _run(nc, [arrays], core_ids=[0]).results[0]["out_dram"]
```

```python
from contextlib import ExitStack, contextmanager
from dataclasses import dataclass, replace

import concourse.bass as bass
from concourse import mybir

F32 = mybir.dt.float32
BF16 = mybir.dt.bfloat16
I32 = mybir.dt.int32
ALU = mybir.AluOpType
ACT = mybir.ActivationFunctionType
AX = mybir.AxisListType

P = 128
B, S, D = 4, 512, 256
M = 1601
TT = S // P
DT = D // P
MT = (M + P - 1) // P
BANK = 512
BANKS = 8
EPS = 1e-5
MASKED = -1e30
TAKEN = -3e38
ROUND = 12582912.0


def kt_rows(n, t):
    return min(P, n - t * P)


used = []


@contextmanager
def stage(nc, *signals):
    with ExitStack() as held:
        last, used[:] = used[:], []
        turn = 1 - last[0][0] if last else 0
        sems = [held.enter_context(nc.semaphore(f"{s}_{turn}")) for s in signals]
        with nc.Block() as block:
            @block.sync
            def _(sp):
                for _turn, old, _held in last:
                    for s in old:
                        sp.sem_clear(s)
            yield (block, *sems)
        for _turn, _old, old_held in last:
            old_held.close()
        used.append((turn, sems, held.pop_all()))


def clear_used(nc):
    if used:
        with stage(nc):
            pass
        used.clear()


@contextmanager
def loop(nc, count):
    clear_used(nc)
    with nc.Fori(0, count) as i:
        yield i
        clear_used(nc)


@contextmanager
def branch(nc, condition):
    clear_used(nc)
    with nc.If(condition):
        yield
        clear_used(nc)


def stepper(engine, sem):
    done = [0]

    def step(instruction):
        done[0] += 1
        instruction.then_inc(sem, 1)
        engine.wait_ge(sem, done[0])

    return step


@dataclass
class Job:
    multiply: object
    engine: str
    evacuate: object


class Core:

    def __init__(self, nc, ctx):
        self.nc = nc
        self.sublayer, self.tensors = "", 0
        sb = lambda name, shape: ctx.enter_context(nc.sbuf_tensor(name, shape, F32))
        self.psum = ctx.enter_context(nc.psum_tensor("psum", [P, BANKS * BANK], F32))
        self.x_all = sb("x_all", [P, B, TT, D])
        self.x = sb("x", [P, TT, D])
        self.xT = sb("xT", [P, DT, S])
        self.delta = sb("delta", [P, TT, D])
        self.ident = sb("ident", [P, P])
        self.ones = sb("ones", [P, BANK])
        sb16 = lambda name, shape: ctx.enter_context(nc.sbuf_tensor(name, shape, BF16))
        self.ident16 = sb16("ident16", [P, P])
        self.causal16 = sb16("causal16", [P, P])
        self.causalT16 = sb16("causalT16", [P, P])
        self.stats = sb("stats", [P, TT, 6])
        self.moments = sb("moments", [P, TT, 2])
        self.spread = sb("spread", [P, TT])
        self.rstd = sb("rstd", [P, TT])

    def named(self, name):
        self.tensors += 1
        return f"{self.sublayer}_{name}_{self.tensors}"

    def bank(self, j):
        return self.psum[:, (j % BANKS) * BANK:(j % BANKS + 1) * BANK]


def triangle(pool, mask, compare, sign, base=0):
    return pool.affine_select(out=mask, in_=mask, compare_op=compare, fill=MASKED, base=base,
                              pattern=[[-sign, mask.shape[1]]], channel_multiplier=sign)


def constants_stage(core, x):
    nc = core.nc
    with ExitStack() as held:
        causal = held.enter_context(nc.sbuf_tensor(core.named("causal"), [P, 2, P], F32))
        with stage(nc, "filled", "x_loaded") as (block, filled, x_loaded):
            @block.gpsimd
            def _(pool):
                pool.memset(core.ident[:], 0.0).then_inc(filled, 1)
                pool.memset(causal[:], 0.0).then_inc(filled, 1)
                pool.memset(core.ones[:], 1.0).then_inc(filled, 1)
                pool.wait_ge(filled, 3)
                pool.affine_select(out=core.ident[:], in_=core.ident[:], compare_op=ALU.not_equal, fill=1.0,
                                   base=0, pattern=[[-1, P]], channel_multiplier=1).then_inc(filled, 1)
                triangle(pool, causal[:, 0], ALU.is_ge, 1).then_inc(filled, 1)
                triangle(pool, causal[:, 1], ALU.is_ge, -1).then_inc(filled, 1)
                pool.wait_ge(filled, 6)
                pool.tensor_copy(core.ident16[:], core.ident[:]).then_inc(filled, 1)
                pool.tensor_copy(core.causal16[:], causal[:, 0]).then_inc(filled, 1)
                pool.tensor_copy(core.causalT16[:], causal[:, 1]).then_inc(filled, 1)
                pool.wait_ge(filled, 9)

            @block.sync
            def _(sp):
                for b in range(B):
                    sp.dma_start(core.x_all[:, b], x[b].rearrange("(t p) d -> p t d", p=P)).then_inc(x_loaded, 16)
                sp.wait_ge(x_loaded, 16 * B)


def load_stage(core, loads, zeroed=(), ones=()):
    nc = core.nc
    with stage(nc, "padding_zeroed", "loaded_by_sp", "loaded_by_act") as (block, padding_zeroed, by_sp, by_act):
        @block.gpsimd
        def _(pool):
            for z in zeroed:
                pool.memset(z, 0.0).then_inc(padding_zeroed, 1)
            if ones:
                pool.wait_ge(padding_zeroed, len(zeroed))
            for o in ones:
                pool.memset(o, 1.0).then_inc(padding_zeroed, 1)

        @block.sync
        def _(sp):
            if zeroed or ones:
                sp.wait_ge(padding_zeroed, len(zeroed) + len(ones))
            with nc.allow_non_contiguous_dma("biases and small tables, a value per partition"):
                for to, of in loads[0::2]:
                    sp.dma_start(to, of).then_inc(by_sp, 16)
            sp.wait_ge(by_sp, 16 * len(loads[0::2]))

        @block.scalar
        def _(act):
            if zeroed or ones:
                act.wait_ge(padding_zeroed, len(zeroed) + len(ones))
            with nc.allow_non_contiguous_dma("biases and small tables, a value per partition"):
                for to, of in loads[1::2]:
                    act.dma_start(to, of).then_inc(by_act, 16)
            if loads[1::2]:
                act.wait_ge(by_act, 16 * len(loads[1::2]))


def take_stage(core, b):
    nc = core.nc
    with stage(nc, "taken") as (block, taken):
        @block.vector
        def _(dve):
            nc.vector.tensor_copy(core.x[:], core.x_all[:, bass.ds(b, 1)].rearrange("p o t d -> p (o t) d")).then_inc(taken, 1)
            dve.wait_ge(taken, 1)


def product_stage(core, jobs):
    nc = core.nc

    def emptied_before(j, engine):
        return sum(job.engine == engine for job in jobs[:j])

    with stage(nc, "products_ready", "emptied_by_act", "emptied_by_dve", "dve_step") as (
            block, products_ready, emptied_by_act, emptied_by_dve, dve_step):
        @block.tensor
        def _(pe):
            for j, job in enumerate(jobs):
                if j >= BANKS:
                    last = jobs[j - BANKS].engine
                    pe.wait_ge(emptied_by_act if last == "act" else emptied_by_dve,
                               emptied_before(j - BANKS + 1, last))
                job.multiply(core.bank(j)).then_inc(products_ready, 1)

        @block.scalar
        def _(act):
            for j, job in enumerate(jobs):
                if job.engine == "act":
                    act.wait_ge(products_ready, j + 1)
                    job.evacuate(core.bank(j)).then_inc(emptied_by_act, 1)

        @block.vector
        def _(dve):
            step = stepper(dve, dve_step)
            for j, job in enumerate(jobs):
                if job.engine == "dve":
                    dve.wait_ge(products_ready, j + 1)
                    step(job.evacuate(core.bank(j)))
                    nc.vector.sem_inc(emptied_by_dve, 1)


def norm_stage(core, source, out, add=None, total=None):
    nc = core.nc
    with stage(nc, "dve_step", "variance_ready", "root_ready") as (block, dve_step, variance_ready, root_ready):
        @block.vector
        def _(dve):
            step = stepper(dve, dve_step)
            y = source
            if add is not None:
                y = total
                step(nc.vector.tensor_tensor(total, source, add, ALU.add))
            for t in range(TT):
                step(nc.vector.bn_stats(core.stats[:, t], y[:, t]))
            for t in range(TT):
                step(nc.vector.bn_aggr(core.moments[:, t], core.stats[:, t]))
            nc.vector.tensor_scalar(core.spread[:], core.moments[:, :, 1], EPS, None, ALU.add).then_inc(variance_ready, 1)
            dve.wait_ge(root_ready, 1)
            step(nc.vector.reciprocal(core.rstd[:], core.rstd[:]))
            for t in range(TT):
                step(nc.vector.tensor_scalar(out(t), y[:, t], core.moments[:, t, 0:1], core.rstd[:, t:t + 1],
                                             ALU.subtract, ALU.mult))

        @block.scalar
        def _(act):
            act.wait_ge(variance_ready, 1)
            nc.scalar.activation(core.rstd[:], core.spread[:], ACT.Sqrt).then_inc(root_ready, 1)


def residual_norm(core, b, delta=None):
    delta = core.delta if delta is None else delta
    norm_stage(core, core.x[:], lambda t: core.x_all[:, bass.ds(b, 1), t].rearrange("p o d -> p (o d)"), add=delta[:], total=delta[:])



def out_of_bank(core, engine, to, scale=None, bias=None, func=None):
    nc = core.nc
    rows, cols = to.shape[0], to.shape[-1]

    def evacuate(bank):
        held = bank[0:rows, 0:cols]
        if engine == "act":
            if bias is None and scale is None:
                return nc.scalar.activation(to, held, func or ACT.Copy)
            return nc.scalar.activation(to, held, func or ACT.Identity, bias=0.0 if bias is None else bias,
                                        scale=1.0 if scale is None else scale)
        if scale is not None:
            return nc.vector.tensor_scalar(to, held, scale, bias, ALU.mult, ALU.add)
        if bias is not None:
            return nc.vector.tensor_scalar(to, held, bias, None, ALU.add)
        return nc.vector.tensor_copy(to, held)

    return evacuate


def accumulate(nc, out, terms):
    for i, (lhsT, rhs) in enumerate(terms):
        last = nc.tensor.matmul(out, lhsT, rhs, start=(i == 0), stop=(i == len(terms) - 1))
    return last


def turned(core, source, to, rows=S, scale=None, bias=None, features=DT):
    nc = core.nc
    jobs = []
    for f in range(features):
        for c in range(0, rows, BANK):
            width = min(BANK, rows - c)

            def multiply(bank, f=f, c=c, width=width):
                for o in range(0, width, P):
                    n = min(P, width - o)
                    last = nc.tensor.transpose(bank[:, o:o + n], source[0:n, (c + o) // P, f * P:(f + 1) * P],
                                               core.ident[0:n, 0:n])
                return last

            engine = ("act", "dve")[len(jobs) % 2]
            jobs.append(Job(multiply, engine, out_of_bank(
                core, engine, to[:, f, c:c + width],
                None if scale is None else scale[:, f:f + 1], None if bias is None else bias[:, f:f + 1])))
    return jobs


def turned_back(core, source, evacuations, features=DT):
    nc = core.nc
    jobs = []
    for t in range(TT):
        def multiply(bank, t=t):
            for f in range(features):
                last = nc.tensor.transpose(bank[:, f * P:(f + 1) * P], source[:, f, t * P:(t + 1) * P], core.ident[:])
            return last

        jobs.append(Job(multiply, *evacuations(t)))
    return jobs


def columns_out(core, weight, xT, to, n, m=P, bias=None, func=None, engines=("act", "dve")):
    nc = core.nc
    kts = weight.shape[1]
    jobs = []
    for o in range(weight.shape[2] // m):
        for c in range(0, n, BANK):
            w = min(BANK, n - c)
            engine = engines[len(jobs) % len(engines)]

            def multiply(bank, o=o, c=c, w=w):
                return accumulate(nc, bank[0:m, 0:w],
                                  [(weight[:, k, o * m:(o + 1) * m], xT[:, k, c:c + w]) for k in range(kts)])

            jobs.append(Job(multiply, engine, out_of_bank(core, engine, to[0:m, o, c:c + w],
                                                          bias=None if bias is None else bias[0:m, o:o + 1], func=func)))
    return jobs


def rows_out(core, xT, weight, n, cols, evacuation, bias_row=None):
    nc = core.nc
    jobs = []
    for t in range((n + P - 1) // P):
        r = kt_rows(n, t)

        def multiply(bank, t=t, r=r):
            terms = [(xT[:, k, t * P:t * P + r], weight[:, k, 0:cols]) for k in range(weight.shape[1])]
            if bias_row is not None:
                terms.append((core.ones[0:1, 0:r], bias_row))
            return accumulate(nc, bank[0:r, 0:cols], terms)

        jobs.append(Job(multiply, *evacuation(t, r)))
    return jobs


def into(core, to):
    def evacuation(t, r=P):
        engine = ("act", "dve")[t % 2]
        return engine, out_of_bank(core, engine, to[0:r, t])
    return evacuation


def added_to(core, other, to):
    def evacuation(t, r=P):
        return "dve", lambda bank: core.nc.vector.tensor_tensor(to[0:r, t], bank[0:r, 0:to.shape[2]], other[0:r, t], ALU.add)
    return evacuation


def columned(v, p=P):
    return v.rearrange("(t p) -> p t", p=p)


def rowed(v):
    return v.rearrange("(a n) -> a n", a=1)


def spread_over(v):
    return v.partition_broadcast(P)



HIGH, MIDDLE, LOW = range(3)
STACKS = {16: [[(HIGH, HIGH), (HIGH, MIDDLE), (HIGH, LOW), (MIDDLE, HIGH), (MIDDLE, MIDDLE), (LOW, HIGH)]],
          64: [[(HIGH, HIGH), (HIGH, MIDDLE)], [(MIDDLE, HIGH), (MIDDLE, MIDDLE)], [(HIGH, LOW), (LOW, HIGH)]]}
PARTS = 3
HEADS = 16


@dataclass
class Heads:
    k_parts: object
    q_parts: object
    v: object
    out: object
    heads: int
    at_once: int
    dh: int
    keys: int
    scale: float
    blocks: object
    valid: object = None
    lag: float = 1.9
    top: int = 0


def parts_stage(core, jobs):
    nc = core.nc
    pieces = [(x, parts, min(P, scratch.shape[1]), t) for x, parts, scratch in jobs for t in range(x.shape[1])]
    scratches = [scratch for x, _, scratch in jobs for _t in range(x.shape[1])]
    with stage(nc, "high_ready", "rest_ready", "middle_ready", "low_ready", "parts_stored") as (
            block, high_ready, rest_ready, middle_ready, low_ready, parts_stored):
        @block.scalar
        def _(act):
            for i in range(len(pieces) + 1):
                if i < len(pieces):
                    x, parts, r, t = pieces[i]
                    nc.scalar.copy(parts[0:r, HIGH, t], x[0:r, t]).then_inc(high_ready, 1)
                if i >= 1:
                    x, parts, r, t = pieces[i - 1]
                    act.wait_ge(rest_ready, i)
                    nc.scalar.copy(parts[0:r, MIDDLE, t], x[0:r, t]).then_inc(middle_ready, 1)

        @block.vector
        def _(dve):
            for i in range(len(pieces) + 1):
                if i < len(pieces):
                    x, parts, r, t = pieces[i]
                    dve.wait_ge(high_ready, i + 1)
                    nc.vector.tensor_tensor(x[0:r, t], x[0:r, t], parts[0:r, HIGH, t], ALU.subtract).then_inc(rest_ready, 1)
                if i >= 1:
                    x, parts, r, t = pieces[i - 1]
                    dve.wait_ge(middle_ready, i)
                    nc.vector.tensor_tensor(parts[0:r, LOW, t], x[0:r, t], parts[0:r, MIDDLE, t], ALU.subtract).then_inc(low_ready, 1)

        @block.sync
        def _(sp):
            for i, (x, parts, r, t) in enumerate(pieces):
                scratch = scratches[i]
                for part, ready in ((HIGH, high_ready), (MIDDLE, middle_ready), (LOW, low_ready)):
                    sp.wait_ge(ready, i + 1)
                    sp.dma_start(scratch[part, t * P:t * P + r], parts[0:r, part, t]).then_inc(parts_stored, 16)
            sp.wait_ge(parts_stored, 16 * PARTS * len(pieces))


def scratch_for(core, name, rows, n):
    return core.nc.dram_tensor(core.named(name), (PARTS, rows, n), BF16, kind="Internal").ap()


def load_batches(heads):
    cuts = [c for c in (0, 2, 6) if c < heads] + [heads]
    return [(x, y) for x, y in zip(cuts, cuts[1:]) if y > x]


def stacked_loads(engine, a, g, to, parts_of, side, semaphores):
    heads_of = parts_of.rearrange("c (h d) n -> c h d n", d=a.dh)
    for (h0, h1), loaded in zip(load_batches(a.at_once), semaphores):
        for term, rows in enumerate(STACKS[a.dh]):
            for r, parts in enumerate(rows):
                of = heads_of[parts[side], bass.ds(g * a.at_once + h0, h1 - h0)].rearrange("h d n -> d h n")
                engine.dma_start(to[r * a.dh:(r + 1) * a.dh, term, h0:h1], of).then_inc(loaded, 16)


def batch_loads(a):
    return 16 * sum(len(rows) for rows in STACKS[a.dh])


def value_slot(dh):
    return 32 if dh < 32 else dh + 1


def copy_values(pool, a, g, vg, copied):
    KT = (a.keys + P - 1) // P
    full = KT if kt_rows(a.keys, KT - 1) == P else KT - 1
    here = bass.ds(g * a.at_once, a.at_once)
    if full:
        pool.tensor_copy(vg[:, 0:full], a.v[:, 0:full, here]).then_inc(copied, 1)
    if full < KT:
        r = kt_rows(a.keys, KT - 1)
        pool.tensor_copy(vg[0:r, full], a.v[0:r, full, here]).then_inc(copied, 1)


def value_pieces(a):
    KT = (a.keys + P - 1) // P
    ragged = kt_rows(a.keys, KT - 1) < P
    return (1 if KT > 1 or not ragged else 0) + (1 if ragged else 0)


def attention_stage(core, a, g, bufs):
    nc = core.nc
    HB, dh = a.at_once, a.dh
    TERMS = STACKS[dh]
    KT = (a.keys + P - 1) // P
    slot = value_slot(dh)
    side_by_side = slot == 32
    stacked = len(TERMS[0]) * dh
    qs, ks, og = bufs.qs, bufs.ks, bufs.og
    vg = bufs.vg
    CHUNK = 2 * BANK
    RING = bufs.ring.shape[1]

    head_chunks = []
    chunks_of_tile = 0
    for q in range(TT):
        bl = a.blocks(q)
        k0, k1 = bl[0][0] * P, min(a.keys, (bl[-1][0] + 1) * P)
        for i, c in enumerate(range(k0, k1, CHUNK)):
            head_chunks.append((q, i, c, min(CHUNK, k1 - c), [(kt, m) for kt, m, _ in bl if m is not None and c <= kt * P < c + CHUNK]))
            chunks_of_tile = max(chunks_of_tile, i + 1)
    CH = len(head_chunks)
    blocks = []
    for kt in range(KT):
        seen = [q for q in range(TT) if any(b[0] == kt for b in a.blocks(q))]
        masks = [(q, next(b[2] for b in a.blocks(q) if b[0] == kt)) for q in seen]
        blocks.append((kt, kt_rows(a.keys, kt), seen[0], len(seen), [(q, m) for q, m in masks if m is not None]))
    BL = len(blocks)
    first_block = [min(i for i, bl in enumerate(blocks) if bl[2] <= q < bl[2] + bl[3]) for q in range(TT)]
    last_block = [max(i for i, bl in enumerate(blocks) if bl[2] <= q < bl[2] + bl[3]) for q in range(TT)]

    order = sorted([(h + (i + 0.5) / CH, 0, h, i) for h in range(HB) for i in range(CH)] +
                   [(h + a.lag + (i + 0.5) / BL, 1, h, i) for h in range(HB) for i in range(BL)])
    plan = []
    turned, behind, outputs = 0, [], []
    for _, stream, h, i in order:
        if stream == 0:
            plan.append(("scores", h, i))
            if turned < h and i >= min(2, CH - 1):
                plan.append(("negative", turned, 0))
                turned += 1
        else:
            while turned <= h:
                plan.append(("negative", turned, 0))
                turned += 1
            plan.append(("shifted", h, i))
            if behind:
                plan.append(("values",) + behind[0])
                if outputs and behind[0][1] == 1 % BL:
                    plan.append(("output", outputs.pop(0), 0))
                if behind[0][1] == BL - 1:
                    outputs.append(behind[0][0])
            behind = [(h, i)]
    plan.append(("values",) + behind[0])
    outputs.append(behind[0][0])
    plan += [("output", h, 0) for h in outputs]

    batches = load_batches(HB)
    with stage(nc, *[f"operands_{i}_loaded" for i in range(len(batches))], "v_copied", "scores_ready", "maximum_taken", "negative_ready",
               "negative_turned", "negative_copied", "gp_step", "parts_ready", "largest_loaded_even", "largest_loaded_odd", "shifted_ready", "exp_ready", "values_added",
               "output_copied", "output_turned", "out_kept", "dve_step") as (block, *sems):
        loaded = sems[:len(batches)]
        (v_copied, scores_ready, maximum_taken, negative_ready, negative_turned, negative_copied, gp_step, parts_ready,
         *largest_loaded, shifted_ready, exp_ready, values_added, output_copied, output_turned, out_kept, dve_step) = sems[len(batches):]

        @block.sync
        def _(sp):
            stacked_loads(sp, a, g, ks, a.k_parts, 0, loaded)
            for h in range(HB):
                sp.wait_ge(parts_ready, h + 1)
                for part in range(PARTS):
                    sp.dma_start(bufs.largest_row(part, h), bufs.max_parts[:, h % 2, part]).then_inc(largest_loaded[h % 2], 16)

        @block.gpsimd
        def _(pool):
            if a.at_once < a.heads:
                copy_values(pool, a, g, vg, v_copied)
            step = stepper(pool, gp_step)
            for h in range(HB):
                pool.wait_ge(negative_copied, h + 1)
                if h >= 2:
                    pool.wait_ge(largest_loaded[h % 2], 16 * PARTS * (h // 2))
                negative, parts = bufs.negative[:, h % 2], bufs.max_parts[:, h % 2]
                step(pool.tensor_copy(parts[:, HIGH], negative))
                step(pool.tensor_tensor(negative, negative, parts[:, HIGH], ALU.subtract))
                step(pool.tensor_copy(parts[:, MIDDLE], negative))
                pool.tensor_tensor(parts[:, LOW], negative, parts[:, MIDDLE], ALU.subtract).then_inc(parts_ready, 1)

        @block.tensor
        def _(pe):
            def scores(h, i):
                n = CH * h + i
                q, _, c, w, masks = head_chunks[i]
                if i == 0 and h in [b[0] for b in batches]:
                    pe.wait_ge(loaded[[b[0] for b in batches].index(h)], 2 * batch_loads(a))
                if n >= 2:
                    pe.wait_ge(maximum_taken, n - 1)
                base = (n % 2) * CHUNK
                for o in range(0, w, BANK):
                    m = min(BANK, w - o)
                    inside = [(kt, mask) for kt, mask in masks if c + o <= kt * P < c + o + m]
                    out = core.psum[:, base + o:base + o + m]
                    for t in range(len(TERMS)):
                        last = nc.tensor.matmul(out, qs[0:stacked, t, h, q * P:(q + 1) * P], ks[0:stacked, t, h, c + o:c + o + m],
                                                start=(t == 0), stop=(t == len(TERMS) - 1 and not inside))
                    for j, (kt, mask) in enumerate(inside):
                        at = base + kt * P - c
                        last = nc.tensor.matmul(core.psum[:, at:at + kt_rows(a.keys, kt)], core.ident16[:], mask,
                                                start=False, stop=(j == len(inside) - 1))
                last.then_inc(scores_ready, 1)

            def shifted(h, i):
                e = BL * h + i
                kt, rows, q0, nq, masks = blocks[i]
                if i == 0:
                    pe.wait_ge(largest_loaded[h % 2], 16 * PARTS * (h // 2 + 1))
                if e >= 2:
                    pe.wait_ge(exp_ready, e - 1)
                bank = core.bank(4 + e % 2)
                terms = bufs.shifted_terms(h, slice(kt * P, kt * P + rows), slice(q0 * P, (q0 + nq) * P), rows)
                for t, (lhsT, rhs) in enumerate(terms):
                    last = nc.tensor.matmul(bank[0:rows, 0:nq * P], lhsT, rhs, start=(t == 0), stop=(t == len(terms) - 1 and not masks))
                for j, (q, mask) in enumerate(masks):
                    last = nc.tensor.matmul(bank[0:rows, (q - q0) * P:(q - q0 + 1) * P], core.ident16[0:rows, 0:rows], mask,
                                            start=False, stop=(j == len(masks) - 1))
                last.then_inc(shifted_ready, 1)

            def values(h, i):
                e = BL * h + i
                kt, rows, q0, nq, _ = blocks[i]
                pe.wait_ge(exp_ready, e + 1)
                if e == 0 and a.at_once < a.heads:
                    pe.wait_ge(v_copied, value_pieces(a))
                if i == 0 and h >= 1:
                    pe.wait_ge(output_copied, h)
                if side_by_side:
                    for q in range(q0, q0 + nq):
                        last = nc.tensor.matmul(core.bank(6)[32 * q:32 * q + 32, 0:P], vg[0:rows, kt, h],
                                                bufs.ring[0:rows, e % RING, (q - q0) * P:(q - q0 + 1) * P],
                                                start=(i == first_block[q]), stop=(i == last_block[q]))
                else:
                    last = nc.tensor.matmul(core.bank(6)[0:slot, 0:nq * P], vg[0:rows, kt, h], bufs.ring[0:rows, e % RING, 0:nq * P],
                                            start=(i == 0), stop=(i == BL - 1))
                last.then_inc(values_added, 1)

            last_in_bank_7 = None
            for what, h, i in plan:
                if what == "scores":
                    scores(h, i)
                elif what == "shifted":
                    shifted(h, i)
                elif what == "values":
                    values(h, i)
                else:
                    if last_in_bank_7:
                        pe.wait_ge(*last_in_bank_7)
                    if what == "negative":
                        pe.wait_ge(negative_ready, h + 1)
                        nc.tensor.transpose(core.bank(7)[0:TT, 0:P], bufs.largest[:, h % 2], core.ident[:]).then_inc(negative_turned, 1)
                        last_in_bank_7 = (negative_copied, h + 1)
                    else:
                        pe.wait_ge(output_copied, h + 1)
                        if side_by_side:
                            last = nc.tensor.transpose(core.bank(7)[:, 0:P], bufs.output[:, 0:P], core.ident[:])
                        else:
                            for q in range(TT):
                                last = nc.tensor.transpose(core.bank(7)[:, q * slot:(q + 1) * slot], bufs.output[0:slot, q * P:(q + 1) * P],
                                                           core.ident[0:slot, 0:slot])
                        last.then_inc(output_turned, 1)
                        last_in_bank_7 = (out_kept, h + 1)

        @block.scalar
        def _(act):
            stacked_loads(act, a, g, qs, a.q_parts, 1, loaded)
            for what, h, i in plan:
                if what == "shifted":
                    e = BL * h + i
                    _, rows, _, nq, _ = blocks[i]
                    act.wait_ge(shifted_ready, e + 1)
                    if e >= RING:
                        act.wait_ge(values_added, e - RING + 1)
                    nc.scalar.activation(bufs.ring[0:rows, e % RING, 0:nq * P], core.bank(4 + e % 2)[0:rows, 0:nq * P], ACT.Exp,
                                         scale=a.scale).then_inc(exp_ready, 1)
                elif what == "values" and i == BL - 1:
                    act.wait_ge(values_added, BL * (h + 1))
                    if h >= 1:
                        act.wait_ge(output_turned, h)
                    if side_by_side:
                        nc.scalar.copy(bufs.output[:, 0:P], core.bank(6)[:, 0:P]).then_inc(output_copied, 1)
                    else:
                        nc.scalar.copy(bufs.output[0:slot, :], core.bank(6)[0:slot, 0:S]).then_inc(output_copied, 1)

        @block.vector
        def _(dve):
            step = stepper(dve, dve_step)
            v = nc.vector
            for what, h, i in plan:
                if what == "scores":
                    n = CH * h + i
                    q, place, _, w, _ = head_chunks[i]
                    dve.wait_ge(scores_ready, n + 1)
                    base = (n % 2) * CHUNK
                    v.reduce_max(bufs.maxima[:, h % 2, q, place:place + 1], core.psum[:, base:base + w], AX.X).then_inc(maximum_taken, 1)
                    if i == CH - 1:
                        dve.wait_ge(maximum_taken, CH * (h + 1))
                        if h >= 2:
                            dve.wait_ge(negative_turned, h - 1)
                        v.tensor_reduce(bufs.largest[:, h % 2], bufs.maxima[:, h % 2, :, 0:chunks_of_tile], AX.X, ALU.max,
                                        negate=True).then_inc(negative_ready, 1)
                elif what == "negative":
                    dve.wait_ge(negative_turned, h + 1)
                    if h >= 2:
                        dve.wait_ge(parts_ready, h - 1)
                    v.tensor_copy(bufs.negative[:, h % 2], core.bank(7)[0:TT, 0:P]).then_inc(negative_copied, 1)
                elif what == "output":
                    dve.wait_ge(output_turned, h + 1)
                    held = core.bank(7)[:, 0:TT * slot].rearrange("p (t s) -> p t s", s=slot)
                    step(v.reciprocal(bufs.share[:], held[:, :, dh]))
                    if a.valid is not None:
                        step(v.tensor_tensor(bufs.share[:], bufs.share[:], a.valid[:], ALU.mult))
                    v.tensor_tensor(og[:, :, h * dh:(h + 1) * dh], held[:, :, 0:dh], bufs.share[:].unsqueeze(2).to_broadcast([P, TT, dh]),
                                    ALU.mult).then_inc(out_kept, 1)
            if a.at_once < a.heads:
                dve.wait_ge(out_kept, HB)
                step(v.tensor_copy(a.out[:, :, bass.ds(g * (HB * dh), HB * dh)], og[:]))


@dataclass
class Buffers:
    qs: object
    ks: object
    vg: object = None
    og: object = None
    ring: object = None
    output: object = None
    maxima: object = None
    largest: object = None
    negative: object = None
    max_parts: object = None
    share: object = None
    largest_row: object = None
    shifted_terms: object = None


def attention_buffers(core, ctx, a):
    nc = core.nc
    KT = (a.keys + P - 1) // P
    HB, dh = a.at_once, a.dh
    TERMS = STACKS[dh]
    stacked = len(TERMS[0]) * dh
    sb = lambda name, shape, dt=F32: ctx.enter_context(nc.sbuf_tensor(core.named(name), shape, dt))
    behind = stacked + PARTS <= P
    rows = stacked + PARTS if behind else P
    bufs = Buffers(qs=sb("qs", [rows, len(TERMS), HB, S], BF16), ks=sb("ks", [rows, len(TERMS), HB, a.keys], BF16),
                   ring=sb("ring", [P, 4, S]), output=sb("output", [P, P if value_slot(dh) == 32 else S]),
                   maxima=sb("maxima", [P, 2, TT, 2]), largest=sb("largest", [P, 2, TT]), negative=sb("negative", [TT, 2, P]),
                   max_parts=sb("max_parts", [TT, 2, PARTS, P], BF16), share=sb("share", [P, TT]))
    if HB < a.heads:
        bufs.vg, bufs.og = sb("vg", [P, KT, HB, value_slot(dh)]), sb("og", [P, TT, HB * dh])
    else:
        bufs.vg, bufs.og = a.v, a.out
    if behind:
        bufs.largest_row = lambda part, h: bufs.qs[stacked + part:stacked + part + 1, 0, h].rearrange("o (t n) -> o t n", n=P)
        bufs.shifted_terms = lambda h, keys, queries, n: [(bufs.ks[:, 0, h, keys], bufs.qs[:, 0, h, queries])]
        ones = bufs.ks[stacked:rows, 0]
    else:
        largest_rows, ones_rows = sb("largest_rows", [PARTS, HB, S], BF16), sb("ones_rows", [PARTS, P], BF16)
        bufs.largest_row = lambda part, h: largest_rows[part:part + 1, h].rearrange("o (t n) -> o t n", n=P)
        bufs.shifted_terms = lambda h, keys, queries, n: [
            *[(bufs.ks[:, t, h, keys], bufs.qs[:, t, h, queries]) for t in range(len(TERMS))],
            (ones_rows[:, 0:n], largest_rows[:, h, queries])]
        ones = ones_rows[:]
    with stage(nc, "filled") as (block, filled):
        @block.vector
        def _(dve):
            nc.vector.memset(ones, 1.0).then_inc(filled, 1)
            dve.wait_ge(filled, 1)
    return bufs


def attention(core, a, bufs=None):
    nc = core.nc
    with ExitStack() as ctx:
        if bufs is None:
            bufs = attention_buffers(core, ctx, a)
        if a.at_once < a.heads:
            with loop(nc, a.heads // a.at_once) as g:
                attention_stage(core, a, g, bufs)
        else:
            attention_stage(core, a, 0, bufs)


@dataclass
class TopBuffers:
    qs: object
    ks: object
    vg: object
    og: object
    exps: object
    below: object
    probs: object
    signs: object
    probsT: object
    output: object
    candidates: object
    first: object
    edge: object
    next_best: object
    negmax: object
    edge_exp: object
    low: object
    balance: object
    wanted: object
    bound: object
    last_kept: object
    picked: object
    kept_signs: object
    kept: object
    share: object
    wrong: object
    flags: object


BEST = 8


def segments_of(keys):
    count = 20
    width = (keys + count - 1) // count
    return [(i, min(width, keys - i)) for i in range(0, keys, width)]


def top_attention_stage(core, a, g, bufs, exact):
    nc = core.nc
    HB, dh, M_ = a.at_once, a.dh, a.keys
    (stack,) = STACKS[dh]
    stacked = len(stack) * dh
    KT = (M_ + P - 1) // P
    slot = value_slot(dh)
    tiles = [(h, q) for h in range(HB) for q in range(TT)]
    N = len(tiles)
    LAG = 1 if exact else 2
    segments = segments_of(M_)
    turns = [(kt, min(BANK // P, KT - kt)) for kt in range(0, KT, BANK // P)]
    TC = len(turns)
    heads_out = {TT * (h + 1) + LAG + 1: h for h in range(HB - 1)}
    scores_held = core.psum[:, 0:M_]
    batches = load_batches(HB)
    with stage(nc, *[f"operands_{i}_loaded" for i in range(len(batches))], "v_copied", "scores_ready", "scores_copied", "first_taken",
               "maximum_ready", "edge_ready", "edge_exp_ready", "low_ready", "exp_ready", "below_ready", "below_taken", "counted",
               "probs_ready", "checked", "probs_turned", "turned_copied", "values_ready", "output_copied", "output_turned", "out_kept",
               "round_step", "last_ready", "bound_ready", "dve_step") as (block, *sems):
        loaded = sems[:len(batches)]
        (v_copied, scores_ready, scores_copied, first_taken, maximum_ready, edge_ready, edge_exp_ready, low_ready, exp_ready,
         below_ready, below_taken, counted, probs_ready, checked, probs_turned, turned_copied, values_ready, output_copied,
         output_turned, out_kept, round_step, last_ready, bound_ready, dve_step) = sems[len(batches):]

        @block.sync
        def _(sp):
            stacked_loads(sp, a, g, bufs.ks, a.k_parts, 0, loaded)

        @block.gpsimd
        def _(pool):
            copy_values(pool, a, g, bufs.vg[:, :, 0:HB], v_copied)
            if exact:
                return

            def keep(n):
                pool.wait_ge(checked, n + 1)
                if n >= 1:
                    pool.wait_ge(probs_turned, TC * n)
                pool.tensor_tensor(bufs.probs[:], bufs.exps[:, n % 2], bufs.kept_signs[:], ALU.mult).then_inc(probs_ready, 1)

            for n in range(N):
                if n >= 1:
                    keep(n - 1)
                pool.wait_ge(counted, n + 1)
                if n >= 1:
                    pool.wait_ge(below_taken, n)
                pool.tensor_tensor(bufs.below[:], bufs.exps[:, n % 2], bufs.signs[:], ALU.mult).then_inc(below_ready, 1)
            keep(N - 1)

        @block.tensor
        def _(pe):
            def scores(n):
                h, q = tiles[n]
                if q == 0 and h in [b[0] for b in batches]:
                    pe.wait_ge(loaded[[b[0] for b in batches].index(h)], 2 * batch_loads(a))
                if n >= 1:
                    pe.wait_ge(scores_copied if exact else exp_ready, n)
                for c in range(0, M_, BANK):
                    w = min(BANK, M_ - c)
                    last = nc.tensor.matmul(core.psum[:, c:c + w], bufs.qs[0:stacked, 0, h, q * P:(q + 1) * P],
                                            bufs.ks[0:stacked, 0, h, c:c + w], start=True, stop=True)
                last.then_inc(scores_ready, 1)

            def turn(n):
                pe.wait_ge(probs_ready, n + 1)
                for i, (kt, count) in enumerate(turns):
                    e = TC * n + i
                    if e >= 2:
                        pe.wait_ge(turned_copied, e - 1)
                    for j in range(count):
                        r = kt_rows(M_, kt + j)
                        last = nc.tensor.transpose(core.bank(4 + e % 2)[0:r, j * P:(j + 1) * P],
                                                   bufs.probs[:, (kt + j) * P:(kt + j) * P + r], core.ident[:])
                    last.then_inc(probs_turned, 1)

            def values(n):
                h, q = tiles[n]
                pe.wait_ge(turned_copied, TC * (n + 1))
                if n == 0:
                    pe.wait_ge(v_copied, value_pieces(a))
                if q == 0 and h >= 1:
                    pe.wait_ge(output_copied, h)
                for kt in range(KT):
                    r = kt_rows(M_, kt)
                    last = nc.tensor.matmul(core.bank(6)[slot * q:slot * (q + 1), 0:P], bufs.vg[0:r, kt, h],
                                            bufs.probsT[0:r, kt, q * P:(q + 1) * P], start=(kt == 0), stop=(kt == KT - 1))
                last.then_inc(values_ready, 1)

            def turn_output(h):
                pe.wait_ge(output_copied, h + 1)
                if h >= 1:
                    pe.wait_ge(out_kept, h)
                nc.tensor.transpose(core.bank(7)[:, 0:P], bufs.output[:], core.ident[:]).then_inc(output_turned, 1)

            for n in range(N + LAG + 1):
                if n < N:
                    scores(n)
                if n >= LAG + 1:
                    values(n - LAG - 1)
                if n in heads_out:
                    turn_output(heads_out[n])
                if LAG <= n < N + LAG:
                    turn(n - LAG)
            turn_output(HB - 1)

        @block.scalar
        def _(act):
            stacked_loads(act, a, g, bufs.qs, a.q_parts, 1, loaded)

            def copy_turned(n):
                h, q = tiles[n]
                for i, (kt, count) in enumerate(turns):
                    e = TC * n + i
                    act.wait_ge(probs_turned, e + 1)
                    if i == 0 and h >= 1:
                        act.wait_ge(values_ready, n - TT + 1)
                    r = kt_rows(M_, kt + count - 1)
                    nc.scalar.activation(bufs.probsT[0:r, kt:kt + count, q * P:(q + 1) * P],
                                         core.bank(4 + e % 2)[0:r, 0:count * P].rearrange("p (k n) -> p k n", n=P), ACT.Relu).then_inc(turned_copied, 1)

            def check(n):
                act.wait_ge(bound_ready, n + 1)
                if n >= 1:
                    act.wait_ge(probs_ready, n)
                nc.scalar.activation(bufs.kept_signs[:], bufs.exps[:, n % 2], ACT.Sign, bias=bufs.bound[:, n % 2:n % 2 + 1],
                                     accum_out=bufs.kept[:, n:n + 1]).then_inc(checked, 1)

            for n in range(N + LAG + 1):
                if LAG <= n < N + LAG and (exact or n >= N):
                    copy_turned(n - LAG)
                if n < N:
                    if exact:
                        act.wait_ge(scores_ready, n + 1)
                        if n >= 1:
                            act.wait_ge(first_taken, n)
                        nc.scalar.copy(bufs.below[:], scores_held).then_inc(scores_copied, 1)
                        act.wait_ge(scores_copied, n + 1)
                    act.wait_ge(maximum_ready, n + 1)
                    if n >= 2:
                        act.wait_ge(probs_ready, n - 1)
                    nc.scalar.activation(bufs.exps[:, n % 2], bufs.below[:] if exact else scores_held, ACT.Exp, scale=a.scale,
                                         bias=bufs.negmax[:, n % 2:n % 2 + 1]).then_inc(exp_ready, 1)
                    if not exact:
                        if n >= LAG:
                            copy_turned(n - LAG)
                        if n >= 1:
                            check(n - 1)
                        act.wait_ge(edge_ready, n + 1)
                        act.wait_ge(exp_ready, n + 1)
                        nc.scalar.activation(bufs.edge_exp[:, n % 2:n % 2 + 1], bufs.edge[:, n % 2, BEST - 1:BEST], ACT.Exp, scale=a.scale,
                                             bias=bufs.negmax[:, n % 2:n % 2 + 1]).then_inc(edge_exp_ready, 1)
                        act.wait_ge(edge_exp_ready, n + 1)
                        nc.scalar.activation(bufs.low[:, n % 2:n % 2 + 1], bufs.edge_exp[:, n % 2:n % 2 + 1], ACT.Copy,
                                             scale=1.0 - 2.0 ** -20).then_inc(low_ready, 1)
                        act.wait_ge(low_ready, n + 1)
                        if n >= 1:
                            act.wait_ge(below_ready, n)
                        nc.scalar.activation(bufs.signs[:], bufs.exps[:, n % 2], ACT.Sign, scale=-1.0, bias=bufs.low[:, n % 2:n % 2 + 1],
                                             accum_out=bufs.balance[:, n % 2:n % 2 + 1]).then_inc(counted, 1)
                if n == N and not exact:
                    check(N - 1)
                if n >= LAG + 1 and (n - LAG) % TT == 0:
                    h = (n - LAG) // TT - 1
                    act.wait_ge(values_ready, TT * (h + 1))
                    if h >= 1:
                        act.wait_ge(output_turned, h)
                    nc.scalar.copy(bufs.output[:], core.bank(6)[:, 0:P]).then_inc(output_copied, 1)

        @block.vector
        def _(dve):
            step = stepper(dve, dve_step)
            v = nc.vector

            def take_maximum(n, best):
                if n >= 2:
                    dve.wait_ge(exp_ready if exact else edge_exp_ready, n - 1)
                v.tensor_scalar(bufs.negmax[:, n % 2:n % 2 + 1], best, -a.scale, None, ALU.mult).then_inc(maximum_ready, 1)

            def all_taken(n):
                dve.wait_ge(scores_copied, n + 1)
                if n >= 1:
                    dve.wait_ge(probs_turned, TC * n)
                source = bufs.below[:]
                for i in range(a.top // BEST):
                    step(v.max(bufs.first[:, n % 2], source))
                    if i == 0:
                        take_maximum(n, bufs.first[:, n % 2, 0:1])
                        dve.wait_ge(maximum_ready, n + 1)
                    step(v.match_replace(bufs.probs[:], bufs.first[:, n % 2], source, TAKEN))
                    if i == 0:
                        v.sem_inc(first_taken, 1)
                    source = bufs.probs[:]
                dve.wait_ge(exp_ready, n + 1)
                v.scalar_tensor_tensor(out=bufs.probs[:], in0=bufs.probs[:], scalar=TAKEN / 2, in1=bufs.exps[:, n % 2],
                                       op0=ALU.is_lt, op1=ALU.mult).then_inc(probs_ready, 1)

            def split(n, between):
                if n >= 1:
                    dve.wait_ge(edge_ready, n)
                dve.wait_ge(scores_ready, n + 1)
                for i, (c, w) in enumerate(segments):
                    last = v.max(bufs.candidates[:, i * BEST:(i + 1) * BEST], core.psum[:, c:c + w])
                step(last)
                rounds = a.top // BEST - 1
                done = n * 2 * (rounds - 1)
                for i in range(rounds - 1):
                    best = bufs.first[:, i % 2]
                    v.max(best, bufs.candidates[:]).then_inc(round_step, 1)
                    if between and i >= 3:
                        between.pop(0)()
                    dve.wait_ge(round_step, done + 2 * i + 1)
                    if i == 0:
                        take_maximum(n, best[:, 0:1])
                    v.match_replace(bufs.candidates[:], best, bufs.candidates[:], TAKEN).then_inc(round_step, 1)
                    if between and i >= 3:
                        between.pop(0)()
                    dve.wait_ge(round_step, done + 2 * i + 2)
                if n >= 2:
                    dve.wait_ge(edge_exp_ready, n - 1)
                v.max(bufs.edge[:, n % 2], bufs.candidates[:]).then_inc(edge_ready, 1)

            def selection(n):
                def take_below():
                    dve.wait_ge(below_ready, n + 1)
                    v.max(bufs.next_best[:], bufs.below[:]).then_inc(below_taken, 1)

                def pick_last():
                    dve.wait_ge(below_taken, n + 1)
                    dve.wait_ge(counted, n + 1)
                    v.scalar_tensor_tensor(out=bufs.picked[:], in0=bufs.wanted[:], scalar=bufs.balance[:, n % 2:n % 2 + 1], in1=bufs.next_best[:],
                                           op0=ALU.is_equal, op1=ALU.mult, accum_out=bufs.last_kept[:]).then_inc(last_ready, 1)

                def bound_it():
                    dve.wait_ge(last_ready, n + 1)
                    if n >= 2:
                        dve.wait_ge(checked, n - 1)
                    v.tensor_scalar(bufs.bound[:, n % 2:n % 2 + 1], bufs.last_kept[:], 2.0 ** -24 - 1.0, None, ALU.mult).then_inc(bound_ready, 1)

                return [take_below, pick_last, bound_it]

            def keep_output(h):
                dve.wait_ge(output_turned, h + 1)
                held = core.bank(7)[:, 0:P].rearrange("p (t s) -> p t s", s=slot)
                step(v.reciprocal(bufs.share[:], held[:, :, dh]))
                v.tensor_tensor(bufs.og[:, :, h * dh:(h + 1) * dh], held[:, :, 0:dh],
                                bufs.share[:].unsqueeze(2).to_broadcast([P, TT, dh]), ALU.mult).then_inc(out_kept, 1)

            for n in range(N + LAG + 1):
                if exact:
                    if n < N:
                        all_taken(n)
                else:
                    if n < N:
                        split(n, selection(n - 1) if n >= 1 else [])
                    elif n == N:
                        for part in selection(N - 1):
                            part()
                if n in heads_out:
                    keep_output(heads_out[n])
            keep_output(HB - 1)
            dve.wait_ge(out_kept, HB)
            step(v.tensor_copy(a.out[:, :, bass.ds(g * (HB * dh), HB * dh)], bufs.og[:, :, 0:HB * dh]))
            if not exact:
                dve.wait_ge(checked, N)
                step(v.tensor_scalar(bufs.kept[:], bufs.kept[:], float(2 * a.top - M_ + 1), None, ALU.is_gt))
                step(v.reduce_max(bufs.wrong[:, 0:HB], bufs.kept[:].rearrange("p (h q) -> p h q", q=TT), AX.X))
                step(v.reduce_max(bufs.wrong[:, HB:HB + 1], bufs.wrong[:, 0:HB], AX.X))


def top_flag_stage(core, bufs):
    nc = core.nc
    n = bufs.wrong.shape[1]
    with stage(nc, "summed", "flag_ready") as (block, summed, flag_ready):
        @block.tensor
        def _(pe):
            nc.tensor.matmul(core.bank(0)[0:1, 0:n], core.ones[:, 0:1], bufs.wrong[:], start=True, stop=True).then_inc(summed, 1)

        @block.vector
        def _(dve):
            dve.wait_ge(summed, 1)
            nc.vector.tensor_copy(bufs.flags[:], core.bank(0)[0:1, 0:n]).then_inc(flag_ready, 1)
            dve.wait_ge(flag_ready, 1)


def top_attention(core, a):
    nc = core.nc
    KT = (a.keys + P - 1) // P
    HB, dh = a.at_once, a.dh
    (stack,) = STACKS[dh]
    stacked = len(stack) * dh
    N = HB * TT
    with ExitStack() as ctx:
        sb = lambda name, shape, dt=F32: ctx.enter_context(nc.sbuf_tensor(core.named(name), shape, dt))
        bufs = TopBuffers(
            qs=sb("qs", [stacked, 1, HB, S], BF16), ks=sb("ks", [stacked, 1, HB, a.keys], BF16), vg=sb("vg", [P, KT, HB, value_slot(dh)]),
            og=sb("og", [P, TT, HB * dh]), exps=sb("exps", [P, 2, a.keys]), below=sb("below", [P, a.keys]), probs=sb("probs", [P, a.keys]),
            signs=sb("signs", [P, a.keys], BF16), probsT=sb("probsT", [P, KT, S]), output=sb("output", [P, P]),
            candidates=sb("candidates", [P, BEST * len(segments_of(a.keys))]), first=sb("first", [P, 2, BEST]), edge=sb("edge", [P, 2, BEST]),
            next_best=sb("next_best", [P, BEST]), negmax=sb("negmax", [P, 2]), edge_exp=sb("edge_exp", [P, 2]), low=sb("low", [P, 2]),
            balance=sb("balance", [P, 2]), wanted=sb("wanted", [P, BEST]), bound=sb("bound", [P, 2]), last_kept=sb("last_kept", [P, 1]),
            picked=sb("picked", [P, BEST]), kept_signs=sb("kept_signs", [P, a.keys], BF16), kept=sb("kept", [P, N]),
            share=sb("share", [P, TT]), wrong=sb("wrong", [P, HB + 1]),
            flags=sb("flags", [1, HB + 1], I32))
        with stage(nc, "filled") as (block, filled):
            @block.vector
            def _(dve):
                for j in range(BEST):
                    nc.vector.memset(bufs.wanted[:, j:j + 1], a.keys - 2.0 * (a.top - (j + 1))).then_inc(filled, 1)
                dve.wait_ge(filled, BEST)
        with loop(nc, a.heads // HB) as g:
            top_attention_stage(core, a, g, bufs, exact=False)
            top_flag_stage(core, bufs)
            wrong = nc.values_load(bufs.flags[0:1, HB:HB + 1], min_val=0, max_val=P)
            with branch(nc, wrong > 0):
                with loop(nc, HB) as h:
                    wrong_of_head = nc.values_load(bufs.flags[0:1, bass.ds(h, 1)], min_val=0, max_val=P)
                    with branch(nc, wrong_of_head > 0):
                        top_attention_stage(core, replace(a, at_once=1), g * HB + h, bufs, exact=True)


def values_into(core, v, dh):
    nc = core.nc

    def evacuation(t, r):
        engine = ("act", "dve")[t % 2]
        to = v[0:r, t, :, 0:dh]

        def evacuate(bank):
            of = bank[0:r, 0:v.shape[2] * dh].rearrange("p (h s) -> p h s", s=dh)
            return nc.scalar.copy(to, of) if engine == "act" else nc.vector.tensor_copy(to, of)
        return engine, evacuate
    return evacuation


class Split:

    def __init__(self, core, ctx, **tiles):
        self.x, self.parts = {}, {}
        for name, (t, n) in tiles.items():
            self.x[name] = ctx.enter_context(core.nc.sbuf_tensor(core.named("whole_" + name), [P, t, n], F32))
            self.parts[name] = ctx.enter_context(core.nc.sbuf_tensor(core.named("parts_" + name), [P, PARTS, t, n], BF16))

    def store(self, core, **scratch):
        parts_stage(core, [(self.x[k], self.parts[k], scratch[k]) for k in scratch])


def all_blocks(keys):
    return lambda q: [(kt, None, None) for kt in range((keys + P - 1) // P)]


def causal_blocks(core):
    return lambda q: [(kt, None, None) for kt in range(q)] + [(q, core.causal16[:], core.causalT16[:])]


def context_columns(core, ctx_in, b, ctxT):
    nc = core.nc
    with ExitStack() as held:
        rows = held.enter_context(nc.sbuf_tensor(core.named("ctx_rows"), [P, MT, D], F32))
        context_load(core, ctx_in, b, rows)
        product_stage(core, turned(core, rows, ctxT, rows=M))


def context_load(core, ctx_in, b, rows):
    nc = core.nc
    full = M // P
    with stage(nc, "context_loaded") as (block, context_loaded):
        @block.sync
        def _(sp):
            here = ctx_in[bass.ds(b, 1)]
            sp.dma_start(rows[:, 0:full], here[:, 0:full * P].rearrange("o (t p) d -> p (o t) d", p=P)).then_inc(context_loaded, 16)
            sp.dma_start(rows[0:M - full * P, full], here[:, full * P:M].rearrange("o p d -> p (o d)")).then_inc(context_loaded, 16)
            sp.wait_ge(context_loaded, 32)



def matrix(w, p=P):
    return w.rearrange("(k p) n -> p k n", p=p)


def l0_attn(core, w):
    nc = core.nc
    FF = w["L0_attn_ff_w1"].shape[1]
    STEPS, STEP, AT_ONCE = 8, 0.1, 4
    with ExitStack() as ctx:
        sb = lambda name, shape: ctx.enter_context(nc.sbuf_tensor(core.named(name), shape, F32))
        wq, wk, wv = sb("wq", [P, DT, D]), sb("wk", [P, DT, D]), sb("wv", [P, DT, D])
        bq, bk, bv = sb("bq", [P, DT]), sb("bk", [P, DT]), sb("bv", [1, D])
        wo, bo_col, bo_row = sb("wo", [P, DT, D]), sb("bo_col", [P, DT]), sb("bo_row", [1, D])
        gains = {k: sb(k, [P, DT]) for k in ("g_attn", "b_attn", "g1", "b1", "g2", "b2", "b_inl")}
        w_ctx, w_x = sb("w_ctx", [P, DT, D]), sb("w_x", [P, DT, D])
        ff1, ff1_b = sb("ff1", [P, DT, FF]), sb("ff1_b", [P, FF // P])
        ff2, ff2_b = sb("ff2", [P, FF // P, D]), sb("ff2_b", [1, D])
        qkv, qkv_b = w["L0_attn_qkv_w"], w["L0_attn_qkv_b"]
        v = sb("v", [P, TT, HEADS, value_slot(D // HEADS)])
        q_parts, k_parts = scratch_for(core, "q_parts", D, S), scratch_for(core, "k_parts", D, S)
        load_stage(core, [
            (wq[:], matrix(qkv[:, 0:D])), (wk[:], matrix(qkv[:, D:2 * D])), (wv[:], matrix(qkv[:, 2 * D:3 * D])),
            (bq[:], columned(qkv_b[0:D])), (bk[:], columned(qkv_b[D:2 * D])), (bv[:], rowed(qkv_b[2 * D:3 * D])),
            (wo[:], matrix(w["L0_attn_out_w"])), (bo_col[:], columned(w["L0_attn_out_b"])), (bo_row[:], rowed(w["L0_attn_out_b"])),
            *[(t[:], columned(w["L0_attn_" + k])) for k, t in gains.items()],
            (w_ctx[:], matrix(w["L0_attn_w_ctx"])), (w_x[:], matrix(w["L0_attn_w_x"])),
            (ff1[:], matrix(w["L0_attn_ff_w1"])), (ff1_b[:], columned(w["L0_attn_ff_b1"])),
            (ff2[:], matrix(w["L0_attn_ff_w2"])), (ff2_b[:], rowed(w["L0_attn_ff_b2"])),
        ], zeroed=[v[:]], ones=[v[:, :, :, 16]])

        y = sb("y", [P, TT, D])
        o, oT = sb("o", [P, TT, D]), sb("oT", [P, DT, S])
        attnT, drive = sb("attnT", [P, DT, S]), sb("drive", [P, DT, S])
        state, speed, rest, u = (sb(n, [P, DT, S]) for n in ("state", "speed", "rest", "u"))
        hT = sb("hT", [P, FF // P, S])
        heads = Heads(k_parts, q_parts, v, o, HEADS, HEADS, 16, S, 0.25, causal_blocks(core), lag=4.0)
        heads_buffers = attention_buffers(core, ctx, heads)
        with loop(nc, B) as b:
            take_stage(core, b)
            norm_stage(core, core.x[:], lambda t: y[:, t])
            product_stage(core, turned(core, y, core.xT, scale=gains["g_attn"], bias=gains["b_attn"]))
            with ExitStack() as early:
                split = Split(core, early, q=(DT, S), k=(DT, S))
                product_stage(core, [
                    *columns_out(core, wq, core.xT, split.x["q"], S, bias=bq), *columns_out(core, wk, core.xT, split.x["k"], S, bias=bk),
                    *rows_out(core, core.xT, wv, S, D, values_into(core, v, 16), bias_row=bv[:])])
                split.store(core, q=q_parts, k=k_parts)
            attention(core, heads, heads_buffers)
            product_stage(core, turned(core, o, oT))
            product_stage(core, [
                *columns_out(core, wo, oT, attnT, S, bias=bo_col),
                *rows_out(core, oT, wo, S, D, added_to(core, core.x, core.delta), bias_row=bo_row[:])])
            norm_stage(core, core.delta[:], lambda t: y[:, t])
            product_stage(core, [
                *turned(core, y, state, scale=gains["g1"], bias=gains["b1"]),
                *columns_out(core, w_ctx, attnT, drive, S, bias=gains["b_inl"])])
            with stage(nc, "rest_ready") as (block, rest_ready):
                @block.vector
                def _(dve):
                    nc.vector.tensor_scalar(rest[:], state[:], -1.0, None, ALU.mult).then_inc(rest_ready, 1)
                    dve.wait_ge(rest_ready, 1)
            with loop(nc, STEPS // AT_ONCE) as _i:
                recurrence_stage(core, w_x, drive, state, speed, rest, u, STEP, AT_ONCE)
            product_stage(core, turned_back(core, state, added_to(core, core.delta, core.delta)))
            norm_stage(core, core.delta[:], lambda t: y[:, t])
            product_stage(core, turned(core, y, core.xT, scale=gains["g2"], bias=gains["b2"]))
            product_stage(core, columns_out(core, ff1, core.xT, hT, S, bias=ff1_b, func=ACT.Gelu, engines=("act",)))
            product_stage(core, rows_out(core, hT, ff2, S, D, added_to(core, core.delta, core.delta), bias_row=ff2_b[:]))
            residual_norm(core, b)


def recurrence_stage(core, w_x, drive, state, speed, rest, u, step_size, steps):
    nc = core.nc
    CHUNKS = 2
    W = S // CHUNKS
    turns = [slice(c * W, (c + 1) * W) for _ in range(steps) for c in range(CHUNKS)]
    with stage(nc, "products_ready", "summed", "tanh_ready", "speed_ready", "state_ready", "damped", "rest_ready") as (
            block, products_ready, summed, tanh_ready, speed_ready, state_ready, damped, rest_ready):
        @block.tensor
        def _(pe):
            for i, cut in enumerate(turns):
                if i >= CHUNKS:
                    pe.wait_ge(state_ready, i - CHUNKS + 1)
                for f in range(DT):
                    last = accumulate(nc, core.bank(i % CHUNKS)[:, f * W:(f + 1) * W],
                                      [(w_x[:, k, f * P:(f + 1) * P], state[:, k, cut]) for k in range(DT)])
                last.then_inc(products_ready, 1)

        @block.vector
        def _(dve):
            v = nc.vector

            def update(i):
                cut = turns[i]
                dve.wait_ge(tanh_ready, i + 1)
                if i >= CHUNKS:
                    dve.wait_ge(rest_ready, i - CHUNKS + 1)
                v.tensor_tensor(speed[:, :, cut], u[:, :, cut], rest[:, :, cut], ALU.add).then_inc(speed_ready, 1)
                dve.wait_ge(speed_ready, i + 1)
                v.scalar_tensor_tensor(out=state[:, :, cut], in0=speed[:, :, cut], scalar=step_size * step_size, in1=state[:, :, cut],
                                       op0=ALU.mult, op1=ALU.add).then_inc(state_ready, 1)

            for i, cut in enumerate(turns):
                if i >= 1:
                    update(i - 1)
                dve.wait_ge(products_ready, i + 1)
                v.tensor_tensor(u[:, :, cut], core.bank(i % CHUNKS)[:, 0:DT * W].rearrange("p (f n) -> p f n", n=W),
                                drive[:, :, cut], ALU.add).then_inc(summed, 1)
            update(len(turns) - 1)

        @block.scalar
        def _(act):
            for i in range(len(turns) + 1):
                if i < len(turns):
                    cut = turns[i]
                    act.wait_ge(summed, i + 1)
                    nc.scalar.activation(u[:, :, cut], u[:, :, cut], ACT.Tanh).then_inc(tanh_ready, 1)
                if i >= 1:
                    cut = turns[i - 1]
                    act.wait_ge(speed_ready, i)
                    nc.scalar.activation(rest[:, :, cut], speed[:, :, cut], ACT.Copy, scale=1.0 - step_size).then_inc(damped, 1)

        @block.gpsimd
        def _(pool):
            for i, cut in enumerate(turns):
                pool.wait_ge(damped, i + 1)
                pool.wait_ge(state_ready, i + 1)
                pool.tensor_tensor(rest[:, :, cut], rest[:, :, cut], state[:, :, cut], ALU.subtract).then_inc(rest_ready, 1)


def l0_xattn(core, w, ctx_in):
    nc = core.nc
    INNER = w["L0_xattn_Wq"].shape[1]
    with ExitStack() as ctx:
        sb = lambda name, shape: ctx.enter_context(nc.sbuf_tensor(core.named(name), shape, F32))
        wq, wk, wv = (sb(n, [P, DT, INNER]) for n in ("wq", "wk", "wv"))
        v = sb("v", [P, MT, INNER // 64, 65])
        q_parts, k_parts = scratch_for(core, "q_parts", INNER, S), scratch_for(core, "k_parts", INNER, M)
        wo, bo = sb("wo", [P, INNER // P, D]), sb("bo", [1, D])
        load_stage(core, [(wq[:], matrix(w["L0_xattn_Wq"])), (wk[:], matrix(w["L0_xattn_Wk"])),
                          (wv[:], matrix(w["L0_xattn_Wv"])), (wo[:], matrix(w["L0_xattn_Wo"])),
                          (bo[:], rowed(w["L0_xattn_bo"]))], zeroed=[v[:]], ones=[v[:, :, :, 64]])
        o = sb("o", [P, TT, INNER])
        with loop(nc, B) as b:
            take_stage(core, b)
            product_stage(core, turned(core, core.x, core.xT))
            with ExitStack() as early:
                ctxT = early.enter_context(nc.sbuf_tensor(core.named("ctxT"), [P, DT, M], F32))
                context_columns(core, ctx_in, b, ctxT)
                split = Split(core, early, q=(INNER // P, S), k=(INNER // P, M))
                product_stage(core, [
                    *columns_out(core, wq, core.xT, split.x["q"], S), *columns_out(core, wk, ctxT, split.x["k"], M),
                    *rows_out(core, ctxT, wv, M, INNER, values_into(core, v, 64))])
                split.store(core, q=q_parts, k=k_parts)
            attention(core, Heads(k_parts, q_parts, v, o, INNER // 64, 8, 64, M, 64 ** -0.5, all_blocks(M)))
            with ExitStack() as late:
                oT = late.enter_context(nc.sbuf_tensor(core.named("oT"), [P, INNER // P, S], F32))
                product_stage(core, turned(core, o, oT, features=INNER // P))
                product_stage(core, rows_out(core, oT, wo, S, D, into(core, core.delta), bias_row=bo[:]))
            residual_norm(core, b)


def l0_ffn(core, w):
    nc = core.nc
    with ExitStack() as ctx:
        sb = lambda name, shape, dt=F32: ctx.enter_context(nc.sbuf_tensor(core.named(name), shape, dt))
        packed, codes = sb("packed", [64, D], I32), sb("codes", [64, 4, D], I32)
        ternary, wT = sb("ternary", [64, 4, D]), sb("wT", [P, DT, D])
        scale, bias = sb("scale", [P, 1]), sb("bias", [P, D])
        load_stage(core, [(packed[:], w["L0_ffn_packed_weight"].rearrange("(r c) -> r c", c=D)),
                          (scale[:], spread_over(w["L0_ffn_weight_scale"])), (bias[:], spread_over(w["L0_ffn_bias"]))])
        with stage(nc, "dve_step") as (block, dve_step):
            @block.vector
            def _(dve):
                step = stepper(dve, dve_step)
                for s in range(4):
                    step(nc.vector.tensor_scalar(codes[:, s], packed[:], 2 * s, 3, ALU.logical_shift_right, ALU.bitwise_and))
                step(nc.vector.tensor_copy(ternary[:], codes[:]))
                step(nc.vector.tensor_scalar(ternary[:], ternary[:], 1.0, None, ALU.subtract))

        def turn(f):
            def multiply(bank):
                for s in range(4):
                    last = nc.tensor.transpose(bank[:, 64 * s:64 * s + 64], ternary[:, s, f * P:(f + 1) * P], core.ident[0:64, 0:64])
                return last
            return multiply

        product_stage(core, [Job(turn(f), "dve", out_of_bank(core, "dve", wT[:, f])) for f in range(DT)])
        xq = sb("xq", [P, TT, D])
        peak, gain, back = sb("peak", [P, TT]), sb("gain", [P, TT]), sb("back", [P, TT])
        with loop(nc, B) as b:
            take_stage(core, b)
            with stage(nc, "dve_step") as (block, dve_step):
                @block.vector
                def _(dve):
                    step = stepper(dve, dve_step)
                    step(nc.vector.tensor_reduce(peak[:], core.x[:], AX.X, ALU.max, apply_absolute_value=True))
                    step(nc.vector.tensor_scalar(peak[:], peak[:], 1e-5, None, ALU.max))
                    step(nc.vector.reciprocal(gain[:], peak[:]))
                    step(nc.vector.tensor_scalar(gain[:], gain[:], 127.0, None, ALU.mult))
                    step(nc.vector.reciprocal(back[:], gain[:]))
                    for t in range(TT):
                        step(nc.vector.tensor_scalar(xq[:, t], core.x[:, t], gain[:, t:t + 1], None, ALU.mult))
                    step(nc.vector.tensor_scalar(xq[:], xq[:], ROUND, None, ALU.add))
                    step(nc.vector.tensor_scalar(xq[:], xq[:], ROUND, None, ALU.subtract))
                    step(nc.vector.tensor_scalar(xq[:], xq[:], -128.0, 127.0, ALU.max, ALU.min))
                    for t in range(TT):
                        step(nc.vector.tensor_scalar(xq[:, t], xq[:, t], back[:, t:t + 1], None, ALU.mult))
            product_stage(core, turned(core, xq, core.xT))
            product_stage(core, rows_out(core, core.xT, wT, S, D, lambda t, r: ("dve", lambda bank: (
                nc.vector.scalar_tensor_tensor(out=core.delta[:, t], in0=bank[:, 0:D], scalar=scale[:, 0:1], in1=bias[:],
                                               op0=ALU.mult, op1=ALU.add)))))
            residual_norm(core, b)


def l1_attn(core, w):
    nc = core.nc
    C = w["L1_attn_W_dq"].shape[1]
    with ExitStack() as ctx:
        sb = lambda name, shape: ctx.enter_context(nc.sbuf_tensor(core.named(name), shape, F32))
        w_dq, w_dkv = sb("w_dq", [P, DT, C]), sb("w_dkv", [P, DT, C])
        w_uq, w_uk, w_uv = sb("w_uq", [C, 1, D]), sb("w_uk", [C, 1, D]), sb("w_uv", [C, 1, D])
        v = sb("v", [P, TT, HEADS, value_slot(D // HEADS)])
        q_parts, k_parts = scratch_for(core, "q_parts", D, S), scratch_for(core, "k_parts", D, S)
        wo = sb("wo", [P, DT, D])
        load_stage(core, [
            (w_dq[:], matrix(w["L1_attn_W_dq"])), (w_dkv[:], matrix(w["L1_attn_W_dkv"])),
            (w_uq[:], matrix(w["L1_attn_W_uq"], C)), (w_uk[:], matrix(w["L1_attn_W_uk"], C)),
            (w_uv[:], matrix(w["L1_attn_W_uv"], C)), (wo[:], matrix(w["L1_attn_W_o"])),
        ], zeroed=[v[:]], ones=[v[:, :, :, 16]])
        cqT, ckvT = sb("cqT", [C, 1, S]), sb("ckvT", [C, 1, S])
        o, oT = sb("o", [P, TT, D]), sb("oT", [P, DT, S])
        heads = Heads(k_parts, q_parts, v, o, HEADS, HEADS, 16, S, 0.25, causal_blocks(core), lag=4.0)
        heads_buffers = attention_buffers(core, ctx, heads)
        with loop(nc, B) as b:
            take_stage(core, b)
            product_stage(core, turned(core, core.x, core.xT))
            product_stage(core, [*columns_out(core, w_dq, core.xT, cqT, S, m=C), *columns_out(core, w_dkv, core.xT, ckvT, S, m=C)])
            with ExitStack() as early:
                split = Split(core, early, q=(DT, S), k=(DT, S))
                product_stage(core, [*columns_out(core, w_uq, cqT, split.x["q"], S), *columns_out(core, w_uk, ckvT, split.x["k"], S),
                                     *rows_out(core, ckvT, w_uv, S, D, values_into(core, v, 16))])
                split.store(core, q=q_parts, k=k_parts)
            attention(core, heads, heads_buffers)
            product_stage(core, turned(core, o, oT))
            product_stage(core, rows_out(core, oT, wo, S, D, into(core, core.delta)))
            residual_norm(core, b)


def l1_xattn(core, w, ctx_in):
    nc = core.nc
    R = w["L1_xattn_Uq"].shape[1]
    assert R == P
    with ExitStack() as ctx:
        sb = lambda name, shape: ctx.enter_context(nc.sbuf_tensor(core.named(name), shape, F32))
        up = {k: sb("up_" + k, [P, DT, R]) for k in "qkvo"}
        down = {k: sb("down_" + k, [R, 1, D]) for k in "qkvo"}
        bq, bk, bv, bo = sb("bq", [P, DT]), sb("bk", [P, DT]), sb("bv", [1, D]), sb("bo", [1, D])
        v, o = sb("v", [P, MT, HEADS, value_slot(16)]), sb("o", [P, TT, D])
        with ExitStack() as early:
            V = {k: early.enter_context(nc.sbuf_tensor(core.named("V" + k), [P, DT, R], F32)) for k in "qkvo"}
            load_stage(core, [
                *[(up[k][:], matrix(w["L1_xattn_U" + k])) for k in "qkvo"], *[(V[k][:], matrix(w["L1_xattn_V" + k])) for k in "qkvo"],
                (bq[:], columned(w["L1_xattn_bq"])), (bk[:], columned(w["L1_xattn_bk"])),
                (bv[:], rowed(w["L1_xattn_bv"])), (bo[:], rowed(w["L1_xattn_bo"])),
            ], zeroed=[v[:]], ones=[v[:, :, :, 16]])

            def turn(k):
                def multiply(bank):
                    for f in range(DT):
                        last = nc.tensor.transpose(bank[:, f * P:(f + 1) * P], V[k][:, f], core.ident[:])
                    return last

                return Job(multiply, "dve", lambda bank: nc.vector.tensor_copy(down[k][:, 0], bank[:, 0:D]))

            product_stage(core, [turn(k) for k in "qkvo"])
        q_parts, k_parts = scratch_for(core, "q_parts", D, S), scratch_for(core, "k_parts", D, M)
        with loop(nc, B) as b:
            take_stage(core, b)
            product_stage(core, turned(core, core.x, core.xT))
            with ExitStack() as early:
                split = Split(core, early, q=(DT, S), k=(DT, M))
                ctxT = early.enter_context(nc.sbuf_tensor(core.named("ctxT"), [P, DT, M], F32))
                low_q, low_k, low_v = (early.enter_context(nc.sbuf_tensor(core.named("low_" + k), [P, 1, S if k == "q" else M], F32)) for k in "qkv")
                context_columns(core, ctx_in, b, ctxT)
                product_stage(core, [*columns_out(core, up["q"], core.xT, low_q, S),
                                     *columns_out(core, up["k"], ctxT, low_k, M), *columns_out(core, up["v"], ctxT, low_v, M)])
                product_stage(core, [*columns_out(core, down["q"], low_q, split.x["q"], S, bias=bq),
                                     *columns_out(core, down["k"], low_k, split.x["k"], M, bias=bk),
                                     *rows_out(core, low_v, down["v"], M, D, values_into(core, v, 16), bias_row=bv[:])])
                split.store(core, q=q_parts, k=k_parts)
            top_attention(core, Heads(k_parts, q_parts, v, o, HEADS, HEADS // 2, 16, M, 0.25, all_blocks(M), top=64))
            with ExitStack() as late:
                oT, low_o = (late.enter_context(nc.sbuf_tensor(core.named(n), [P, k, S], F32)) for n, k in (("oT", DT), ("low_o", 1)))
                product_stage(core, turned(core, o, oT))
                product_stage(core, columns_out(core, up["o"], oT, low_o, S))
                product_stage(core, rows_out(core, low_o, down["o"], S, D, into(core, core.delta), bias_row=bo[:]))
            residual_norm(core, b)


def first_of_equal(nc, step, onehot, values, best, ties, counted, ones):
    rows, n = values.shape[1], values.shape[2]
    step(nc.vector.tensor_tensor(ties, values, best.unsqueeze(2).to_broadcast([values.shape[0], rows, n]), ALU.is_equal))
    for t in range(rows):
        step(nc.vector.tensor_tensor_scan(counted[:, t], ties[:, t], ones, 0.0, ALU.add, ALU.mult))
    step(nc.vector.scalar_tensor_tensor(out=onehot, in0=counted, scalar=1.0, in1=ties, op0=ALU.is_equal, op1=ALU.mult))


def l1_ffn(core, w):
    nc = core.nc
    E, _, H = w["L1_ffn_W1"].shape
    HT = H // P
    with ExitStack() as ctx:
        sb = lambda name, shape: ctx.enter_context(nc.sbuf_tensor(core.named(name), shape, F32))
        wg, bg = sb("wg", [P, DT, E]), sb("bg", [1, E])
        w1, b1 = sb("w1", [P, E, DT, H]), sb("b1", [P, E, HT])
        w2, b2 = sb("w2", [P, E, HT, D]), sb("b2", [E, D])
        load_stage(core, [
            (wg[:], matrix(w["L1_ffn_Wg"])), (bg[:], rowed(w["L1_ffn_bg"])), (b2[:], w["L1_ffn_b2"]),
            *[(w1[:, e], matrix(w["L1_ffn_W1"][e])) for e in range(E)], *[(w2[:, e], matrix(w["L1_ffn_W2"][e])) for e in range(E)],
            *[(b1[:, e], columned(w["L1_ffn_b1"][e])) for e in range(E)]])
        logits, ties, counted = (sb(n, [P, TT, E]) for n in ("logits", "ties", "counted"))
        first, second, mix = (sb(n, [P, TT, E]) for n in ("first", "second", "mix"))
        top1, top2, ratio = (sb(n, [P, TT]) for n in ("top1", "top2", "ratio"))
        mixT, hT = sb("mixT", [E, S]), sb("hT", [P, 2, HT, S])
        with loop(nc, B) as b:
            take_stage(core, b)
            product_stage(core, turned(core, core.x, core.xT))
            product_stage(core, rows_out(core, core.xT, wg, S, E, into(core, logits), bias_row=bg[:]))
            with stage(nc, "dve_step", "gap_ready", "ratio_ready") as (block, dve_step, gap_ready, ratio_ready):
                @block.vector
                def _(dve):
                    step = stepper(dve, dve_step)
                    step(nc.vector.reduce_max(top1[:], logits[:], AX.X))
                    first_of_equal(nc, step, first[:], logits[:], top1[:], ties[:], counted[:], core.ones[:, 0:E])
                    step(nc.vector.scalar_tensor_tensor(out=logits[:], in0=first[:], scalar=MASKED, in1=logits[:], op0=ALU.mult, op1=ALU.add))
                    step(nc.vector.reduce_max(top2[:], logits[:], AX.X))
                    first_of_equal(nc, step, second[:], logits[:], top2[:], ties[:], counted[:], core.ones[:, 0:E])
                    nc.vector.tensor_tensor(ratio[:], top2[:], top1[:], ALU.subtract).then_inc(gap_ready, 1)
                    dve.wait_ge(ratio_ready, 1)
                    step(nc.vector.tensor_scalar(top1[:], ratio[:], 1.0, None, ALU.add))
                    step(nc.vector.reciprocal(top1[:], top1[:]))
                    step(nc.vector.tensor_tensor(top2[:], ratio[:], top1[:], ALU.mult))
                    step(nc.vector.tensor_tensor(first[:], first[:], top1[:].unsqueeze(2).to_broadcast([P, TT, E]), ALU.mult))
                    step(nc.vector.tensor_tensor(second[:], second[:], top2[:].unsqueeze(2).to_broadcast([P, TT, E]), ALU.mult))
                    step(nc.vector.tensor_tensor(mix[:], first[:], second[:], ALU.add))

                @block.scalar
                def _(act):
                    act.wait_ge(gap_ready, 1)
                    nc.scalar.activation(ratio[:], ratio[:], ACT.Exp).then_inc(ratio_ready, 1)

            def turn_mix(bank):
                for t in range(TT):
                    last = nc.tensor.transpose(bank[0:E, t * P:(t + 1) * P], mix[:, t], core.ident[:])
                return last

            product_stage(core, [Job(turn_mix, "dve", out_of_bank(core, "dve", mixT[:]))])
            experts_stage(core, w1, b1, w2, b2, mix, mixT, hT)
            residual_norm(core, b)


def experts_stage(core, w1, b1, w2, b2, mix, mixT, hT):
    nc = core.nc
    E, HT = w1.shape[1], hT.shape[2]
    with stage(nc, "hidden_products", "hidden_ready", "out_products", "summed") as (
            block, hidden_products, hidden_ready, out_products, summed):
        @block.tensor
        def _(pe):
            for t in range(TT):
                nc.tensor.matmul(core.bank(4 + t)[:, 0:D], mixT[:, t * P:(t + 1) * P], b2[:], start=True, stop=True).then_inc(out_products, 1)

            def hidden(e):
                for h in range(HT):
                    if e >= 1:
                        pe.wait_ge(hidden_ready, HT * (e - 1) + h + 1)
                    accumulate(nc, core.bank(h), [(w1[:, e, k, h * P:(h + 1) * P], core.xT[:, k]) for k in range(DT)]
                               ).then_inc(hidden_products, 1)

            def output(e):
                pe.wait_ge(hidden_ready, HT * (e + 1))
                for t in range(TT):
                    pe.wait_ge(summed, TT * e + t + 1)
                    accumulate(nc, core.bank(4 + t)[:, 0:D], [(hT[:, e % 2, h, t * P:(t + 1) * P], w2[:, e, h]) for h in range(HT)]
                               ).then_inc(out_products, 1)

            hidden(0)
            for e in range(E):
                if e + 1 < E:
                    hidden(e + 1)
                output(e)

        @block.scalar
        def _(act):
            for e in range(E):
                for h in range(HT):
                    act.wait_ge(hidden_products, HT * e + h + 1)
                    if e >= 2:
                        act.wait_ge(out_products, TT * e)
                    nc.scalar.activation(hT[:, e % 2, h], core.bank(h), ACT.Gelu, bias=b1[:, e, h:h + 1]).then_inc(hidden_ready, 1)

        @block.vector
        def _(dve):
            for t in range(TT):
                dve.wait_ge(out_products, t + 1)
                nc.vector.tensor_copy(core.delta[:, t], core.bank(4 + t)[:, 0:D]).then_inc(summed, 1)
            for e in range(E):
                for t in range(TT):
                    dve.wait_ge(out_products, TT * (e + 1) + t + 1)
                    dve.wait_ge(summed, TT * e + t + 1)
                    nc.vector.scalar_tensor_tensor(out=core.delta[:, t], in0=core.bank(4 + t)[:, 0:D], scalar=mix[:, t, e:e + 1],
                                                   in1=core.delta[:, t], op0=ALU.mult, op1=ALU.add).then_inc(summed, 1)


def l2_attn(core, w):
    nc = core.nc
    NS = w["L2_attn_B"].shape[0]
    K = 9
    TWO_PI_HI, TWO_PI_MID, TWO_PI_LO = 6.28125, 0.0019350051879882812, 3.0199159819567e-07
    with ExitStack() as ctx:
        sb = lambda name, shape: ctx.enter_context(nc.sbuf_tensor(core.named(name), shape, F32))
        cosT, sinT, drive, decay = (sb(n, [P, S]) for n in ("cosT", "sinT", "drive", "decay"))
        inT, outP, outQ = sb("inT", [P, DT, P]), sb("outP", [P, D]), sb("outQ", [P, D])
        skip = sb("skip", [P, D])
        with ExitStack() as early:
            eb = lambda name, shape: early.enter_context(nc.sbuf_tensor(core.named(name), shape, F32))
            lar, aim, ls = eb("lar", [P, 1]), eb("aim", [P, 1]), eb("ls", [P, 1])
            b_rows, c_rows, c_sorted = eb("b_rows", [NS, D]), eb("c_rows", [P, DT, NS, 2]), eb("c_sorted", [P, DT, 2, P])
            la, ai = w["L2_attn_log_A_real"].rearrange("(n o) -> n o", o=1), w["L2_attn_A_imag"].rearrange("(n o) -> n o", o=1)
            load_stage(core, [
                (lar[0:NS], la), (lar[NS:P], la), (aim[0:NS], ai), (aim[NS:P], ai), (ls[:], spread_over(w["L2_attn_log_step"])),
                (b_rows[:], w["L2_attn_B"]), (skip[:], spread_over(w["L2_attn_D"])),
                *[(c_rows[:, t], w["L2_attn_C"][t * P:(t + 1) * P]) for t in range(DT)]])
            dt_, are, r, angle, turns, half = eb("dt", [P, 1]), eb("are", [P, 1]), eb("r", [P, 1]), eb("angle", [P, K]), eb("turns", [P, K]), eb("half", [P, K])
            cosK, sinK = eb("cosK", [P, K]), eb("sinK", [P, K])
            nr, ni, den, cr, ci, t0, ga, gb = (eb(n, [P, 1]) for n in ("nr", "ni", "den", "cr", "ci", "t0", "ga", "gb"))
            tmp = eb("tmp", [P, S])
            with stage(nc, "dve_step", "act_step", "product_ready", "angle_ready", "sines_ready") as (
                    block, dve_step, act_step, product_ready, angle_ready, sines_ready):
                @block.scalar
                def _(act):
                    step = stepper(act, act_step)
                    step(nc.scalar.activation(dt_[:], ls[:], ACT.Exp))
                    step(nc.scalar.activation(are[:], lar[:], ACT.Exp))
                    act.wait_ge(product_ready, 1)
                    nc.scalar.activation(r[:], r[:], ACT.Exp).then_inc(sines_ready, 1)
                    act.wait_ge(angle_ready, 1)
                    nc.scalar.activation(sinK[:], angle[:], ACT.Sin).then_inc(sines_ready, 1)
                    nc.scalar.activation(half[:], half[:], ACT.Sin).then_inc(sines_ready, 1)

                @block.vector
                def _(dve):
                    v = nc.vector
                    step = stepper(dve, dve_step)
                    dve.wait_ge(act_step, 2)
                    step(v.tensor_scalar(are[:], are[:], -1.0, None, ALU.mult))
                    v.tensor_tensor(r[:], are[:], dt_[:], ALU.mult).then_inc(product_ready, 1)
                    step(v.tensor_tensor(angle[:, 0:1], aim[:], dt_[:], ALU.mult))
                    for k in range(1, K):
                        step(v.tensor_scalar(angle[:, k:k + 1], angle[:, k - 1:k], 2.0, None, ALU.mult))
                    step(v.tensor_scalar(turns[:], angle[:], 0.15915494309189535, None, ALU.mult))
                    step(v.tensor_scalar(turns[:], turns[:], ROUND, None, ALU.add))
                    step(v.tensor_scalar(turns[:], turns[:], ROUND, None, ALU.subtract))
                    for part in (TWO_PI_HI, TWO_PI_MID, TWO_PI_LO):
                        step(v.scalar_tensor_tensor(out=angle[:], in0=turns[:], scalar=-part, in1=angle[:], op0=ALU.mult, op1=ALU.add))
                    step(v.tensor_scalar(angle[:], angle[:], -3.1415925, 3.1415925, ALU.max, ALU.min))
                    v.tensor_scalar(half[:], angle[:], 0.5, None, ALU.mult).then_inc(angle_ready, 1)
                    dve.wait_ge(sines_ready, 3)
                    step(v.tensor_tensor(cosK[:], half[:], half[:], ALU.mult))
                    step(v.tensor_scalar(cosK[:], cosK[:], -2.0, 1.0, ALU.mult, ALU.add))
                    step(v.tensor_tensor(nr[:], r[:], cosK[:, 0:1], ALU.mult))
                    step(v.tensor_scalar(nr[:], nr[:], -1.0, None, ALU.add))
                    step(v.tensor_tensor(ni[:], r[:], sinK[:, 0:1], ALU.mult))
                    step(v.tensor_tensor(den[:], are[:], are[:], ALU.mult))
                    step(v.tensor_tensor(t0[:], aim[:], aim[:], ALU.mult))
                    step(v.tensor_tensor(den[:], den[:], t0[:], ALU.add))
                    step(v.reciprocal(den[:], den[:]))
                    step(v.tensor_tensor(cr[:], nr[:], are[:], ALU.mult))
                    step(v.scalar_tensor_tensor(out=cr[:], in0=ni[:], scalar=aim[:, 0:1], in1=cr[:], op0=ALU.mult, op1=ALU.add))
                    step(v.tensor_tensor(cr[:], cr[:], den[:], ALU.mult))
                    step(v.tensor_tensor(t0[:], nr[:], aim[:], ALU.mult))
                    step(v.scalar_tensor_tensor(out=ci[:], in0=ni[:], scalar=are[:, 0:1], in1=t0[:], op0=ALU.mult, op1=ALU.subtract))
                    step(v.tensor_tensor(ci[:], ci[:], den[:], ALU.mult))
                    step(v.memset(cosT[:, 0:1], 1.0))
                    step(v.memset(sinT[:, 0:1], 0.0))
                    for k in range(K):
                        n = 1 << k
                        for to, a, bb, op in ((cosT, cosT, sinT, ALU.subtract), (sinT, sinT, cosT, ALU.add)):
                            step(v.tensor_scalar(tmp[:, 0:n], bb[:, 0:n], sinK[:, k:k + 1], None, ALU.mult))
                            step(v.scalar_tensor_tensor(out=to[:, n:2 * n], in0=a[:, 0:n], scalar=cosK[:, k:k + 1], in1=tmp[:, 0:n],
                                                        op0=ALU.mult, op1=op))
                    step(v.tensor_copy(ga[0:NS], cr[0:NS]))
                    step(v.tensor_copy(ga[NS:P], ci[NS:P]))
                    step(v.tensor_copy(gb[0:NS], ci[0:NS]))
                    step(v.tensor_scalar(gb[NS:P], cr[NS:P], -1.0, None, ALU.mult))
                    step(v.tensor_scalar(tmp[:], sinT[:], gb[:, 0:1], None, ALU.mult))
                    step(v.scalar_tensor_tensor(out=drive[:], in0=cosT[:], scalar=ga[:, 0:1], in1=tmp[:], op0=ALU.mult, op1=ALU.add))
                    step(v.tensor_scalar(decay[:], core.ones[:], r[:, 0:1], None, ALU.mult))
                    for t in range(DT):
                        step(v.tensor_copy(c_sorted[:, t, 0, 0:NS], c_rows[:, t, :, 0]))
                        step(v.tensor_scalar(c_sorted[:, t, 0, NS:P], c_rows[:, t, :, 1], -1.0, None, ALU.mult))
                        step(v.tensor_scalar(c_sorted[:, t, 1, 0:NS], c_rows[:, t, :, 1], -1.0, None, ALU.mult))
                        step(v.tensor_scalar(c_sorted[:, t, 1, NS:P], c_rows[:, t, :, 0], -1.0, None, ALU.mult))

            def turn_b(bank):
                for f in range(DT):
                    for half_ in range(2):
                        last = nc.tensor.transpose(bank[:, f * P + half_ * NS:f * P + half_ * NS + NS], b_rows[:, f * P:(f + 1) * P], core.ident[0:NS, 0:NS])
                return last

            def turn_c(i):
                def multiply(bank):
                    for t in range(DT):
                        last = nc.tensor.transpose(bank[:, t * P:(t + 1) * P], c_sorted[:, t, i], core.ident[:])
                    return last
                return multiply

            product_stage(core, [Job(turn_b, "dve", out_of_bank(core, "dve", inT[:].rearrange("p k n -> p (k n)"))),
                                 Job(turn_c(0), "act", out_of_bank(core, "act", outP[:])), Job(turn_c(1), "dve", out_of_bank(core, "dve", outQ[:]))])
        z, zc, zs = sb("z", [P, S]), sb("zc", [P, S]), sb("zs", [P, S])
        with loop(nc, B) as b:
            take_stage(core, b)
            product_stage(core, turned(core, core.x, core.xT))
            with stage(nc, "drive_product", "dve_step", "state_ready", "out_products") as (
                    block, drive_product, dve_step, state_ready, out_products):
                @block.tensor
                def _(pe):
                    accumulate(nc, core.bank(0), [(inT[:, k], core.xT[:, k]) for k in range(DT)]).then_inc(drive_product, 1)
                    pe.wait_ge(state_ready, 1)
                    for t in range(TT):
                        cut = slice(t * P, (t + 1) * P)
                        accumulate(nc, core.bank(1 + t)[:, 0:D], [(zc[:, cut], outP[:]), (zs[:, cut], outQ[:])]).then_inc(out_products, 1)

                @block.vector
                def _(dve):
                    v = nc.vector
                    step = stepper(dve, dve_step)
                    dve.wait_ge(drive_product, 1)
                    step(v.tensor_tensor(zc[:], core.bank(0), drive[:], ALU.mult))
                    step(v.tensor_tensor_scan(z[:], decay[:], zc[:], 0.0, ALU.mult, ALU.add))
                    step(v.tensor_tensor(zc[:], z[:], cosT[:], ALU.mult))
                    v.tensor_tensor(zs[:], z[:], sinT[:], ALU.mult).then_inc(state_ready, 1)
                    for t in range(TT):
                        step(v.tensor_tensor(core.delta[:, t], core.x[:, t], skip[:], ALU.mult))
                    for t in range(TT):
                        dve.wait_ge(out_products, t + 1)
                        step(v.tensor_tensor(core.delta[:, t], core.bank(1 + t)[:, 0:D], core.delta[:, t], ALU.add))
            residual_norm(core, b)


def turn_square(core, source, to, rows_tiles, cols_tiles):
    nc = core.nc
    jobs = []
    for c in range(cols_tiles):
        def multiply(bank, c=c):
            for r in range(rows_tiles):
                last = nc.tensor.transpose(bank[:, r * P:(r + 1) * P], source[:, r, c * P:(c + 1) * P], core.ident[:])
            return last
        jobs.append(Job(multiply, "dve", out_of_bank(core, "dve", to[:, c, 0:rows_tiles * P])))
    return jobs


def l2_xattn(core, w, ctx_in):
    nc = core.nc
    with ExitStack() as ctx:
        sb = lambda name, shape: ctx.enter_context(nc.sbuf_tensor(core.named(name), shape, F32))
        wr, wT, bias = sb("wr", [P, DT, 2 * D]), sb("wT", [P, 2 * DT, D]), sb("bias", [1, D])
        load_stage(core, [(wr[:], matrix(w["L2_xattn_W"])), (bias[:], rowed(w["L2_xattn_b"]))])
        product_stage(core, turn_square(core, wr, wT, DT, 2 * DT))
        rows, mean, pooled = sb("rows", [P, MT, D]), sb("mean", [P, DT]), sb("pooled", [1, D])
        with loop(nc, B) as b:
            take_stage(core, b)
            context_load(core, ctx_in, b, rows)

            def sums(bank):
                for f in range(DT):
                    last = accumulate(nc, bank[:, f:f + 1], [(rows[0:kt_rows(M, t), t, f * P:(f + 1) * P], core.ones[0:kt_rows(M, t), 0:1]) for t in range(MT)])
                return last

            product_stage(core, [*turned(core, core.x, core.xT), Job(sums, "dve", lambda bank: nc.vector.tensor_scalar(
                mean[:], bank[:, 0:DT], 1.0 / M, None, ALU.mult))])
            product_stage(core, [Job(lambda bank: accumulate(nc, bank[0:1, 0:D], [(mean[:, k:k + 1], wT[:, DT + k]) for k in range(DT)]), "dve",
                                     lambda bank: nc.vector.tensor_tensor(pooled[:], bank[0:1, 0:D], bias[:], ALU.add))])
            product_stage(core, rows_out(core, core.xT, wT[:, 0:DT], S, D, into(core, core.delta), bias_row=pooled[:]))
            residual_norm(core, b)


def l2_ffn(core, w):
    nc = core.nc
    E, _, R = w["L2_ffn_down_W"].shape
    with ExitStack() as ctx:
        sb = lambda name, shape: ctx.enter_context(nc.sbuf_tensor(core.named(name), shape, F32))
        base, baseT, base_b = sb("base", [P, DT, D]), sb("baseT", [P, DT, D]), sb("base_b", [1, D])
        mu, iv, muiv, mu2iv = (sb(n, [P, DT, E]) for n in ("mu", "iv", "muiv", "mu2iv"))
        down, up, conv = sb("down", [P, E, DT, R]), sb("up", [R, E, D]), sb("conv", [P, E, DT, D])
        down_b, up_b, conv_b = sb("down_b", [E, R]), sb("up_b", [E, D]), sb("conv_b", [E, D])
        by_feature = lambda v: v.rearrange("e (k p) -> p k e", p=P)
        with nc.allow_non_contiguous_dma("small tables of the experts' statistics"):
            load_stage(core, [
                (base[:], matrix(w["L2_ffn_base_W"])), (base_b[:], rowed(w["L2_ffn_base_b"])),
                *[(mu[:, k], by_feature(w["L2_ffn_disc_mu"])[:, k]) for k in range(DT)],
                *[(iv[:, k], by_feature(w["L2_ffn_disc_sigma"])[:, k]) for k in range(DT)],
                *[(down[:, e], matrix(w["L2_ffn_down_W"][e])) for e in range(E)], (up[:], w["L2_ffn_up_W"].rearrange("e r d -> r e d")),
                *[(conv[:, e], matrix(w["L2_ffn_conv_W"][e])) for e in range(E)],
                (down_b[:], w["L2_ffn_down_b"]), (up_b[:], w["L2_ffn_up_b"]), (conv_b[:], w["L2_ffn_conv_b"])])
        with stage(nc, "dve_step") as (block, dve_step):
            @block.vector
            def _(dve):
                v = nc.vector
                step = stepper(dve, dve_step)
                step(v.tensor_tensor(iv[:], iv[:], iv[:], ALU.mult))
                step(v.reciprocal(iv[:], iv[:]))
                step(v.tensor_tensor(muiv[:], mu[:], iv[:], ALU.mult))
                step(v.tensor_tensor(mu2iv[:], mu[:], muiv[:], ALU.mult))
                step(v.tensor_scalar(muiv[:], muiv[:], -2.0, None, ALU.mult))
        product_stage(core, turn_square(core, base, baseT, DT, DT))
        m1, m2, square = sb("m1", [P, DT]), sb("m2", [P, DT]), sb("square", [P, DT, S])
        loss, least, ties, counted, pick = sb("loss", [1, 1, E]), sb("least", [1, 1]), sb("ties", [1, 1, E]), sb("counted", [1, 1, E]), sb("pick", [1, 1, E])
        everywhere, picked = sb("everywhere", [P, E]), sb("picked", [E, 1])
        wd, wu, wc, wcT = sb("wd", [P, DT, R]), sb("wu", [R, 1, D]), sb("wc", [P, DT, D]), sb("wcT", [P, DT, D])
        bd, bu, bc = sb("bd", [R, 1]), sb("bu", [P, DT]), sb("bc", [1, D])
        hT, aT = sb("hT", [R, 1, S]), sb("aT", [P, DT, S])
        with loop(nc, B) as b:
            take_stage(core, b)
            product_stage(core, turned(core, core.x, core.xT))
            with stage(nc, "dve_step", "act_step") as (block, dve_step, act_step):
                @block.vector
                def _(dve):
                    step = stepper(dve, dve_step)
                    step(nc.vector.reduce_sum(m1[:], core.xT[:], AX.X))
                    step(nc.vector.tensor_scalar(m1[:], m1[:], 1.0 / S, None, ALU.mult))
                    dve.wait_ge(act_step, DT)
                    step(nc.vector.tensor_scalar(m2[:], m2[:], 1.0 / S, None, ALU.mult))

                @block.scalar
                def _(act):
                    step = stepper(act, act_step)
                    for f in range(DT):
                        step(nc.scalar.activation(square[:, f], core.xT[:, f], ACT.Square, accum_out=m2[:, f:f + 1]))

            def losses(bank):
                terms = []
                for k in range(DT):
                    terms += [(m2[:, k:k + 1], iv[:, k]), (m1[:, k:k + 1], muiv[:, k]), (core.ones[:, 0:1], mu2iv[:, k])]
                return accumulate(nc, bank[0:1, 0:E], terms)

            product_stage(core, [Job(losses, "dve", lambda bank: nc.vector.tensor_scalar(loss[:, 0], bank[0:1, 0:E], -1.0 / D, None, ALU.mult))])
            with stage(nc, "dve_step") as (block, dve_step):
                @block.vector
                def _(dve):
                    step = stepper(dve, dve_step)
                    step(nc.vector.reduce_max(least[:], loss[:], AX.X))
                    first_of_equal(nc, step, pick[:], loss[:], least[:], ties[:], counted[:], core.ones[0:1, 0:E])
            product_stage(core, [
                Job(lambda bank: nc.tensor.matmul(bank[:, 0:E], core.ones[0:1, 0:P], pick[:, 0], start=True, stop=True), "dve",
                    out_of_bank(core, "dve", everywhere[:])),
                Job(lambda bank: nc.tensor.matmul(bank[0:E, 0:1], pick[:, 0], core.ones[0:1, 0:1], start=True, stop=True), "dve",
                    out_of_bank(core, "dve", picked[:]))])
            with stage(nc, "dve_step") as (block, dve_step):
                @block.vector
                def _(dve):
                    step = stepper(dve, dve_step)
                    for e in range(E):
                        for to, of, p in ((wd[:], down[:, e], P), (wu[:, 0], up[:, e], R), (wc[:], conv[:, e], P)):
                            if e == 0:
                                step(nc.vector.tensor_scalar(to, of, everywhere[0:p, 0:1], None, ALU.mult))
                            else:
                                step(nc.vector.scalar_tensor_tensor(out=to, in0=of, scalar=everywhere[0:p, e:e + 1], in1=to, op0=ALU.mult, op1=ALU.add))

            def column(bias, cut, rows):
                return lambda bank: nc.tensor.matmul(bank[0:rows, 0:1], bias[:, cut], picked[:], start=True, stop=True)

            product_stage(core, [
                *turn_square(core, wc, wcT, DT, DT),
                Job(column(down_b, slice(0, R), R), "dve", out_of_bank(core, "dve", bd[:])),
                *[Job(column(up_b, slice(f * P, (f + 1) * P), P), "dve", out_of_bank(core, "dve", bu[:, f:f + 1])) for f in range(DT)],
                Job(lambda bank: nc.tensor.matmul(bank[0:1, 0:D], picked[:], conv_b[:], start=True, stop=True), "dve", out_of_bank(core, "dve", bc[:]))])
            product_stage(core, columns_out(core, wd, core.xT, hT, S, m=R, bias=bd, func=ACT.Relu, engines=("act",)))
            product_stage(core, columns_out(core, wu, hT, aT, S, bias=bu))

            def both(t):
                cut = slice(t * P, (t + 1) * P)
                terms = [(core.xT[:, k, cut], baseT[:, k]) for k in range(DT)] + [(aT[:, k, cut], wcT[:, k]) for k in range(DT)]
                terms += [(core.ones[0:1, 0:P], base_b[:]), (core.ones[0:1, 0:P], bc[:])]
                return lambda bank: accumulate(nc, bank[:, 0:D], terms)

            product_stage(core, [Job(both(t), *into(core, core.delta)(t)) for t in range(TT)])
            residual_norm(core, b)


def l3_attn(core, w):
    nc = core.nc
    L, CH, HD = 64, S // 64, 16
    with ExitStack() as ctx:
        sb = lambda name, shape: ctx.enter_context(nc.sbuf_tensor(core.named(name), shape, F32))
        wq, wk, wv = sb("wq", [P, DT, D]), sb("wk", [P, DT, D]), sb("wv", [P, DT, D])
        bq, bk, bv = sb("bq", [P, DT]), sb("bk", [P, DT]), sb("bv", [1, D])
        rq, rk, rv = sb("rq", [P, DT, L]), sb("rk", [P, DT, L]), sb("rv", [P, DT, L])
        rbq, rbk, rbv = sb("rbq", [L, 1]), sb("rbk", [L, 1]), sb("rbv", [1, L])
        v, rvr = sb("v", [P, TT, HEADS, value_slot(HD)]), sb("rvr", [L, 1, L // HD, value_slot(HD)])
        q_parts, k_parts = scratch_for(core, "q_parts", D, S), scratch_for(core, "k_parts", D, S)
        rq_parts, rk_parts = scratch_for(core, "rq_parts", L, S), scratch_for(core, "rk_parts", L, L)
        rout, rout_b = sb("rout", [L, 1, D]), sb("rout_b", [1, D])
        wo, bo = sb("wo", [P, DT, D]), sb("bo", [1, D])
        gl, gr = sb("gl", [P, HD]), sb("gr", [P, HD])
        some_key, some_chunk = sb("some_key", [P, TT]), sb("some_chunk", [P, TT])
        sb16 = lambda name, shape: ctx.enter_context(nc.sbuf_tensor(core.named(name), shape, BF16))
        before16, after16, chunks16 = sb16("before16", [P, P]), sb16("after16", [P, P]), sb16("chunks16", [P, TT, L])
        beforeT16, afterT16, chunksT16 = sb16("beforeT16", [P, P]), sb16("afterT16", [P, P]), sb16("chunksT16", [L, TT, P])
        qkv, qkv_b = w["L3_attn_qkv_w"], w["L3_attn_qkv_b"]
        load_stage(core, [
            (wq[:], matrix(qkv[:, 0:D])), (wk[:], matrix(qkv[:, D:2 * D])), (wv[:], matrix(qkv[:, 2 * D:3 * D])),
            (bq[:], columned(qkv_b[0:D])), (bk[:], columned(qkv_b[D:2 * D])), (bv[:], rowed(qkv_b[2 * D:3 * D])),
            (rq[:], matrix(w["L3_attn_rq_w"])), (rk[:], matrix(w["L3_attn_rkv_w"][:, 0:L])), (rv[:], matrix(w["L3_attn_rkv_w"][:, L:2 * L])),
            (rbq[:], columned(w["L3_attn_rq_b"], L)), (rbk[:], columned(w["L3_attn_rkv_b"][0:L], L)), (rbv[:], rowed(w["L3_attn_rkv_b"][L:2 * L])),
            (rout[:], matrix(w["L3_attn_rout_w"], L)), (rout_b[:], rowed(w["L3_attn_rout_b"])),
            (wo[:], matrix(w["L3_attn_out_w"])), (bo[:], rowed(w["L3_attn_out_b"])),
            (gl[:], spread_over(w["L3_attn_gl_w"].rearrange("a b -> (a b)"))), (gr[:], spread_over(w["L3_attn_gr_w"].rearrange("a b -> (a b)"))),
        ], zeroed=[v[:], rvr[:]], ones=[v[:, :, :, HD], rvr[:, :, :, HD]])
        with ExitStack() as early:
            eb = lambda name, shape: early.enter_context(nc.sbuf_tensor(core.named(name), shape, F32))
            square, chunks, chunksT = eb("square", [P, 4, P]), eb("chunks", [P, TT, L]), eb("chunksT", [L, TT, P])
            with stage(nc, "filled") as (block, filled):
                @block.gpsimd
                def _(pool):
                    for t, value in ((some_key, 1.0), (some_chunk, 1.0), (square, 0.0), (chunks, 0.0), (chunksT, 0.0)):
                        pool.memset(t[:], value).then_inc(filled, 1)
                    pool.wait_ge(filled, 5)
                    triangle(pool, square[:, 0], ALU.is_gt, 1).then_inc(filled, 1)
                    triangle(pool, square[:, 1], ALU.is_ge, -1).then_inc(filled, 1)
                    triangle(pool, square[:, 2], ALU.is_gt, -1).then_inc(filled, 1)
                    triangle(pool, square[:, 3], ALU.is_ge, 1).then_inc(filled, 1)
                    for q in range(TT):
                        pool.affine_select(out=chunks[:, q], in_=chunks[:, q], compare_op=ALU.is_ge, fill=MASKED, base=q * P - CH, pattern=[[-CH, L]], channel_multiplier=1).then_inc(filled, 1)
                        pool.affine_select(out=chunksT[:, q], in_=chunksT[:, q], compare_op=ALU.is_ge, fill=MASKED, base=q * P - CH, pattern=[[1, P]], channel_multiplier=-CH).then_inc(filled, 1)
                    pool.affine_select(out=some_key[:, 0:1], in_=some_key[:, 0:1], compare_op=ALU.is_gt, fill=0.0, base=0, pattern=[[0, 1]], channel_multiplier=1).then_inc(filled, 1)
                    pool.affine_select(out=some_chunk[:, 0:1], in_=some_chunk[:, 0:1], compare_op=ALU.is_ge, fill=0.0, base=-CH, pattern=[[0, 1]], channel_multiplier=1).then_inc(filled, 1)
                    pool.wait_ge(filled, 11 + 2 * TT)
                    for to, of in ((before16, square[:, 0]), (after16, square[:, 1]), (beforeT16, square[:, 2]), (afterT16, square[:, 3]),
                                   (chunks16, chunks[:]), (chunksT16, chunksT[:])):
                        pool.tensor_copy(to[:], of).then_inc(filled, 1)
                    pool.wait_ge(filled, 17 + 2 * TT)

        def local_blocks(q):
            return ([(q - 1, after16[:], afterT16[:])] if q else []) + [(q, before16[:], beforeT16[:])]

        o, oT, pooledT = sb("o", [P, TT, D]), sb("oT", [P, DT, S]), sb("pooledT", [P, DT, L])
        lat, latT, remote = sb("lat", [P, TT, L]), sb("latT", [L, 1, S]), sb("remote", [P, TT, D])
        gated, gate, gate2 = sb("gated", [P, TT * 16, HD]), sb("gate", [P, TT * 16]), sb("gate2", [P, TT * 16])
        local = Heads(k_parts, q_parts, v, o, HEADS, HEADS, HD, S, 0.25, local_blocks, valid=some_key, lag=4.0)
        local_buffers = attention_buffers(core, ctx, local)
        remote_heads = Heads(rk_parts, rq_parts, rvr, lat, L // HD, 4, HD, L, 0.25, lambda q: [(0, chunks16[:, q], chunksT16[:, q])], valid=some_chunk)
        remote_heads_buffers = attention_buffers(core, ctx, remote_heads)
        with loop(nc, B) as b:
            take_stage(core, b)
            product_stage(core, turned(core, core.x, core.xT))
            with stage(nc, "dve_step") as (block, dve_step):
                @block.vector
                def _(dve):
                    step = stepper(dve, dve_step)
                    for k in range(DT):
                        step(nc.vector.reduce_sum(pooledT[:, k], core.xT[:, k].rearrange("p (l c) -> p l c", c=CH), AX.X))
                    step(nc.vector.tensor_scalar(pooledT[:], pooledT[:], 1.0 / CH, None, ALU.mult))
            with ExitStack() as early:
                split = Split(core, early, q=(DT, S), k=(DT, S), rq=(1, S), rk=(1, L))
                product_stage(core, [
                    *columns_out(core, wq, core.xT, split.x["q"], S, bias=bq), *columns_out(core, wk, core.xT, split.x["k"], S, bias=bk),
                    *rows_out(core, core.xT, wv, S, D, values_into(core, v, HD), bias_row=bv[:]),
                    *columns_out(core, rq, core.xT, split.x["rq"], S, m=L, bias=rbq), *columns_out(core, rk, pooledT, split.x["rk"], L, m=L, bias=rbk),
                    *rows_out(core, pooledT, rv, L, L, values_into(core, rvr, HD), bias_row=rbv[:])])
                split.store(core, q=q_parts, k=k_parts, rq=rq_parts, rk=rk_parts)
            attention(core, local, local_buffers)
            attention(core, remote_heads, remote_heads_buffers)

            def turn_lat(bank):
                for t in range(TT):
                    last = nc.tensor.transpose(bank[0:L, t * P:(t + 1) * P], lat[:, t], core.ident[:])
                return last

            product_stage(core, [Job(turn_lat, "dve", out_of_bank(core, "dve", latT[:, 0]))])
            product_stage(core, rows_out(core, latT, rout, S, D, into(core, remote), bias_row=rout_b[:]))
            with stage(nc, "dve_step", "logit_ready", "gate_ready") as (block, dve_step, logit_ready, gate_ready):
                by_head = lambda t: t[:].rearrange("p t (h s) -> p (t h) s", s=HD)
                wide = lambda t: t[:].unsqueeze(1).to_broadcast([P, TT * 16, HD])

                @block.vector
                def _(dve):
                    v_ = nc.vector
                    step = stepper(dve, dve_step)
                    step(v_.tensor_tensor(gated[:], by_head(o), wide(gl), ALU.mult))
                    step(v_.reduce_sum(gate[:], gated[:], AX.X))
                    step(v_.tensor_tensor(gated[:], by_head(remote), wide(gr), ALU.mult))
                    step(v_.reduce_sum(gate2[:], gated[:], AX.X))
                    v_.tensor_tensor(gate[:], gate[:], gate2[:], ALU.add).then_inc(logit_ready, 1)
                    step(v_.tensor_tensor(gated[:], by_head(o), by_head(remote), ALU.subtract))
                    dve.wait_ge(gate_ready, 1)
                    step(v_.tensor_tensor(gated[:], gated[:], gate[:].unsqueeze(2).to_broadcast([P, TT * 16, HD]), ALU.mult))
                    step(v_.tensor_tensor(by_head(o), gated[:], by_head(remote), ALU.add))

                @block.scalar
                def _(act):
                    act.wait_ge(logit_ready, 1)
                    nc.scalar.activation(gate[:], gate[:], ACT.Sigmoid).then_inc(gate_ready, 1)
            product_stage(core, turned(core, o, oT))
            product_stage(core, rows_out(core, oT, wo, S, D, into(core, core.delta), bias_row=bo[:]))
            residual_norm(core, b)


def l3_xattn(core, w, ctx_in):
    nc = core.nc
    with ExitStack() as ctx:
        sb = lambda name, shape: ctx.enter_context(nc.sbuf_tensor(core.named(name), shape, F32))
        wq, wk, wv = sb("wq", [P, DT, D]), sb("wk", [P, DT, D]), sb("wv", [P, DT, D])
        bq, bk, bv = sb("bq", [P, DT]), sb("bk", [P, DT]), sb("bv", [1, D])
        wo, bo = sb("wo", [P, DT, D]), sb("bo", [1, D])
        v = sb("v", [P, MT, HEADS, value_slot(D // HEADS)])
        q_parts, k_parts = scratch_for(core, "q_parts", D, S), scratch_for(core, "k_parts", D, M)
        load_stage(core, [
            (wq[:], matrix(w["L3_xattn_Wq"])), (wk[:], matrix(w["L3_xattn_Wk"])), (wv[:], matrix(w["L3_xattn_Wv"])),
            (bq[:], columned(w["L3_xattn_bq"])), (bk[:], columned(w["L3_xattn_bk"])), (bv[:], rowed(w["L3_xattn_bv"])),
            (wo[:], matrix(w["L3_xattn_Wo"])), (bo[:], rowed(w["L3_xattn_bo"])),
        ], zeroed=[v[:]], ones=[v[:, :, :, 16]])
        o, oT = sb("o", [P, TT, D]), sb("oT", [P, DT, S])
        heads = Heads(k_parts, q_parts, v, o, HEADS, HEADS, 16, M, 0.25, all_blocks(M))
        heads_buffers = attention_buffers(core, ctx, heads)
        with loop(nc, B) as b:
            take_stage(core, b)
            product_stage(core, turned(core, core.x, core.xT))
            with ExitStack() as early:
                ctxT = early.enter_context(nc.sbuf_tensor(core.named("ctxT"), [P, DT, M], F32))
                context_columns(core, ctx_in, b, ctxT)
                split = Split(core, early, q=(DT, S), k=(DT, M))
                product_stage(core, [
                    *columns_out(core, wq, core.xT, split.x["q"], S, bias=bq), *columns_out(core, wk, ctxT, split.x["k"], M, bias=bk),
                    *rows_out(core, ctxT, wv, M, D, values_into(core, v, 16), bias_row=bv[:])])
                split.store(core, q=q_parts, k=k_parts)
            attention(core, heads, heads_buffers)
            product_stage(core, turned(core, o, oT))
            product_stage(core, rows_out(core, oT, wo, S, D, into(core, core.delta), bias_row=bo[:]))
            residual_norm(core, b)


def l3_ffn(core, w):
    nc = core.nc
    FF = w["L3_ffn_w1"].shape[1]
    with ExitStack() as ctx:
        sb = lambda name, shape: ctx.enter_context(nc.sbuf_tensor(core.named(name), shape, F32))
        w1, b1 = sb("w1", [P, DT, FF]), sb("b1", [P, FF // P])
        w2, b2 = sb("w2", [P, FF // P, D]), sb("b2", [1, D])
        load_stage(core, [(w1[:], matrix(w["L3_ffn_w1"])), (b1[:], columned(w["L3_ffn_b1"])),
                          (w2[:], matrix(w["L3_ffn_w2"])), (b2[:], rowed(w["L3_ffn_b2"]))])
        hT = sb("hT", [P, FF // P, S])
        with loop(nc, B) as b:
            take_stage(core, b)
            product_stage(core, turned(core, core.x, core.xT))
            product_stage(core, columns_out(core, w1, core.xT, hT, S, bias=b1, func=ACT.Gelu, engines=("act",)))
            product_stage(core, rows_out(core, hT, w2, S, D, into(core, core.delta), bias_row=b2[:]))
            residual_norm(core, b)


def decoder(nc, w, out, layers=range(12)):
    with ExitStack() as ctx:
        core = Core(nc, ctx)
        constants_stage(core, w["x"])
        context = w["ctx_1024"]
        sublayers = [lambda: l0_attn(core, w), lambda: l0_xattn(core, w, context), lambda: l0_ffn(core, w),
                     lambda: l1_attn(core, w), lambda: l1_xattn(core, w, context), lambda: l1_ffn(core, w),
                     lambda: l2_attn(core, w), lambda: l2_xattn(core, w, context), lambda: l2_ffn(core, w),
                     lambda: l3_attn(core, w), lambda: l3_xattn(core, w, context), lambda: l3_ffn(core, w)]
        for n in layers:
            core.sublayer = f"l{n // 3}_{n % 3}"
            sublayers[n]()
        with stage(nc, "stored") as (block, stored):
            @block.sync
            def _(sp):
                for b in range(B):
                    sp.dma_start(out[b].rearrange("(t p) d -> p t d", p=P), core.x_all[:, b]).then_inc(stored, 16)
                sp.wait_ge(stored, 16 * B)


def kernel(**inputs):
    import numpy as _np
    import concourse.bacc as _bacc
    from concourse import mybir as _mybir
    from concourse.bass_utils import run_bass_kernel_spmd as _run

    nc = _bacc.Bacc("TRN2", target_bir_lowering=False, num_devices=1)
    arrays, args = {}, {}
    for name, value in inputs.items():
        a = _np.ascontiguousarray(value)
        arrays[name + "_dram"] = a
        args[name] = nc.dram_tensor(name + "_dram", a.shape, _mybir.dt.from_np(a.dtype), kind="ExternalInput").ap()
    out = nc.dram_tensor("out_dram", (B, S, D), F32, kind="ExternalOutput").ap()
    decoder(nc, args, out)
    return _run(nc, [arrays], core_ids=[0]).results[0]["out_dram"]
```

```python
from contextlib import ExitStack, contextmanager
from dataclasses import dataclass, replace

import concourse.bass as bass
from concourse import mybir

F32 = mybir.dt.float32
BF16 = mybir.dt.bfloat16
I32 = mybir.dt.int32
ALU = mybir.AluOpType
ACT = mybir.ActivationFunctionType
AX = mybir.AxisListType

P = 128
B, S, D = 4, 512, 256
M = 1601
TT = S // P
DT = D // P
MT = (M + P - 1) // P
BANK = 512
BANKS = 8
EPS = 1e-5
MASKED = -1e30
TAKEN = -3e38
ROUND = 12582912.0


def kt_rows(n, t):
    return min(P, n - t * P)


used = []


@contextmanager
def stage(nc, *signals):
    with ExitStack() as held:
        last, used[:] = used[:], []
        turn = 1 - last[0][0] if last else 0
        sems = [held.enter_context(nc.semaphore(f"{s}_{turn}")) for s in signals]
        with nc.Block() as block:
            @block.sync
            def _(sp):
                for _turn, old, _held in last:
                    for s in old:
                        sp.sem_clear(s)
            yield (block, *sems)
        for _turn, _old, old_held in last:
            old_held.close()
        used.append((turn, sems, held.pop_all()))


def clear_used(nc):
    if used:
        with stage(nc):
            pass
        used.clear()


@contextmanager
def loop(nc, count):
    clear_used(nc)
    with nc.Fori(0, count) as i:
        yield i
        clear_used(nc)


@contextmanager
def branch(nc, condition):
    clear_used(nc)
    with nc.If(condition):
        yield
        clear_used(nc)


def stepper(engine, sem):
    done = [0]

    def step(instruction):
        done[0] += 1
        instruction.then_inc(sem, 1)
        engine.wait_ge(sem, done[0])

    return step


@dataclass
class Job:
    multiply: object
    engine: str
    evacuate: object


class Core:

    def __init__(self, nc, ctx):
        self.nc = nc
        self.sublayer, self.tensors = "", 0
        sb = lambda name, shape: ctx.enter_context(nc.sbuf_tensor(name, shape, F32))
        self.psum = ctx.enter_context(nc.psum_tensor("psum", [P, BANKS * BANK], F32))
        self.x_all = sb("x_all", [P, B, TT, D])
        self.x = sb("x", [P, TT, D])
        self.xT = sb("xT", [P, DT, S])
        self.delta = sb("delta", [P, TT, D])
        self.ident = sb("ident", [P, P])
        self.ones = sb("ones", [P, BANK])
        sb16 = lambda name, shape: ctx.enter_context(nc.sbuf_tensor(name, shape, BF16))
        self.ident16 = sb16("ident16", [P, P])
        self.causal16 = sb16("causal16", [P, P])
        self.causalT16 = sb16("causalT16", [P, P])
        self.stats = sb("stats", [P, TT, 6])
        self.moments = sb("moments", [P, TT, 2])
        self.spread = sb("spread", [P, TT])
        self.root = sb("root", [P, TT])
        self.rstd = sb("rstd", [P, TT])

    def named(self, name):
        self.tensors += 1
        return f"{self.sublayer}_{name}_{self.tensors}"

    def bank(self, j):
        return self.psum[:, (j % BANKS) * BANK:(j % BANKS + 1) * BANK]


def triangle(pool, mask, compare, sign, base=0):
    return pool.affine_select(out=mask, in_=mask, compare_op=compare, fill=MASKED, base=base,
                              pattern=[[-sign, mask.shape[1]]], channel_multiplier=sign)


def constants_stage(core, x):
    nc = core.nc
    with ExitStack() as held:
        causal = held.enter_context(nc.sbuf_tensor(core.named("causal"), [P, 2, P], F32))
        with stage(nc, "filled", "x_loaded") as (block, filled, x_loaded):
            @block.gpsimd
            def _(pool):
                pool.memset(core.ident[:], 0.0).then_inc(filled, 1)
                pool.memset(causal[:], 0.0).then_inc(filled, 1)
                pool.memset(core.ones[:], 1.0).then_inc(filled, 1)
                pool.wait_ge(filled, 3)
                pool.affine_select(out=core.ident[:], in_=core.ident[:], compare_op=ALU.not_equal, fill=1.0,
                                   base=0, pattern=[[-1, P]], channel_multiplier=1).then_inc(filled, 1)
                triangle(pool, causal[:, 0], ALU.is_ge, 1).then_inc(filled, 1)
                triangle(pool, causal[:, 1], ALU.is_ge, -1).then_inc(filled, 1)
                pool.wait_ge(filled, 6)
                pool.tensor_copy(core.ident16[:], core.ident[:]).then_inc(filled, 1)
                pool.tensor_copy(core.causal16[:], causal[:, 0]).then_inc(filled, 1)
                pool.tensor_copy(core.causalT16[:], causal[:, 1]).then_inc(filled, 1)
                pool.wait_ge(filled, 9)

            @block.sync
            def _(sp):
                for b in range(B):
                    sp.dma_start(core.x_all[:, b], x[b].rearrange("(t p) d -> p t d", p=P)).then_inc(x_loaded, 16)
                sp.wait_ge(x_loaded, 16 * B)


def load_stage(core, loads, zeroed=(), ones=()):
    nc = core.nc
    with stage(nc, "filled_by_pool", "filled_by_dve", "loaded_by_sp", "loaded_by_act") as (block, by_pool, by_dve, by_sp, by_act):
        @block.gpsimd
        def _(pool):
            for z in zeroed:
                pool.memset(z, 0.0).then_inc(by_pool, 1)
            if zeroed:
                pool.wait_ge(by_pool, len(zeroed))

        @block.vector
        def _(dve):
            for o in ones:
                nc.vector.memset(o, 1.0).then_inc(by_dve, 1)
            if ones:
                dve.wait_ge(by_dve, len(ones))

        @block.sync
        def _(sp):
            with nc.allow_non_contiguous_dma("biases and small tables, a value per partition"):
                for to, of in loads[0::2]:
                    sp.dma_start(to, of).then_inc(by_sp, 16)
            sp.wait_ge(by_sp, 16 * len(loads[0::2]))

        @block.scalar
        def _(act):
            with nc.allow_non_contiguous_dma("biases and small tables, a value per partition"):
                for to, of in loads[1::2]:
                    act.dma_start(to, of).then_inc(by_act, 16)
            if loads[1::2]:
                act.wait_ge(by_act, 16 * len(loads[1::2]))


def take_stage(core, b):
    nc = core.nc
    with stage(nc, "taken") as (block, taken):
        @block.vector
        def _(dve):
            nc.vector.tensor_copy(core.x[:], core.x_all[:, bass.ds(b, 1)].rearrange("p o t d -> p (o t) d")).then_inc(taken, 1)
            dve.wait_ge(taken, 1)


def take_turned_stage(core, b):
    nc = core.nc
    with stage(nc, "taken_by_dve", "taken_by_act", "turned_ready", "copied_by_dve", "copied_by_act") as (
            block, taken_by_dve, taken_by_act, turned_ready, copied_by_dve, copied_by_act):
        half = TT // 2
        rows = lambda cut: core.x_all[:, bass.ds(b, 1), cut].rearrange("p o t d -> p (o t) d")

        @block.vector
        def _(dve):
            nc.vector.tensor_copy(core.x[:, 0:half], rows(slice(0, half))).then_inc(taken_by_dve, 1)
            dve.wait_ge(turned_ready, 1)
            nc.vector.tensor_copy(core.xT[:, 0], core.bank(0)).then_inc(copied_by_dve, 1)
            dve.wait_ge(copied_by_dve, 1)

        @block.scalar
        def _(act):
            nc.scalar.copy(core.x[:, half:TT], rows(slice(half, TT))).then_inc(taken_by_act, 1)
            act.wait_ge(turned_ready, 2)
            nc.scalar.copy(core.xT[:, 1], core.bank(1)).then_inc(copied_by_act, 1)
            act.wait_ge(copied_by_act, 1)

        @block.tensor
        def _(pe):
            for f in range(DT):
                for t in range(TT):
                    if f == 0 and t == 0:
                        pe.wait_ge(taken_by_dve, 1)
                    if f == 0 and t == half:
                        pe.wait_ge(taken_by_act, 1)
                    last = nc.tensor.transpose(core.bank(f)[:, t * P:(t + 1) * P], core.x[:, t, f * P:(f + 1) * P], core.ident[:])
                last.then_inc(turned_ready, 1)


def product_stage(core, jobs):
    nc = core.nc

    def emptied_before(j, engine):
        return sum(job.engine == engine for job in jobs[:j])

    with stage(nc, "products_ready", "emptied_by_act", "emptied_by_dve", "dve_step") as (
            block, products_ready, emptied_by_act, emptied_by_dve, dve_step):
        @block.tensor
        def _(pe):
            for j, job in enumerate(jobs):
                if j >= BANKS:
                    last = jobs[j - BANKS].engine
                    pe.wait_ge(emptied_by_act if last == "act" else emptied_by_dve,
                               emptied_before(j - BANKS + 1, last))
                job.multiply(core.bank(j)).then_inc(products_ready, 1)

        @block.scalar
        def _(act):
            for j, job in enumerate(jobs):
                if job.engine == "act":
                    act.wait_ge(products_ready, j + 1)
                    job.evacuate(core.bank(j)).then_inc(emptied_by_act, 1)

        @block.vector
        def _(dve):
            step = stepper(dve, dve_step)
            for j, job in enumerate(jobs):
                if job.engine == "dve":
                    dve.wait_ge(products_ready, j + 1)
                    step(job.evacuate(core.bank(j)))
                    nc.vector.sem_inc(emptied_by_dve, 1)


def norm_stage(core, source, out, add=None, total=None):
    nc = core.nc
    with stage(nc, "added", "stats_ready", "moments_ready", "variance_ready", "root_ready", "rstd_ready", "normed") as (
            block, added, stats_ready, moments_ready, variance_ready, root_ready, rstd_ready, normed):
        @block.vector
        def _(dve):
            v = nc.vector
            y = source
            if add is not None:
                y = total
                for t in range(TT):
                    v.tensor_tensor(total[:, t], source[:, t], add[:, t], ALU.add).then_inc(added, 1)
            for t in range(TT):
                if add is not None:
                    dve.wait_ge(added, t + 1)
                v.bn_stats(core.stats[:, t], y[:, t]).then_inc(stats_ready, 1)
            for t in range(TT):
                dve.wait_ge(stats_ready, t + 1)
                v.bn_aggr(core.moments[:, t], core.stats[:, t]).then_inc(moments_ready, 1)
            dve.wait_ge(moments_ready, TT)
            v.tensor_scalar(core.spread[:], core.moments[:, :, 1], EPS, None, ALU.add).then_inc(variance_ready, 1)
            dve.wait_ge(root_ready, 2)
            v.reciprocal(core.rstd[:], core.root[:]).then_inc(rstd_ready, 1)
            dve.wait_ge(rstd_ready, 1)
            for t in range(TT):
                v.tensor_scalar(out(t), y[:, t], core.moments[:, t, 0:1], core.rstd[:, t:t + 1],
                                ALU.subtract, ALU.mult).then_inc(normed, 1)
            dve.wait_ge(normed, TT)

        @block.scalar
        def _(act):
            nc.scalar.activation(core.root[:], core.ones[:, 0:TT], ACT.Sqrt).then_inc(root_ready, 1)
            act.wait_ge(variance_ready, 1)
            act.wait_ge(root_ready, 1)
            nc.scalar.activation(core.root[:], core.spread[:], ACT.Sqrt).then_inc(root_ready, 1)


def residual_norm(core, b, delta=None):
    delta = core.delta if delta is None else delta
    norm_stage(core, core.x[:], lambda t: core.x_all[:, bass.ds(b, 1), t].rearrange("p o d -> p (o d)"), add=delta[:], total=delta[:])



def out_of_bank(core, engine, to, scale=None, bias=None, func=None):
    nc = core.nc
    rows, cols = to.shape[0], to.shape[-1]

    def evacuate(bank):
        held = bank[0:rows, 0:cols]
        if engine == "act":
            if bias is None and scale is None:
                return nc.scalar.activation(to, held, func or ACT.Copy)
            return nc.scalar.activation(to, held, func or ACT.Identity, bias=0.0 if bias is None else bias,
                                        scale=1.0 if scale is None else scale)
        if scale is not None:
            return nc.vector.tensor_scalar(to, held, scale, bias, ALU.mult, ALU.add)
        if bias is not None:
            return nc.vector.tensor_scalar(to, held, bias, None, ALU.add)
        return nc.vector.tensor_copy(to, held)

    return evacuate


def accumulate(nc, out, terms):
    for i, (lhsT, rhs) in enumerate(terms):
        last = nc.tensor.matmul(out, lhsT, rhs, start=(i == 0), stop=(i == len(terms) - 1))
    return last


def turned(core, source, to, rows=S, scale=None, bias=None, features=DT):
    nc = core.nc
    jobs = []
    for f in range(features):
        for c in range(0, rows, BANK):
            width = min(BANK, rows - c)

            def multiply(bank, f=f, c=c, width=width):
                for o in range(0, width, P):
                    n = min(P, width - o)
                    last = nc.tensor.transpose(bank[:, o:o + n], source[0:n, (c + o) // P, f * P:(f + 1) * P],
                                               core.ident[0:n, 0:n])
                return last

            engine = ("act", "dve")[len(jobs) % 2]
            jobs.append(Job(multiply, engine, out_of_bank(
                core, engine, to[:, f, c:c + width],
                None if scale is None else scale[:, f:f + 1], None if bias is None else bias[:, f:f + 1])))
    return jobs


def turned_back(core, source, evacuations, features=DT):
    nc = core.nc
    jobs = []
    for t in range(TT):
        def multiply(bank, t=t):
            for f in range(features):
                last = nc.tensor.transpose(bank[:, f * P:(f + 1) * P], source[:, f, t * P:(t + 1) * P], core.ident[:])
            return last

        jobs.append(Job(multiply, *evacuations(t)))
    return jobs


def columns_out(core, weight, xT, to, n, m=P, bias=None, func=None, engines=("act", "dve")):
    nc = core.nc
    kts = weight.shape[1]
    jobs = []
    for o in range(weight.shape[2] // m):
        for c in range(0, n, BANK):
            w = min(BANK, n - c)
            engine = engines[len(jobs) % len(engines)]

            def multiply(bank, o=o, c=c, w=w):
                return accumulate(nc, bank[0:m, 0:w],
                                  [(weight[:, k, o * m:(o + 1) * m], xT[:, k, c:c + w]) for k in range(kts)])

            jobs.append(Job(multiply, engine, out_of_bank(core, engine, to[0:m, o, c:c + w],
                                                          bias=None if bias is None else bias[0:m, o:o + 1], func=func)))
    return jobs


def rows_out(core, xT, weight, n, cols, evacuation, bias_row=None):
    nc = core.nc
    jobs = []
    for t in range((n + P - 1) // P):
        r = kt_rows(n, t)

        def multiply(bank, t=t, r=r):
            terms = [(xT[:, k, t * P:t * P + r], weight[:, k, 0:cols]) for k in range(weight.shape[1])]
            if bias_row is not None:
                terms.append((core.ones[0:1, 0:r], bias_row))
            return accumulate(nc, bank[0:r, 0:cols], terms)

        jobs.append(Job(multiply, *evacuation(t, r)))
    return jobs


def into(core, to):
    def evacuation(t, r=P):
        engine = ("act", "dve")[t % 2]
        return engine, out_of_bank(core, engine, to[0:r, t])
    return evacuation


def added_to(core, other, to):
    def evacuation(t, r=P):
        return "dve", lambda bank: core.nc.vector.tensor_tensor(to[0:r, t], bank[0:r, 0:to.shape[2]], other[0:r, t], ALU.add)
    return evacuation


def columned(v, p=P):
    return v.rearrange("(t p) -> p t", p=p)


def rowed(v):
    return v.rearrange("(a n) -> a n", a=1)


def spread_over(v):
    return v.partition_broadcast(P)



HIGH, MIDDLE, LOW = range(3)
STACKS = {16: [[(HIGH, HIGH), (HIGH, MIDDLE), (HIGH, LOW), (MIDDLE, HIGH), (MIDDLE, MIDDLE), (LOW, HIGH)]],
          64: [[(HIGH, HIGH), (HIGH, MIDDLE)], [(MIDDLE, HIGH), (MIDDLE, MIDDLE)], [(HIGH, LOW), (LOW, HIGH)]]}
PARTS = 3
HEADS = 16


@dataclass
class Heads:
    k_parts: object
    q_parts: object
    v: object
    out: object
    heads: int
    at_once: int
    dh: int
    keys: int
    scale: float
    blocks: object
    valid: object = None
    lag: float = 2.5
    top: int = 0


def parts_stage(core, jobs):
    nc = core.nc
    pieces = [(x, parts, min(P, scratch.shape[1]), t) for x, parts, scratch in jobs for t in range(x.shape[1])]
    scratches = [scratch for x, _, scratch in jobs for _t in range(x.shape[1])]
    with stage(nc, "high_ready", "rest_ready", "middle_ready", "low_ready", "parts_stored") as (
            block, high_ready, rest_ready, middle_ready, low_ready, parts_stored):
        @block.scalar
        def _(act):
            for i in range(len(pieces) + 1):
                if i < len(pieces):
                    x, parts, r, t = pieces[i]
                    nc.scalar.copy(parts[0:r, HIGH, t], x[0:r, t]).then_inc(high_ready, 1)
                if i >= 1:
                    x, parts, r, t = pieces[i - 1]
                    act.wait_ge(rest_ready, i)
                    nc.scalar.copy(parts[0:r, MIDDLE, t], x[0:r, t]).then_inc(middle_ready, 1)

        @block.vector
        def _(dve):
            for i in range(len(pieces) + 1):
                if i < len(pieces):
                    x, parts, r, t = pieces[i]
                    dve.wait_ge(high_ready, i + 1)
                    nc.vector.tensor_tensor(x[0:r, t], x[0:r, t], parts[0:r, HIGH, t], ALU.subtract).then_inc(rest_ready, 1)
                if i >= 1:
                    x, parts, r, t = pieces[i - 1]
                    dve.wait_ge(middle_ready, i)
                    nc.vector.tensor_tensor(parts[0:r, LOW, t], x[0:r, t], parts[0:r, MIDDLE, t], ALU.subtract).then_inc(low_ready, 1)

        @block.sync
        def _(sp):
            for i, (x, parts, r, t) in enumerate(pieces):
                scratch = scratches[i]
                for part, ready in ((HIGH, high_ready), (MIDDLE, middle_ready), (LOW, low_ready)):
                    sp.wait_ge(ready, i + 1)
                    sp.dma_start(scratch[part, t * P:t * P + r], parts[0:r, part, t]).then_inc(parts_stored, 16)
            sp.wait_ge(parts_stored, 16 * PARTS * len(pieces))


def scratch_for(core, name, rows, n):
    return core.nc.dram_tensor(core.named(name), (PARTS, rows, n), BF16, kind="Internal").ap()


def load_batches(heads):
    cuts = [c for c in (0, 2) if c < heads] + [heads]
    return [(x, y) for x, y in zip(cuts, cuts[1:]) if y > x]


def stacked_loads(engine, a, g, to, parts_of, side, semaphores):
    heads_of = parts_of.rearrange("c (h d) n -> c h d n", d=a.dh)
    for (h0, h1), loaded in zip(load_batches(a.at_once), semaphores):
        for term, rows in enumerate(STACKS[a.dh]):
            for r, parts in enumerate(rows):
                of = heads_of[parts[side], bass.ds(g * a.at_once + h0, h1 - h0)].rearrange("h d n -> d h n")
                engine.dma_start(to[r * a.dh:(r + 1) * a.dh, term, h0:h1], of).then_inc(loaded, 16)


def batch_loads(a):
    return 16 * sum(len(rows) for rows in STACKS[a.dh])


def value_slot(dh):
    return 32 if dh < 32 else dh


def copy_values(pool, a, g, vg, copied):
    KT = (a.keys + P - 1) // P
    full = KT if kt_rows(a.keys, KT - 1) == P else KT - 1
    here = bass.ds(g * a.at_once, a.at_once)
    if full:
        pool.tensor_copy(vg[:, 0:full], a.v[:, 0:full, here]).then_inc(copied, 1)
    if full < KT:
        r = kt_rows(a.keys, KT - 1)
        pool.tensor_copy(vg[0:r, full], a.v[0:r, full, here]).then_inc(copied, 1)


def value_pieces(a):
    KT = (a.keys + P - 1) // P
    ragged = kt_rows(a.keys, KT - 1) < P
    return (1 if KT > 1 or not ragged else 0) + (1 if ragged else 0)


def attention_stage(core, a, g, bufs):
    nc = core.nc
    HB, dh = a.at_once, a.dh
    TERMS = STACKS[dh]
    KT = (a.keys + P - 1) // P
    slot = value_slot(dh)
    side_by_side = slot == 32
    stacked = len(TERMS[0]) * dh
    qs, ks, og = bufs.qs, bufs.ks, bufs.og
    vg = bufs.vg
    CHUNK = 2 * BANK
    HALF = S // 2
    RING = bufs.ring.shape[1]

    head_chunks = []
    chunks_of_tile = 0
    for q in range(TT):
        bl = a.blocks(q)
        k0, k1 = bl[0][0] * P, min(a.keys, (bl[-1][0] + 1) * P)
        for i, c in enumerate(range(k0, k1, CHUNK)):
            head_chunks.append((q, i, c, min(CHUNK, k1 - c), [(kt, m) for kt, m, _ in bl if m is not None and c <= kt * P < c + CHUNK]))
            chunks_of_tile = max(chunks_of_tile, i + 1)
    CH = len(head_chunks)
    blocks = []
    for kt in range(KT):
        seen = [q for q in range(TT) if any(b[0] == kt for b in a.blocks(q))]
        masks = [(q, next(b[2] for b in a.blocks(q) if b[0] == kt)) for q in seen]
        blocks.append((kt, kt_rows(a.keys, kt), seen[0], len(seen), [(q, m) for q, m in masks if m is not None]))
    BL = len(blocks)
    first_block = [min(i for i, bl in enumerate(blocks) if bl[2] <= q < bl[2] + bl[3]) for q in range(TT)]
    last_block = [max(i for i, bl in enumerate(blocks) if bl[2] <= q < bl[2] + bl[3]) for q in range(TT)]

    order = sorted([(h + (i + 0.5) / CH, 0, h, i) for h in range(HB) for i in range(CH)] +
                   [(h + a.lag + (i + 0.5) / BL, 1, h, i) for h in range(HB) for i in range(BL)])
    plan = []
    turned, behind, outputs = 0, [], []
    apart = 2 if BL > TT else 1

    def add_values():
        h, i = behind.pop(0)
        plan.append(("values", h, i))
        if outputs and i == 1 % BL:
            plan.append(("output", outputs.pop(0), 0))
        if i == BL - 1:
            outputs.append(h)

    for _, stream, h, i in order:
        if stream == 0:
            plan.append(("scores", h, i))
            if turned < h and i >= min(2, CH - 1):
                plan.append(("negative", turned, 0))
                turned += 1
        else:
            while turned <= h:
                plan.append(("negative", turned, 0))
                turned += 1
            plan.append(("shifted", h, i))
            behind.append((h, i))
            if len(behind) > apart:
                add_values()
    while behind:
        add_values()
    plan += [("output", h, 0) for h in outputs]

    batches = load_batches(HB)
    with stage(nc, *[f"operands_{i}_loaded" for i in range(len(batches))], "v_copied", "scores_ready", "maximum_taken", "negative_ready",
               "negative_turned", "negative_copied", "gp_step", "parts_ready", "largest_loaded_even", "largest_loaded_odd", "shifted_ready", "exp_ready", "values_added",
               "output_copied", "output_turned", "out_kept", "summed", "dve_step") as (block, *sems):
        loaded = sems[:len(batches)]
        (v_copied, scores_ready, maximum_taken, negative_ready, negative_turned, negative_copied, gp_step, parts_ready,
         *largest_loaded, shifted_ready, exp_ready, values_added, output_copied, output_turned, out_kept, summed, dve_step) = sems[len(batches):]

        @block.sync
        def _(sp):
            stacked_loads(sp, a, g, ks, a.k_parts, 0, loaded)
            for h in range(HB):
                sp.wait_ge(parts_ready, h + 1)
                for part in range(PARTS):
                    sp.dma_start(bufs.largest_row(part, h), bufs.max_parts[:, h % 2, part]).then_inc(largest_loaded[h % 2], 16)

        @block.gpsimd
        def _(pool):
            if a.at_once < a.heads:
                copy_values(pool, a, g, vg, v_copied)
            step = stepper(pool, gp_step)

            def split_maxima(h):
                pool.wait_ge(negative_copied, h + 1)
                if h >= 2:
                    pool.wait_ge(largest_loaded[h % 2], 16 * PARTS * (h // 2))
                negative, parts = bufs.negative[:, h % 2], bufs.max_parts[:, h % 2]
                step(pool.tensor_copy(parts[:, HIGH], negative))
                step(pool.tensor_tensor(negative, negative, parts[:, HIGH], ALU.subtract))
                step(pool.tensor_copy(parts[:, MIDDLE], negative))
                pool.tensor_tensor(parts[:, LOW], negative, parts[:, MIDDLE], ALU.subtract).then_inc(parts_ready, 1)

            def sum_up(h, i):
                e = BL * h + i
                rows = blocks[i][1]
                sums, block_held = bufs.sums[:, h % 2], bufs.ring[:, e % RING]
                pool.wait_ge(exp_ready, e + 1)
                if i == 0:
                    if h >= 2:
                        pool.wait_ge(output_turned, h - 1)
                    pool.tensor_copy(sums, block_held).then_inc(summed, 1)
                else:
                    pool.wait_ge(summed, e)
                    pool.tensor_tensor(sums[0:rows], sums[0:rows], block_held[0:rows], ALU.add).then_inc(summed, 1)

            for what, h, i in plan:
                if what == "negative":
                    split_maxima(h)
                elif what == "values" and not side_by_side:
                    sum_up(h, i)

        @block.tensor
        def _(pe):
            def scores(h, i):
                n = CH * h + i
                q, _, c, w, masks = head_chunks[i]
                if i == 0 and h in [b[0] for b in batches]:
                    pe.wait_ge(loaded[[b[0] for b in batches].index(h)], 2 * batch_loads(a))
                if n >= 2:
                    pe.wait_ge(maximum_taken, n - 1)
                base = (n % 2) * CHUNK
                for o in range(0, w, BANK):
                    m = min(BANK, w - o)
                    inside = [(kt, mask) for kt, mask in masks if c + o <= kt * P < c + o + m]
                    out = core.psum[:, base + o:base + o + m]
                    for t in range(len(TERMS)):
                        last = nc.tensor.matmul(out, qs[0:stacked, t, h, q * P:(q + 1) * P], ks[0:stacked, t, h, c + o:c + o + m],
                                                start=(t == 0), stop=(t == len(TERMS) - 1 and not inside))
                    for j, (kt, mask) in enumerate(inside):
                        at = base + kt * P - c
                        last = nc.tensor.matmul(core.psum[:, at:at + kt_rows(a.keys, kt)], core.ident16[:], mask,
                                                start=False, stop=(j == len(inside) - 1))
                last.then_inc(scores_ready, 1)

            def shifted(h, i):
                e = BL * h + i
                kt, rows, q0, nq, masks = blocks[i]
                if i == 0:
                    pe.wait_ge(largest_loaded[h % 2], 16 * PARTS * (h // 2 + 1))
                if e >= 2:
                    pe.wait_ge(exp_ready, e - 1)
                bank = core.bank(4 + e % 2)
                terms = bufs.shifted_terms(h, slice(kt * P, kt * P + rows), slice(q0 * P, (q0 + nq) * P), rows)
                for t, (lhsT, rhs) in enumerate(terms):
                    last = nc.tensor.matmul(bank[0:rows, 0:nq * P], lhsT, rhs, start=(t == 0), stop=(t == len(terms) - 1 and not masks))
                for j, (q, mask) in enumerate(masks):
                    last = nc.tensor.matmul(bank[0:rows, (q - q0) * P:(q - q0 + 1) * P], core.ident16[0:rows, 0:rows], mask,
                                            start=False, stop=(j == len(masks) - 1))
                last.then_inc(shifted_ready, 1)

            def values(h, i):
                e = BL * h + i
                kt, rows, q0, nq, _ = blocks[i]
                pe.wait_ge(exp_ready, e + 1)
                if e == 0 and a.at_once < a.heads:
                    pe.wait_ge(v_copied, value_pieces(a))
                if i == 0 and h >= 1:
                    pe.wait_ge(output_copied, h)
                if side_by_side:
                    for q in range(q0, q0 + nq):
                        last = nc.tensor.matmul(core.bank(6)[32 * q:32 * q + 32, 0:P], vg[0:rows, kt, h],
                                                bufs.ring[0:rows, e % RING, (q - q0) * P:(q - q0 + 1) * P],
                                                start=(i == first_block[q]), stop=(i == last_block[q]))
                else:
                    for half in range(2):
                        last = nc.tensor.matmul(core.bank(6)[half * dh:(half + 1) * dh, 0:HALF], vg[0:rows, kt, h],
                                                bufs.ring[0:rows, e % RING, half * HALF:(half + 1) * HALF],
                                                start=(i == 0), stop=(i == BL - 1))
                last.then_inc(values_added, 1)

            last_in_bank_7 = None
            for what, h, i in plan:
                if what == "scores":
                    scores(h, i)
                elif what == "shifted":
                    shifted(h, i)
                elif what == "values":
                    values(h, i)
                else:
                    if last_in_bank_7:
                        pe.wait_ge(*last_in_bank_7)
                    if what == "negative":
                        pe.wait_ge(negative_ready, h + 1)
                        nc.tensor.transpose(core.bank(7)[0:TT, 0:P], bufs.largest[:, h % 2], core.ident[:]).then_inc(negative_turned, 1)
                        last_in_bank_7 = (negative_copied, h + 1)
                    else:
                        pe.wait_ge(output_copied, h + 1)
                        if side_by_side:
                            last = nc.tensor.transpose(core.bank(7)[:, 0:P], bufs.output[:, 0:P], core.ident[:])
                        else:
                            pe.wait_ge(summed, BL * (h + 1))
                            for at in range(0, HALF, P):
                                nc.tensor.transpose(core.bank(7)[:, at:at + P], bufs.output[:, at:at + P], core.ident[:])
                            for q in range(TT):
                                last = nc.tensor.matmul(core.bank(7)[:, TT * dh + q:TT * dh + q + 1], bufs.sums[:, h % 2, q * P:(q + 1) * P],
                                                        core.ones[:, 0:1], start=True, stop=True)
                        last.then_inc(output_turned, 1)
                        last_in_bank_7 = (out_kept, h + 1)

        @block.scalar
        def _(act):
            stacked_loads(act, a, g, qs, a.q_parts, 1, loaded)
            for what, h, i in plan:
                if what == "shifted":
                    e = BL * h + i
                    _, rows, _, nq, _ = blocks[i]
                    act.wait_ge(shifted_ready, e + 1)
                    if e >= RING:
                        act.wait_ge(values_added, e - RING + 1)
                        if not side_by_side:
                            act.wait_ge(summed, e - RING + 1)
                    nc.scalar.activation(bufs.ring[0:rows, e % RING, 0:nq * P], core.bank(4 + e % 2)[0:rows, 0:nq * P], ACT.Exp,
                                         scale=a.scale).then_inc(exp_ready, 1)
                elif what == "values" and i == BL - 1:
                    act.wait_ge(values_added, BL * (h + 1))
                    if h >= 1:
                        act.wait_ge(output_turned, h)
                    if side_by_side:
                        nc.scalar.copy(bufs.output[:, 0:P], core.bank(6)[:, 0:P]).then_inc(output_copied, 1)
                    else:
                        nc.scalar.copy(bufs.output[:], core.bank(6)[:, 0:HALF]).then_inc(output_copied, 1)

        @block.vector
        def _(dve):
            step = stepper(dve, dve_step)
            v = nc.vector
            for what, h, i in plan:
                if what == "scores":
                    n = CH * h + i
                    q, place, _, w, _ = head_chunks[i]
                    dve.wait_ge(scores_ready, n + 1)
                    base = (n % 2) * CHUNK
                    v.reduce_max(bufs.maxima[:, h % 2, q, place:place + 1], core.psum[:, base:base + w], AX.X).then_inc(maximum_taken, 1)
                    if i == CH - 1:
                        dve.wait_ge(maximum_taken, CH * (h + 1))
                        if h >= 2:
                            dve.wait_ge(negative_turned, h - 1)
                        v.tensor_reduce(bufs.largest[:, h % 2], bufs.maxima[:, h % 2, :, 0:chunks_of_tile], AX.X, ALU.max,
                                        negate=True).then_inc(negative_ready, 1)
                elif what == "negative":
                    dve.wait_ge(negative_turned, h + 1)
                    if h >= 2:
                        dve.wait_ge(parts_ready, h - 1)
                    v.tensor_copy(bufs.negative[:, h % 2], core.bank(7)[0:TT, 0:P]).then_inc(negative_copied, 1)
                elif what == "output":
                    dve.wait_ge(output_turned, h + 1)
                    held = core.bank(7)[:, 0:TT * slot].rearrange("p (t s) -> p t s", s=slot)
                    step(v.reciprocal(bufs.share[:], held[:, :, dh] if side_by_side else core.bank(7)[:, TT * dh:TT * dh + TT]))
                    if a.valid is not None:
                        step(v.tensor_tensor(bufs.share[:], bufs.share[:], a.valid[:], ALU.mult))
                    if not side_by_side:
                        held = held.rearrange("p (t f) s -> p f t s", f=2)
                        for half in range(2):
                            tiles = slice(half * TT // 2, (half + 1) * TT // 2)
                            last = v.tensor_tensor(og[:, tiles, h * dh:(h + 1) * dh], held[:, half],
                                                   bufs.share[:, tiles].unsqueeze(2).to_broadcast([P, TT // 2, dh]), ALU.mult)
                        last.then_inc(out_kept, 1)
                    else:
                        v.tensor_tensor(og[:, :, h * dh:(h + 1) * dh], held[:, :, 0:dh],
                                        bufs.share[:].unsqueeze(2).to_broadcast([P, TT, dh]), ALU.mult).then_inc(out_kept, 1)
            if a.at_once < a.heads:
                dve.wait_ge(out_kept, HB)
                step(v.tensor_copy(a.out[:, :, bass.ds(g * (HB * dh), HB * dh)], og[:]))


@dataclass
class Buffers:
    qs: object
    ks: object
    vg: object = None
    og: object = None
    ring: object = None
    output: object = None
    sums: object = None
    maxima: object = None
    largest: object = None
    negative: object = None
    max_parts: object = None
    share: object = None
    largest_row: object = None
    shifted_terms: object = None


def attention_buffers(core, ctx, a):
    nc = core.nc
    KT = (a.keys + P - 1) // P
    HB, dh = a.at_once, a.dh
    TERMS = STACKS[dh]
    stacked = len(TERMS[0]) * dh
    sb = lambda name, shape, dt=F32: ctx.enter_context(nc.sbuf_tensor(core.named(name), shape, dt))
    behind = stacked + PARTS <= P
    rows = stacked + PARTS if behind else P
    bufs = Buffers(qs=sb("qs", [rows, len(TERMS), HB, S], BF16), ks=sb("ks", [rows, len(TERMS), HB, a.keys], BF16),
                   ring=sb("ring", [P, 4, S]), output=sb("output", [P, P if dh < 32 else S // 2]),
                   maxima=sb("maxima", [P, 2, TT, 2]), largest=sb("largest", [P, 2, TT]), negative=sb("negative", [TT, 2, P]),
                   max_parts=sb("max_parts", [TT, 2, PARTS, P], BF16), share=sb("share", [P, TT]))
    if dh >= 32:
        bufs.sums = sb("sums", [P, 2, S])
    if HB < a.heads:
        bufs.vg, bufs.og = sb("vg", [P, KT, HB, value_slot(dh)]), sb("og", [P, TT, HB * dh])
    else:
        bufs.vg, bufs.og = a.v, a.out
    if behind:
        bufs.largest_row = lambda part, h: bufs.qs[stacked + part:stacked + part + 1, 0, h].rearrange("o (t n) -> o t n", n=P)
        bufs.shifted_terms = lambda h, keys, queries, n: [(bufs.ks[:, 0, h, keys], bufs.qs[:, 0, h, queries])]
        ones = bufs.ks[stacked:rows, 0]
    else:
        largest_rows, ones_rows = sb("largest_rows", [PARTS, HB, S], BF16), sb("ones_rows", [PARTS, P], BF16)
        bufs.largest_row = lambda part, h: largest_rows[part:part + 1, h].rearrange("o (t n) -> o t n", n=P)
        bufs.shifted_terms = lambda h, keys, queries, n: [
            *[(bufs.ks[:, t, h, keys], bufs.qs[:, t, h, queries]) for t in range(len(TERMS))],
            (ones_rows[:, 0:n], largest_rows[:, h, queries])]
        ones = ones_rows[:]
    with stage(nc, "filled") as (block, filled):
        @block.vector
        def _(dve):
            nc.vector.memset(ones, 1.0).then_inc(filled, 1)
            dve.wait_ge(filled, 1)
    return bufs


def attention(core, a, bufs=None):
    nc = core.nc
    with ExitStack() as ctx:
        if bufs is None:
            bufs = attention_buffers(core, ctx, a)
        if a.at_once < a.heads:
            with loop(nc, a.heads // a.at_once) as g:
                attention_stage(core, a, g, bufs)
        else:
            attention_stage(core, a, 0, bufs)


@dataclass
class TopBuffers:
    qs: object
    ks: object
    vg: object
    og: object
    exps: object
    below: object
    probs: object
    signs: object
    probsT: object
    output: object
    candidates: object
    first: object
    edge: object
    next_best: object
    negmax: object
    edge_exp: object
    low: object
    balance: object
    wanted: object
    bound: object
    last_kept: object
    picked: object
    kept_signs: object
    kept: object
    share: object
    wrong: object
    flags: object


BEST = 8


def segments_of(keys):
    count = 20
    width = (keys + count - 1) // count
    return [(i, min(width, keys - i)) for i in range(0, keys, width)]


def top_attention_stage(core, a, bufs, exact_tile=None):
    nc = core.nc
    exact = exact_tile is not None
    HB, NT = (1, 1) if exact else (a.heads, TT)
    dh, M_ = a.dh, a.keys
    (stack,) = STACKS[dh]
    stacked = len(stack) * dh
    KT = (M_ + P - 1) // P
    slot = value_slot(dh)
    OUT = slot * NT
    tiles = [(h, q) for h in range(HB) for q in range(NT)]
    N = len(tiles)
    LAG = 3
    EXPS = bufs.exps.shape[1]
    segments = segments_of(M_)
    turns = [(kt, min(BANK // P, KT - kt)) for kt in range(0, KT, BANK // P)]
    TC = len(turns)
    heads_out = {NT * (h + 1) + LAG + 1: h for h in range(HB - 1)}
    ROUNDS = a.top // BEST - 2
    beside = {}
    for i in range(len(segments)):
        beside.setdefault(5 + i * (2 * ROUNDS - 4) // len(segments), []).append(i)
    scores_held = core.psum[:, 0:M_]
    vg, og = (bufs.vg, bufs.og) if exact else (a.v, a.out)
    GROUP = 1 if exact else 2
    SLOTS = bufs.ks.shape[2] // GROUP
    query_batches = [(x, y) for x, y in ((0, GROUP), (GROUP, HB)) if y > x]
    with stage(nc, *[f"keys_{i}_loaded" for i in range(SLOTS)], "first_queries_loaded", "queries_loaded", "v_copied", "scores_ready", "scores_copied",
               "maximum_ready", "edge_ready", "edge_exp_ready", "low_ready", "exp_ready", "below_ready", "below_taken", "counted",
               "probs_ready", "checked", "probs_turned", "turned_copied", "values_ready", "output_copied", "output_turned", "out_kept",
               "segment_step", "round_step", "last_ready", "bound_ready", "dve_step") as (block, *sems):
        keys_loaded, queries_loaded = sems[:SLOTS], sems[SLOTS:SLOTS + 2]
        (v_copied, scores_ready, scores_copied, maximum_ready, edge_ready, edge_exp_ready, low_ready, exp_ready,
         below_ready, below_taken, counted, probs_ready, checked, probs_turned, turned_copied, values_ready, output_copied,
         output_turned, out_kept, segment_step, round_step, last_ready, bound_ready, dve_step) = sems[SLOTS + 2:]

        @block.sync
        def _(sp):
            keys_of = a.k_parts.rearrange("c (h d) n -> c d h n", d=dh)
            for i, h in enumerate(range(0, HB, GROUP)):
                if i >= SLOTS:
                    sp.wait_ge(scores_ready, NT * (h - (SLOTS - 1) * GROUP))
                at = (i % SLOTS) * GROUP
                here = bass.ds(exact_tile[0], 1) if exact else slice(h, h + GROUP)
                for r, parts in enumerate(stack):
                    sp.dma_start(bufs.ks[r * dh:(r + 1) * dh, 0, at:at + GROUP], keys_of[parts[0], :, here]).then_inc(keys_loaded[i % SLOTS], 16)

        @block.gpsimd
        def _(pool):
            if exact:
                full = M_ // P
                here = bass.ds(exact_tile[0], 1)
                pool.tensor_copy(vg[:, 0:full], a.v[:, 0:full, here]).then_inc(v_copied, 1)
                pool.tensor_copy(vg[0:M_ - full * P, full], a.v[0:M_ - full * P, full, here]).then_inc(v_copied, 1)
                return

            def keep(n):
                pool.wait_ge(checked, n + 1)
                if n >= 1:
                    pool.wait_ge(probs_turned, TC * n)
                pool.tensor_tensor(bufs.probs[:], bufs.exps[:, n % EXPS], bufs.kept_signs[:], ALU.mult).then_inc(probs_ready, 1)

            def below(n):
                pool.wait_ge(counted, n + 1)
                if n >= 1:
                    pool.wait_ge(below_taken, n)
                pool.tensor_tensor(bufs.below[:], bufs.exps[:, n % EXPS], bufs.signs[:], ALU.mult).then_inc(below_ready, 1)

            for n in range(N + 1):
                if n < N:
                    below(n)
                if n >= 1:
                    keep(n - 1)

        @block.tensor
        def _(pe):
            def scores(n):
                h, q = tiles[n]
                group = h // GROUP
                if q == 0 and h % GROUP == 0:
                    pe.wait_ge(keys_loaded[group % SLOTS], 16 * len(stack) * (group // SLOTS + 1))
                    if group < 2:
                        pe.wait_ge(queries_loaded[group], 16 * len(stack))
                if n >= 1:
                    pe.wait_ge(scores_copied if exact else exp_ready, n)
                for c in range(0, M_, BANK):
                    w = min(BANK, M_ - c)
                    last = nc.tensor.matmul(core.psum[:, c:c + w], bufs.qs[0:stacked, 0, h, q * P:(q + 1) * P],
                                            bufs.ks[0:stacked, 0, h % (SLOTS * GROUP), c:c + w], start=True, stop=True)
                last.then_inc(scores_ready, 1)

            def turn(n):
                pe.wait_ge(probs_ready, n + 1)
                for i, (kt, count) in enumerate(turns):
                    e = TC * n + i
                    if e >= 2:
                        pe.wait_ge(turned_copied, e - 1)
                    for j in range(count):
                        r = kt_rows(M_, kt + j)
                        last = nc.tensor.transpose(core.bank(4 + e % 2)[0:r, j * P:(j + 1) * P],
                                                   bufs.probs[:, (kt + j) * P:(kt + j) * P + r], core.ident[:])
                    last.then_inc(probs_turned, 1)

            def values(n):
                h, q = tiles[n]
                pe.wait_ge(turned_copied, TC * (n + 1))
                if n == 0 and exact:
                    pe.wait_ge(v_copied, 2)
                if q == 0 and h >= 1:
                    pe.wait_ge(output_copied, h)
                for kt in range(KT):
                    r = kt_rows(M_, kt)
                    last = nc.tensor.matmul(core.bank(6)[slot * q:slot * (q + 1), 0:P], vg[0:r, kt, h],
                                            bufs.probsT[0:r, kt, q * P:(q + 1) * P], start=(kt == 0), stop=(kt == KT - 1))
                last.then_inc(values_ready, 1)

            def turn_output(h):
                pe.wait_ge(output_copied, h + 1)
                if h >= 1:
                    pe.wait_ge(out_kept, h)
                nc.tensor.transpose(core.bank(7)[:, 0:OUT], bufs.output[0:OUT], core.ident[0:OUT, 0:OUT]).then_inc(output_turned, 1)

            for n in range(N + LAG + 2):
                if n < N:
                    scores(n)
                if n - 1 in heads_out:
                    turn_output(heads_out[n - 1])
                if 0 <= n - 1 - LAG < N:
                    turn(n - 1 - LAG)
                if n - 2 - LAG >= 0:
                    values(n - 2 - LAG)
            turn_output(HB - 1)

        @block.scalar
        def _(act):
            queries_of = a.q_parts.rearrange("c (h d) n -> c d h n", d=dh)
            for (h0, h1), loaded in zip(query_batches, queries_loaded):
                here = bass.ds(exact_tile[0], 1) if exact else slice(h0, h1)
                tokens = bass.ds(exact_tile[1] * P, P) if exact else slice(0, S)
                for r, parts in enumerate(stack):
                    act.dma_start(bufs.qs[r * dh:(r + 1) * dh, 0, h0:h1, 0:NT * P], queries_of[parts[1], :, here, tokens]).then_inc(loaded, 16)

            def copy_turned(n):
                h, q = tiles[n]
                for i, (kt, count) in enumerate(turns):
                    e = TC * n + i
                    act.wait_ge(probs_turned, e + 1)
                    if i == 0 and h >= 1:
                        act.wait_ge(values_ready, n - NT + 1)
                    r = kt_rows(M_, kt + count - 1)
                    nc.scalar.activation(bufs.probsT[0:r, kt:kt + count, q * P:(q + 1) * P],
                                         core.bank(4 + e % 2)[0:r, 0:count * P].rearrange("p (k n) -> p k n", n=P), ACT.Relu).then_inc(turned_copied, 1)

            def count_below(n):
                act.wait_ge(edge_ready, n + 1)
                act.wait_ge(exp_ready, n + 1)
                nc.scalar.activation(bufs.edge_exp[:, n % 2:n % 2 + 1], bufs.edge[:, n % 2, BEST - 1:BEST], ACT.Exp, scale=a.scale,
                                     bias=bufs.negmax[:, n % 2:n % 2 + 1]).then_inc(edge_exp_ready, 1)
                act.wait_ge(edge_exp_ready, n + 1)
                nc.scalar.activation(bufs.low[:, n % 2:n % 2 + 1], bufs.edge_exp[:, n % 2:n % 2 + 1], ACT.Copy,
                                     scale=1.0 - 2.0 ** -20).then_inc(low_ready, 1)
                act.wait_ge(low_ready, n + 1)
                if n >= 1:
                    act.wait_ge(below_ready, n)
                nc.scalar.activation(bufs.signs[:], bufs.exps[:, n % EXPS], ACT.Sign, scale=-1.0, bias=bufs.low[:, n % 2:n % 2 + 1],
                                     accum_out=bufs.balance[:, n % 2:n % 2 + 1]).then_inc(counted, 1)

            def check(n):
                act.wait_ge(bound_ready, n + 1)
                if n >= 1:
                    act.wait_ge(probs_ready, n)
                nc.scalar.activation(bufs.kept_signs[:], bufs.exps[:, n % EXPS], ACT.Sign, bias=bufs.bound[:, n % 2:n % 2 + 1],
                                     accum_out=bufs.kept[:, n:n + 1]).then_inc(checked, 1)

            for n in range(N + LAG + 1):
                if n < N:
                    if exact:
                        act.wait_ge(scores_ready, n + 1)
                        nc.scalar.copy(bufs.below[:], scores_held).then_inc(scores_copied, 1)
                        act.wait_ge(scores_copied, n + 1)
                    act.wait_ge(maximum_ready, n + 1)
                    if n >= EXPS:
                        act.wait_ge(probs_ready, n - EXPS + 1)
                    nc.scalar.activation(bufs.exps[:, n % EXPS], bufs.below[:] if exact else scores_held, ACT.Exp, scale=a.scale,
                                         bias=bufs.negmax[:, n % 2:n % 2 + 1]).then_inc(exp_ready, 1)
                if 1 <= n <= N and not exact:
                    count_below(n - 1)
                if 2 <= n <= N + 1 and not exact:
                    check(n - 2)
                if 0 <= n - LAG < N:
                    copy_turned(n - LAG)
                if n >= LAG + 1 and (n - LAG) % NT == 0:
                    h = (n - LAG) // NT - 1
                    act.wait_ge(values_ready, NT * (h + 1))
                    if h >= 1:
                        act.wait_ge(output_turned, h)
                    nc.scalar.copy(bufs.output[0:OUT], core.bank(6)[0:OUT, 0:P]).then_inc(output_copied, 1)

        @block.vector
        def _(dve):
            step = stepper(dve, dve_step)
            v = nc.vector

            def take_maximum(n, best):
                if n >= 2:
                    dve.wait_ge(exp_ready if exact else edge_exp_ready, n - 1)
                v.tensor_scalar(bufs.negmax[:, n % 2:n % 2 + 1], best, -a.scale, None, ALU.mult).then_inc(maximum_ready, 1)

            def all_taken():
                dve.wait_ge(scores_copied, 1)
                source = bufs.below[:]
                for i in range(a.top // BEST):
                    step(v.max(bufs.first[:, 0], source))
                    if i == 0:
                        take_maximum(0, bufs.first[:, 0, 0:1])
                        dve.wait_ge(maximum_ready, 1)
                    step(v.match_replace(bufs.probs[:], bufs.first[:, 0], source, TAKEN))
                    source = bufs.probs[:]
                dve.wait_ge(exp_ready, 1)
                v.scalar_tensor_tensor(out=bufs.probs[:], in0=bufs.probs[:], scalar=TAKEN / 2, in1=bufs.exps[:, 0],
                                       op0=ALU.is_lt, op1=ALU.mult).then_inc(probs_ready, 1)

            def segment(n, i):
                if i == 0:
                    if n >= 2:
                        dve.wait_ge(edge_ready, n - 1)
                    dve.wait_ge(scores_ready, n + 1)
                c, w = segments[i]
                v.max(bufs.candidates[:, n % 2, i * BEST:(i + 1) * BEST], core.psum[:, c:c + w]).then_inc(segment_step, 1)

            def first_round(n):
                dve.wait_ge(segment_step, len(segments) * (n + 1))
                v.max(bufs.first[:, 0], bufs.candidates[:, n % 2]).then_inc(round_step, 1)

            def keep_maximum(n):
                dve.wait_ge(round_step, n * 2 * ROUNDS + 1)
                take_maximum(n, bufs.first[:, 0, 0:1])

            def split(n, between):
                candidates = bufs.candidates[:, n % 2]
                for k in range(1, 2 * ROUNDS + 1):
                    best = bufs.first[:, (k // 2) % 2]
                    dve.wait_ge(round_step, n * 2 * ROUNDS + k)
                    if k == 2 * ROUNDS:
                        if n >= 2:
                            dve.wait_ge(edge_exp_ready, n - 1)
                        v.max(bufs.edge[:, n % 2], candidates).then_inc(edge_ready, 1)
                    elif k % 2 == 0:
                        v.max(best, candidates).then_inc(round_step, 1)
                    else:
                        v.match_replace(candidates, best, candidates, TAKEN).then_inc(round_step, 1)
                    if between:
                        between.pop(0)()
                    if n + 1 < N:
                        for i in beside.get(k, []):
                            segment(n + 1, i)
                if n + 1 < N:
                    first_round(n + 1)
                    keep_maximum(n + 1)

            def selection(n):
                def take_below():
                    dve.wait_ge(below_ready, n + 1)
                    v.max(bufs.next_best[:], bufs.below[:]).then_inc(below_taken, 1)

                def pick_last():
                    dve.wait_ge(below_taken, n + 1)
                    dve.wait_ge(counted, n + 1)
                    v.scalar_tensor_tensor(out=bufs.picked[:], in0=bufs.wanted[:], scalar=bufs.balance[:, n % 2:n % 2 + 1], in1=bufs.next_best[:],
                                           op0=ALU.is_equal, op1=ALU.mult, accum_out=bufs.last_kept[:]).then_inc(last_ready, 1)

                def bound_it():
                    dve.wait_ge(last_ready, n + 1)
                    if n >= 2:
                        dve.wait_ge(checked, n - 1)
                    v.tensor_scalar(bufs.bound[:, n % 2:n % 2 + 1], bufs.last_kept[:], 2.0 ** -24 - 1.0, None, ALU.mult).then_inc(bound_ready, 1)

                return [take_below, pick_last, bound_it]

            def keep_output(h):
                dve.wait_ge(output_turned, h + 1)
                held = core.bank(7)[:, 0:OUT].rearrange("p (t s) -> p t s", s=slot)
                step(v.reciprocal(bufs.share[:, 0:NT], held[:, :, dh]))
                v.tensor_tensor(og[:, 0:NT, h * dh:(h + 1) * dh], held[:, :, 0:dh],
                                bufs.share[:, 0:NT].unsqueeze(2).to_broadcast([P, NT, dh]), ALU.mult).then_inc(out_kept, 1)

            for n in range(N + LAG + 1):
                if exact:
                    if n == 0:
                        all_taken()
                else:
                    if n == 0:
                        for i in range(len(segments)):
                            segment(0, i)
                        first_round(0)
                        keep_maximum(0)
                    if n < N:
                        split(n, selection(n - 2) if n >= 2 else [])
                    elif n <= N + 1:
                        for part in selection(n - 2):
                            part()
                if n in heads_out:
                    keep_output(heads_out[n])
            keep_output(HB - 1)
            dve.wait_ge(out_kept, HB)
            if exact:
                h, q = exact_tile
                step(v.tensor_copy(a.out[:, bass.ds(q, 1), bass.ds(h * dh, dh)], og[:]))
            else:
                dve.wait_ge(checked, N)
                wrong, wrong_heads = bufs.wrong[:, 0:N], bufs.wrong[:, N:N + HB]
                step(v.tensor_scalar(wrong, bufs.kept[:], float(2 * a.top - M_ + 1), None, ALU.is_gt))
                step(v.reduce_max(wrong_heads, wrong.rearrange("p (h q) -> p h q", q=TT), AX.X))
                step(v.reduce_max(bufs.wrong[:, N + HB:N + HB + 1], wrong_heads, AX.X))


def top_flag_stage(core, bufs):
    nc = core.nc
    n = bufs.wrong.shape[1]
    with stage(nc, "summed", "flag_ready") as (block, summed, flag_ready):
        @block.tensor
        def _(pe):
            nc.tensor.matmul(core.bank(0)[0:1, 0:n], core.ones[:, 0:1], bufs.wrong[:], start=True, stop=True).then_inc(summed, 1)

        @block.vector
        def _(dve):
            dve.wait_ge(summed, 1)
            nc.vector.tensor_copy(bufs.flags[:], core.bank(0)[0:1, 0:n]).then_inc(flag_ready, 1)
            dve.wait_ge(flag_ready, 1)


def top_attention(core, a):
    nc = core.nc
    KT = (a.keys + P - 1) // P
    H, dh = a.heads, a.dh
    (stack,) = STACKS[dh]
    stacked = len(stack) * dh
    N = H * TT
    with ExitStack() as ctx:
        sb = lambda name, shape, dt=F32: ctx.enter_context(nc.sbuf_tensor(core.named(name), shape, dt))
        bufs = TopBuffers(
            qs=sb("qs", [stacked, 1, H, S], BF16), ks=sb("ks", [stacked, 1, 6, a.keys], BF16), vg=sb("vg", [P, KT, 1, value_slot(dh)]),
            og=sb("og", [P, 1, dh]), exps=sb("exps", [P, 4, a.keys]), below=sb("below", [P, a.keys]), probs=sb("probs", [P, a.keys]),
            signs=sb("signs", [P, a.keys], BF16), probsT=sb("probsT", [P, KT, S]), output=sb("output", [P, P]),
            candidates=sb("candidates", [P, 2, BEST * len(segments_of(a.keys))]), first=sb("first", [P, 2, BEST]), edge=sb("edge", [P, 2, BEST]),
            next_best=sb("next_best", [P, BEST]), negmax=sb("negmax", [P, 2]), edge_exp=sb("edge_exp", [P, 2]), low=sb("low", [P, 2]),
            balance=sb("balance", [P, 2]), wanted=sb("wanted", [P, BEST]), bound=sb("bound", [P, 2]), last_kept=sb("last_kept", [P, 1]),
            picked=sb("picked", [P, BEST]), kept_signs=sb("kept_signs", [P, a.keys], BF16), kept=sb("kept", [P, N]),
            share=sb("share", [P, TT]), wrong=sb("wrong", [P, N + H + 1]), flags=sb("flags", [1, N + H + 1], I32))
        with stage(nc, "filled") as (block, filled):
            @block.vector
            def _(dve):
                for j in range(BEST):
                    nc.vector.memset(bufs.wanted[:, j:j + 1], a.keys - 2.0 * (a.top - (j + 1))).then_inc(filled, 1)
                dve.wait_ge(filled, BEST)
        top_attention_stage(core, a, bufs)
        top_flag_stage(core, bufs)
        flag = lambda i: nc.values_load(bufs.flags[0:1, i], min_val=0, max_val=P)
        with branch(nc, flag(slice(N + H, N + H + 1)) > 0):
            with loop(nc, H) as h:
                with branch(nc, flag(bass.ds(N + h, 1)) > 0):
                    with loop(nc, TT) as q:
                        with branch(nc, flag(bass.ds(h * TT + q, 1)) > 0):
                            top_attention_stage(core, a, bufs, exact_tile=(h, q))


def values_into(core, v, dh):
    nc = core.nc

    def evacuation(t, r):
        engine = ("act", "dve")[t % 2]
        to = v[0:r, t, :, 0:dh]

        def evacuate(bank):
            of = bank[0:r, 0:v.shape[2] * dh].rearrange("p (h s) -> p h s", s=dh)
            return nc.scalar.copy(to, of) if engine == "act" else nc.vector.tensor_copy(to, of)
        return engine, evacuate
    return evacuation


class Split:

    def __init__(self, core, ctx, **tiles):
        self.x, self.parts = {}, {}
        for name, (t, n) in tiles.items():
            self.x[name] = ctx.enter_context(core.nc.sbuf_tensor(core.named("whole_" + name), [P, t, n], F32))
            self.parts[name] = ctx.enter_context(core.nc.sbuf_tensor(core.named("parts_" + name), [P, PARTS, t, n], BF16))

    def store(self, core, **scratch):
        parts_stage(core, [(self.x[k], self.parts[k], scratch[k]) for k in scratch])


def all_blocks(keys):
    return lambda q: [(kt, None, None) for kt in range((keys + P - 1) // P)]


def causal_blocks(core):
    return lambda q: [(kt, None, None) for kt in range(q)] + [(q, core.causal16[:], core.causalT16[:])]


def inputs_stage(core, b, ctx_in, rows, ctxT):
    nc = core.nc
    PER_BANK = BANK // P
    chunks = [(t, min(PER_BANK, MT - t), kt_rows(M, min(t + PER_BANK, MT) - 1)) for t in range(0, MT, PER_BANK)]
    with stage(nc, *[f"context_{i}_loaded" for i in range(len(chunks))], "taken_by_dve", "taken_by_act", "turned_ready",
               "copied_by_act", "copied_by_dve") as (block, *sems):
        context_loaded = sems[:len(chunks)]
        taken_by_dve, taken_by_act, turned_ready, copied_by_act, copied_by_dve = sems[len(chunks):]
        half = TT // 2
        rows_of_x = lambda cut: core.x_all[:, bass.ds(b, 1), cut].rearrange("p o t d -> p (o t) d")
        banks = [(core.xT[:, f], S) for f in range(DT)]
        banks += [(ctxT[:, f, t * P:t * P + (n - 1) * P + r], (n - 1) * P + r) for t, n, r in chunks for f in range(DT)]

        @block.sync
        def _(sp):
            here = ctx_in[bass.ds(b, 1)]
            for (t, n, r), loaded in zip(chunks, context_loaded):
                if r == P:
                    sp.dma_start(rows[:, t:t + n], here[:, t * P:(t + n) * P].rearrange("o (t p) d -> p (o t) d", p=P)).then_inc(loaded, 16)
                else:
                    assert n == 1
                    sp.dma_start(rows[0:r, t], here[:, t * P:t * P + r].rearrange("o p d -> p (o d)")).then_inc(loaded, 16)

        def copy_out(engine, first, copy, copied):
            for i, (to, n) in enumerate(banks):
                if i % 2 == first:
                    engine.wait_ge(turned_ready, i + 1)
                    copy(to, core.bank(i)[:, 0:n]).then_inc(copied, 1)
            engine.wait_ge(copied, len(banks[first::2]))

        @block.vector
        def _(dve):
            nc.vector.tensor_copy(core.x[:, 0:half], rows_of_x(slice(0, half))).then_inc(taken_by_dve, 1)
            copy_out(dve, 1, nc.vector.tensor_copy, copied_by_dve)

        @block.scalar
        def _(act):
            nc.scalar.copy(core.x[:, half:TT], rows_of_x(slice(half, TT))).then_inc(taken_by_act, 1)
            copy_out(act, 0, nc.scalar.copy, copied_by_act)

        @block.tensor
        def _(pe):
            for f in range(DT):
                for t in range(TT):
                    if f == 0 and t == 0:
                        pe.wait_ge(taken_by_dve, 1)
                    if f == 0 and t == half:
                        pe.wait_ge(taken_by_act, 1)
                    last = nc.tensor.transpose(core.bank(f)[:, t * P:(t + 1) * P], core.x[:, t, f * P:(f + 1) * P], core.ident[:])
                last.then_inc(turned_ready, 1)
            for c, (t, n, r) in enumerate(chunks):
                pe.wait_ge(context_loaded[c], 16)
                for f in range(DT):
                    i = DT * (c + 1) + f
                    if i >= BANKS:
                        pe.wait_ge(copied_by_dve if i % 2 else copied_by_act, (i - BANKS) // 2 + 1)
                    for j in range(n):
                        m = kt_rows(M, t + j)
                        last = nc.tensor.transpose(core.bank(i)[:, j * P:j * P + m], rows[0:m, t + j, f * P:(f + 1) * P], core.ident[0:m, 0:m])
                    last.then_inc(turned_ready, 1)


def context_load(core, ctx_in, b, rows):
    nc = core.nc
    full = M // P
    with stage(nc, "context_loaded") as (block, context_loaded):
        @block.sync
        def _(sp):
            here = ctx_in[bass.ds(b, 1)]
            sp.dma_start(rows[:, 0:full], here[:, 0:full * P].rearrange("o (t p) d -> p (o t) d", p=P)).then_inc(context_loaded, 16)
            sp.dma_start(rows[0:M - full * P, full], here[:, full * P:M].rearrange("o p d -> p (o d)")).then_inc(context_loaded, 16)
            sp.wait_ge(context_loaded, 32)



def matrix(w, p=P):
    return w.rearrange("(k p) n -> p k n", p=p)


def l0_attn(core, w):
    nc = core.nc
    FF = w["L0_attn_ff_w1"].shape[1]
    STEPS, STEP, AT_ONCE = 8, 0.1, 4
    with ExitStack() as ctx:
        sb = lambda name, shape: ctx.enter_context(nc.sbuf_tensor(core.named(name), shape, F32))
        wq, wk, wv = sb("wq", [P, DT, D]), sb("wk", [P, DT, D]), sb("wv", [P, DT, D])
        bq, bk, bv = sb("bq", [P, DT]), sb("bk", [P, DT]), sb("bv", [1, D])
        wo, bo_col, bo_row = sb("wo", [P, DT, D]), sb("bo_col", [P, DT]), sb("bo_row", [1, D])
        gains = {k: sb(k, [P, DT]) for k in ("g_attn", "b_attn", "g1", "b1", "g2", "b2", "b_inl")}
        w_ctx, w_x = sb("w_ctx", [P, DT, D]), sb("w_x", [P, DT, D])
        ff1, ff1_b = sb("ff1", [P, DT, FF]), sb("ff1_b", [P, FF // P])
        ff2, ff2_b = sb("ff2", [P, FF // P, D]), sb("ff2_b", [1, D])
        qkv, qkv_b = w["L0_attn_qkv_w"], w["L0_attn_qkv_b"]
        v = sb("v", [P, TT, HEADS, value_slot(D // HEADS)])
        q_parts, k_parts = scratch_for(core, "q_parts", D, S), scratch_for(core, "k_parts", D, S)
        load_stage(core, [
            (wq[:], matrix(qkv[:, 0:D])), (wk[:], matrix(qkv[:, D:2 * D])), (wv[:], matrix(qkv[:, 2 * D:3 * D])),
            (bq[:], columned(qkv_b[0:D])), (bk[:], columned(qkv_b[D:2 * D])), (bv[:], rowed(qkv_b[2 * D:3 * D])),
            (wo[:], matrix(w["L0_attn_out_w"])), (bo_col[:], columned(w["L0_attn_out_b"])), (bo_row[:], rowed(w["L0_attn_out_b"])),
            *[(t[:], columned(w["L0_attn_" + k])) for k, t in gains.items()],
            (w_ctx[:], matrix(w["L0_attn_w_ctx"])), (w_x[:], matrix(w["L0_attn_w_x"])),
            (ff1[:], matrix(w["L0_attn_ff_w1"])), (ff1_b[:], columned(w["L0_attn_ff_b1"])),
            (ff2[:], matrix(w["L0_attn_ff_w2"])), (ff2_b[:], rowed(w["L0_attn_ff_b2"])),
        ], zeroed=[v[:, :, :, 17:]], ones=[v[:, :, :, 16]])

        y = sb("y", [P, TT, D])
        o, oT = sb("o", [P, TT, D]), sb("oT", [P, DT, S])
        attnT, drive = sb("attnT", [P, DT, S]), sb("drive", [P, DT, S])
        state, speed, rest, u = (sb(n, [P, DT, S]) for n in ("state", "speed", "rest", "u"))
        hT = sb("hT", [P, FF // P, S])
        heads = Heads(k_parts, q_parts, v, o, HEADS, HEADS, 16, S, 0.25, causal_blocks(core), lag=3.6)
        heads_buffers = attention_buffers(core, ctx, heads)
        with loop(nc, B) as b:
            take_stage(core, b)
            norm_stage(core, core.x[:], lambda t: y[:, t])
            product_stage(core, turned(core, y, core.xT, scale=gains["g_attn"], bias=gains["b_attn"]))
            with ExitStack() as early:
                split = Split(core, early, q=(DT, S), k=(DT, S))
                product_stage(core, [
                    *columns_out(core, wq, core.xT, split.x["q"], S, bias=bq), *columns_out(core, wk, core.xT, split.x["k"], S, bias=bk),
                    *rows_out(core, core.xT, wv, S, D, values_into(core, v, 16), bias_row=bv[:])])
                split.store(core, q=q_parts, k=k_parts)
            attention(core, heads, heads_buffers)
            product_stage(core, turned(core, o, oT))
            product_stage(core, [
                *columns_out(core, wo, oT, attnT, S, bias=bo_col),
                *rows_out(core, oT, wo, S, D, added_to(core, core.x, core.delta), bias_row=bo_row[:])])
            norm_stage(core, core.delta[:], lambda t: y[:, t])
            product_stage(core, [
                *turned(core, y, state, scale=gains["g1"], bias=gains["b1"]),
                *columns_out(core, w_ctx, attnT, drive, S, bias=gains["b_inl"])])
            with stage(nc, "rest_ready") as (block, rest_ready):
                @block.vector
                def _(dve):
                    nc.vector.tensor_scalar(rest[:], state[:], -1.0, None, ALU.mult).then_inc(rest_ready, 1)
                    dve.wait_ge(rest_ready, 1)
            with loop(nc, STEPS // AT_ONCE) as _i:
                recurrence_stage(core, w_x, drive, state, speed, rest, u, STEP, AT_ONCE)
            product_stage(core, turned_back(core, state, added_to(core, core.delta, core.delta)))
            norm_stage(core, core.delta[:], lambda t: y[:, t])
            product_stage(core, turned(core, y, core.xT, scale=gains["g2"], bias=gains["b2"]))
            product_stage(core, columns_out(core, ff1, core.xT, hT, S, bias=ff1_b, func=ACT.Gelu, engines=("act",)))
            product_stage(core, rows_out(core, hT, ff2, S, D, added_to(core, core.delta, core.delta), bias_row=ff2_b[:]))
            residual_norm(core, b)


def recurrence_stage(core, w_x, drive, state, speed, rest, u, step_size, steps):
    nc = core.nc
    CHUNKS = 2
    W = S // CHUNKS
    turns = [slice(c * W, (c + 1) * W) for _ in range(steps) for c in range(CHUNKS)]
    with stage(nc, "products_ready", "summed", "tanh_ready", "speed_ready", "state_ready", "damped", "rest_ready") as (
            block, products_ready, summed, tanh_ready, speed_ready, state_ready, damped, rest_ready):
        @block.tensor
        def _(pe):
            for i, cut in enumerate(turns):
                if i >= CHUNKS:
                    pe.wait_ge(state_ready, i - CHUNKS + 1)
                for f in range(DT):
                    last = accumulate(nc, core.bank(i % CHUNKS)[:, f * W:(f + 1) * W],
                                      [(w_x[:, k, f * P:(f + 1) * P], state[:, k, cut]) for k in range(DT)])
                last.then_inc(products_ready, 1)

        @block.vector
        def _(dve):
            v = nc.vector

            def update(i):
                cut = turns[i]
                dve.wait_ge(tanh_ready, i + 1)
                if i >= CHUNKS:
                    dve.wait_ge(rest_ready, i - CHUNKS + 1)
                v.tensor_tensor(speed[:, :, cut], u[:, :, cut], rest[:, :, cut], ALU.add).then_inc(speed_ready, 1)
                dve.wait_ge(speed_ready, i + 1)
                v.scalar_tensor_tensor(out=state[:, :, cut], in0=speed[:, :, cut], scalar=step_size * step_size, in1=state[:, :, cut],
                                       op0=ALU.mult, op1=ALU.add).then_inc(state_ready, 1)

            for i, cut in enumerate(turns):
                if i >= 1:
                    update(i - 1)
                dve.wait_ge(products_ready, i + 1)
                v.tensor_tensor(u[:, :, cut], core.bank(i % CHUNKS)[:, 0:DT * W].rearrange("p (f n) -> p f n", n=W),
                                drive[:, :, cut], ALU.add).then_inc(summed, 1)
            update(len(turns) - 1)

        @block.scalar
        def _(act):
            for i in range(len(turns) + 1):
                if i < len(turns):
                    cut = turns[i]
                    act.wait_ge(summed, i + 1)
                    nc.scalar.activation(u[:, :, cut], u[:, :, cut], ACT.Tanh).then_inc(tanh_ready, 1)
                if i >= 1:
                    cut = turns[i - 1]
                    act.wait_ge(speed_ready, i)
                    nc.scalar.activation(rest[:, :, cut], speed[:, :, cut], ACT.Copy, scale=1.0 - step_size).then_inc(damped, 1)

        @block.gpsimd
        def _(pool):
            for i, cut in enumerate(turns):
                pool.wait_ge(damped, i + 1)
                pool.wait_ge(state_ready, i + 1)
                pool.tensor_tensor(rest[:, :, cut], rest[:, :, cut], state[:, :, cut], ALU.subtract).then_inc(rest_ready, 1)


def l0_xattn(core, w, ctx_in):
    nc = core.nc
    INNER = w["L0_xattn_Wq"].shape[1]
    with ExitStack() as ctx:
        sb = lambda name, shape: ctx.enter_context(nc.sbuf_tensor(core.named(name), shape, F32))
        wq, wk, wv = (sb(n, [P, DT, INNER]) for n in ("wq", "wk", "wv"))
        v = sb("v", [P, MT, INNER // 64, 64])
        q_parts, k_parts = scratch_for(core, "q_parts", INNER, S), scratch_for(core, "k_parts", INNER, M)
        wo, bo = sb("wo", [P, INNER // P, D]), sb("bo", [1, D])
        load_stage(core, [(wq[:], matrix(w["L0_xattn_Wq"])), (wk[:], matrix(w["L0_xattn_Wk"])),
                          (wv[:], matrix(w["L0_xattn_Wv"])), (wo[:], matrix(w["L0_xattn_Wo"])),
                          (bo[:], rowed(w["L0_xattn_bo"]))])
        o = sb("o", [P, TT, INNER])
        with loop(nc, B) as b:
            with ExitStack() as early:
                ctxT = early.enter_context(nc.sbuf_tensor(core.named("ctxT"), [P, DT, M], F32))
                with ExitStack() as first:
                    inputs_stage(core, b, ctx_in, first.enter_context(nc.sbuf_tensor(core.named("ctx_rows"), [P, MT, D], F32)), ctxT)
                split = Split(core, early, q=(INNER // P, S), k=(INNER // P, M))
                product_stage(core, [
                    *columns_out(core, wq, core.xT, split.x["q"], S), *columns_out(core, wk, ctxT, split.x["k"], M),
                    *rows_out(core, ctxT, wv, M, INNER, values_into(core, v, 64))])
                split.store(core, q=q_parts, k=k_parts)
            attention(core, Heads(k_parts, q_parts, v, o, INNER // 64, 8, 64, M, 64 ** -0.5, all_blocks(M)))
            with ExitStack() as late:
                oT = late.enter_context(nc.sbuf_tensor(core.named("oT"), [P, INNER // P, S], F32))
                product_stage(core, turned(core, o, oT, features=INNER // P))
                product_stage(core, rows_out(core, oT, wo, S, D, into(core, core.delta), bias_row=bo[:]))
            residual_norm(core, b)


def l0_ffn(core, w):
    nc = core.nc
    with ExitStack() as ctx:
        sb = lambda name, shape, dt=F32: ctx.enter_context(nc.sbuf_tensor(core.named(name), shape, dt))
        packed, codes = sb("packed", [64, D], I32), sb("codes", [64, 4, D], I32)
        ternary, wT = sb("ternary", [64, 4, D]), sb("wT", [P, DT, D])
        scale, bias = sb("scale", [P, 1]), sb("bias", [P, D])
        load_stage(core, [(packed[:], w["L0_ffn_packed_weight"].rearrange("(r c) -> r c", c=D)),
                          (scale[:], spread_over(w["L0_ffn_weight_scale"])), (bias[:], spread_over(w["L0_ffn_bias"]))])
        with stage(nc, "dve_step") as (block, dve_step):
            @block.vector
            def _(dve):
                step = stepper(dve, dve_step)
                for s in range(4):
                    step(nc.vector.tensor_scalar(codes[:, s], packed[:], 2 * s, 3, ALU.logical_shift_right, ALU.bitwise_and))
                step(nc.vector.tensor_copy(ternary[:], codes[:]))
                step(nc.vector.tensor_scalar(ternary[:], ternary[:], 1.0, None, ALU.subtract))

        def turn(f):
            def multiply(bank):
                for s in range(4):
                    last = nc.tensor.transpose(bank[:, 64 * s:64 * s + 64], ternary[:, s, f * P:(f + 1) * P], core.ident[0:64, 0:64])
                return last
            return multiply

        product_stage(core, [Job(turn(f), "dve", out_of_bank(core, "dve", wT[:, f])) for f in range(DT)])
        xq = sb("xq", [P, TT, D])
        peak, gain, back = sb("peak", [P, TT]), sb("gain", [P, TT]), sb("back", [P, TT])
        with loop(nc, B) as b:
            take_stage(core, b)
            with stage(nc, "dve_step") as (block, dve_step):
                @block.vector
                def _(dve):
                    step = stepper(dve, dve_step)
                    step(nc.vector.tensor_reduce(peak[:], core.x[:], AX.X, ALU.max, apply_absolute_value=True))
                    step(nc.vector.tensor_scalar(peak[:], peak[:], 1e-5, None, ALU.max))
                    step(nc.vector.reciprocal(gain[:], peak[:]))
                    step(nc.vector.tensor_scalar(gain[:], gain[:], 127.0, None, ALU.mult))
                    step(nc.vector.reciprocal(back[:], gain[:]))
                    for t in range(TT):
                        step(nc.vector.tensor_scalar(xq[:, t], core.x[:, t], gain[:, t:t + 1], None, ALU.mult))
                    step(nc.vector.tensor_scalar(xq[:], xq[:], ROUND, None, ALU.add))
                    step(nc.vector.tensor_scalar(xq[:], xq[:], ROUND, None, ALU.subtract))
                    step(nc.vector.tensor_scalar(xq[:], xq[:], -128.0, 127.0, ALU.max, ALU.min))
                    for t in range(TT):
                        step(nc.vector.tensor_scalar(xq[:, t], xq[:, t], back[:, t:t + 1], None, ALU.mult))
            product_stage(core, turned(core, xq, core.xT))
            product_stage(core, rows_out(core, core.xT, wT, S, D, lambda t, r: ("dve", lambda bank: (
                nc.vector.scalar_tensor_tensor(out=core.delta[:, t], in0=bank[:, 0:D], scalar=scale[:, 0:1], in1=bias[:],
                                               op0=ALU.mult, op1=ALU.add)))))
            residual_norm(core, b)


def l1_attn(core, w):
    nc = core.nc
    C = w["L1_attn_W_dq"].shape[1]
    with ExitStack() as ctx:
        sb = lambda name, shape: ctx.enter_context(nc.sbuf_tensor(core.named(name), shape, F32))
        w_dq, w_dkv = sb("w_dq", [P, DT, C]), sb("w_dkv", [P, DT, C])
        w_uq, w_uk, w_uv = sb("w_uq", [C, 1, D]), sb("w_uk", [C, 1, D]), sb("w_uv", [C, 1, D])
        v = sb("v", [P, TT, HEADS, value_slot(D // HEADS)])
        q_parts, k_parts = scratch_for(core, "q_parts", D, S), scratch_for(core, "k_parts", D, S)
        wo = sb("wo", [P, DT, D])
        load_stage(core, [
            (w_dq[:], matrix(w["L1_attn_W_dq"])), (w_dkv[:], matrix(w["L1_attn_W_dkv"])),
            (w_uq[:], matrix(w["L1_attn_W_uq"], C)), (w_uk[:], matrix(w["L1_attn_W_uk"], C)),
            (w_uv[:], matrix(w["L1_attn_W_uv"], C)), (wo[:], matrix(w["L1_attn_W_o"])),
        ], zeroed=[v[:, :, :, 17:]], ones=[v[:, :, :, 16]])
        cqT, ckvT = sb("cqT", [C, 1, S]), sb("ckvT", [C, 1, S])
        o, oT = sb("o", [P, TT, D]), sb("oT", [P, DT, S])
        heads = Heads(k_parts, q_parts, v, o, HEADS, HEADS, 16, S, 0.25, causal_blocks(core), lag=3.6)
        heads_buffers = attention_buffers(core, ctx, heads)
        with loop(nc, B) as b:
            take_turned_stage(core, b)
            product_stage(core, [*columns_out(core, w_dq, core.xT, cqT, S, m=C), *columns_out(core, w_dkv, core.xT, ckvT, S, m=C)])
            with ExitStack() as early:
                split = Split(core, early, q=(DT, S), k=(DT, S))
                product_stage(core, [*columns_out(core, w_uq, cqT, split.x["q"], S), *columns_out(core, w_uk, ckvT, split.x["k"], S),
                                     *rows_out(core, ckvT, w_uv, S, D, values_into(core, v, 16))])
                split.store(core, q=q_parts, k=k_parts)
            attention(core, heads, heads_buffers)
            product_stage(core, turned(core, o, oT))
            product_stage(core, rows_out(core, oT, wo, S, D, into(core, core.delta)))
            residual_norm(core, b)


def l1_xattn(core, w, ctx_in):
    nc = core.nc
    R = w["L1_xattn_Uq"].shape[1]
    assert R == P
    with ExitStack() as ctx:
        sb = lambda name, shape: ctx.enter_context(nc.sbuf_tensor(core.named(name), shape, F32))
        up = {k: sb("up_" + k, [P, DT, R]) for k in "qkvo"}
        down = {k: sb("down_" + k, [R, 1, D]) for k in "qkvo"}
        bq, bk, bv, bo = sb("bq", [P, DT]), sb("bk", [P, DT]), sb("bv", [1, D]), sb("bo", [1, D])
        v, o = sb("v", [P, MT, HEADS, value_slot(16)]), sb("o", [P, TT, D])
        with ExitStack() as early:
            V = {k: early.enter_context(nc.sbuf_tensor(core.named("V" + k), [P, DT, R], F32)) for k in "qkvo"}
            load_stage(core, [
                *[(up[k][:], matrix(w["L1_xattn_U" + k])) for k in "qkvo"], *[(V[k][:], matrix(w["L1_xattn_V" + k])) for k in "qkvo"],
                (bq[:], columned(w["L1_xattn_bq"])), (bk[:], columned(w["L1_xattn_bk"])),
                (bv[:], rowed(w["L1_xattn_bv"])), (bo[:], rowed(w["L1_xattn_bo"])),
            ], zeroed=[v[:, :, :, 17:]], ones=[v[:, :, :, 16]])

            def turn(k):
                def multiply(bank):
                    for f in range(DT):
                        last = nc.tensor.transpose(bank[:, f * P:(f + 1) * P], V[k][:, f], core.ident[:])
                    return last

                return Job(multiply, "dve", lambda bank: nc.vector.tensor_copy(down[k][:, 0], bank[:, 0:D]))

            product_stage(core, [turn(k) for k in "qkvo"])
        q_parts, k_parts = scratch_for(core, "q_parts", D, S), scratch_for(core, "k_parts", D, M)
        with loop(nc, B) as b:
            with ExitStack() as early:
                split = Split(core, early, q=(DT, S), k=(DT, M))
                ctxT = early.enter_context(nc.sbuf_tensor(core.named("ctxT"), [P, DT, M], F32))
                low_q, low_k, low_v = (early.enter_context(nc.sbuf_tensor(core.named("low_" + k), [P, 1, S if k == "q" else M], F32)) for k in "qkv")
                with ExitStack() as first:
                    inputs_stage(core, b, ctx_in, first.enter_context(nc.sbuf_tensor(core.named("ctx_rows"), [P, MT, D], F32)), ctxT)
                product_stage(core, [*columns_out(core, up["q"], core.xT, low_q, S),
                                     *columns_out(core, up["k"], ctxT, low_k, M), *columns_out(core, up["v"], ctxT, low_v, M)])
                product_stage(core, [*columns_out(core, down["q"], low_q, split.x["q"], S, bias=bq),
                                     *columns_out(core, down["k"], low_k, split.x["k"], M, bias=bk),
                                     *rows_out(core, low_v, down["v"], M, D, values_into(core, v, 16), bias_row=bv[:])])
                split.store(core, q=q_parts, k=k_parts)
            top_attention(core, Heads(k_parts, q_parts, v, o, HEADS, HEADS, 16, M, 0.25, all_blocks(M), top=64))
            with ExitStack() as late:
                oT, low_o = (late.enter_context(nc.sbuf_tensor(core.named(n), [P, k, S], F32)) for n, k in (("oT", DT), ("low_o", 1)))
                product_stage(core, turned(core, o, oT))
                product_stage(core, columns_out(core, up["o"], oT, low_o, S))
                product_stage(core, rows_out(core, low_o, down["o"], S, D, into(core, core.delta), bias_row=bo[:]))
            residual_norm(core, b)


def first_of_equal(nc, step, onehot, values, best, ties, counted, ones):
    rows, n = values.shape[1], values.shape[2]
    step(nc.vector.tensor_tensor(ties, values, best.unsqueeze(2).to_broadcast([values.shape[0], rows, n]), ALU.is_equal))
    for t in range(rows):
        step(nc.vector.tensor_tensor_scan(counted[:, t], ties[:, t], ones, 0.0, ALU.add, ALU.mult))
    step(nc.vector.scalar_tensor_tensor(out=onehot, in0=counted, scalar=1.0, in1=ties, op0=ALU.is_equal, op1=ALU.mult))


def l1_ffn(core, w):
    nc = core.nc
    E, _, H = w["L1_ffn_W1"].shape
    HT = H // P
    with ExitStack() as ctx:
        sb = lambda name, shape: ctx.enter_context(nc.sbuf_tensor(core.named(name), shape, F32))
        wg, bg = sb("wg", [P, DT, E]), sb("bg", [1, E])
        w1, b1 = sb("w1", [P, E, DT, H]), sb("b1", [P, E, HT])
        w2, b2 = sb("w2", [P, E, HT, D]), sb("b2", [E, D])
        load_stage(core, [
            (wg[:], matrix(w["L1_ffn_Wg"])), (bg[:], rowed(w["L1_ffn_bg"])), (b2[:], w["L1_ffn_b2"]),
            *[(w1[:, e], matrix(w["L1_ffn_W1"][e])) for e in range(E)], *[(w2[:, e], matrix(w["L1_ffn_W2"][e])) for e in range(E)],
            *[(b1[:, e], columned(w["L1_ffn_b1"][e])) for e in range(E)]])
        logits, ties, counted = (sb(n, [P, TT, E]) for n in ("logits", "ties", "counted"))
        first, second, mix = (sb(n, [P, TT, E]) for n in ("first", "second", "mix"))
        top1, top2, ratio = (sb(n, [P, TT]) for n in ("top1", "top2", "ratio"))
        mixT, hT = sb("mixT", [E, S]), sb("hT", [P, 2, HT, S])
        with loop(nc, B) as b:
            take_turned_stage(core, b)
            product_stage(core, rows_out(core, core.xT, wg, S, E, into(core, logits), bias_row=bg[:]))
            with stage(nc, "dve_step", "gap_ready", "ratio_ready") as (block, dve_step, gap_ready, ratio_ready):
                @block.vector
                def _(dve):
                    step = stepper(dve, dve_step)
                    step(nc.vector.reduce_max(top1[:], logits[:], AX.X))
                    first_of_equal(nc, step, first[:], logits[:], top1[:], ties[:], counted[:], core.ones[:, 0:E])
                    step(nc.vector.scalar_tensor_tensor(out=logits[:], in0=first[:], scalar=MASKED, in1=logits[:], op0=ALU.mult, op1=ALU.add))
                    step(nc.vector.reduce_max(top2[:], logits[:], AX.X))
                    first_of_equal(nc, step, second[:], logits[:], top2[:], ties[:], counted[:], core.ones[:, 0:E])
                    nc.vector.tensor_tensor(ratio[:], top2[:], top1[:], ALU.subtract).then_inc(gap_ready, 1)
                    dve.wait_ge(ratio_ready, 1)
                    step(nc.vector.tensor_scalar(top1[:], ratio[:], 1.0, None, ALU.add))
                    step(nc.vector.reciprocal(top1[:], top1[:]))
                    step(nc.vector.tensor_tensor(top2[:], ratio[:], top1[:], ALU.mult))
                    step(nc.vector.tensor_tensor(first[:], first[:], top1[:].unsqueeze(2).to_broadcast([P, TT, E]), ALU.mult))
                    step(nc.vector.tensor_tensor(second[:], second[:], top2[:].unsqueeze(2).to_broadcast([P, TT, E]), ALU.mult))
                    step(nc.vector.tensor_tensor(mix[:], first[:], second[:], ALU.add))

                @block.scalar
                def _(act):
                    act.wait_ge(gap_ready, 1)
                    nc.scalar.activation(ratio[:], ratio[:], ACT.Exp).then_inc(ratio_ready, 1)

            def turn_mix(bank):
                for t in range(TT):
                    last = nc.tensor.transpose(bank[0:E, t * P:(t + 1) * P], mix[:, t], core.ident[:])
                return last

            product_stage(core, [Job(turn_mix, "dve", out_of_bank(core, "dve", mixT[:]))])
            experts_stage(core, w1, b1, w2, b2, mix, mixT, hT)
            residual_norm(core, b)


def experts_stage(core, w1, b1, w2, b2, mix, mixT, hT):
    nc = core.nc
    E, HT = w1.shape[1], hT.shape[2]
    with stage(nc, "hidden_products", "hidden_ready", "out_products", "summed") as (
            block, hidden_products, hidden_ready, out_products, summed):
        @block.tensor
        def _(pe):
            for t in range(TT):
                nc.tensor.matmul(core.bank(4 + t)[:, 0:D], mixT[:, t * P:(t + 1) * P], b2[:], start=True, stop=True).then_inc(out_products, 1)

            def hidden(e):
                for h in range(HT):
                    if e >= 1:
                        pe.wait_ge(hidden_ready, HT * (e - 1) + h + 1)
                    accumulate(nc, core.bank(h), [(w1[:, e, k, h * P:(h + 1) * P], core.xT[:, k]) for k in range(DT)]
                               ).then_inc(hidden_products, 1)

            def output(e):
                pe.wait_ge(hidden_ready, HT * (e + 1))
                for t in range(TT):
                    pe.wait_ge(summed, TT * e + t + 1)
                    accumulate(nc, core.bank(4 + t)[:, 0:D], [(hT[:, e % 2, h, t * P:(t + 1) * P], w2[:, e, h]) for h in range(HT)]
                               ).then_inc(out_products, 1)

            hidden(0)
            for e in range(E):
                if e + 1 < E:
                    hidden(e + 1)
                output(e)

        @block.scalar
        def _(act):
            for e in range(E):
                for h in range(HT):
                    act.wait_ge(hidden_products, HT * e + h + 1)
                    if e >= 2:
                        act.wait_ge(out_products, TT * e)
                    nc.scalar.activation(hT[:, e % 2, h], core.bank(h), ACT.Gelu, bias=b1[:, e, h:h + 1]).then_inc(hidden_ready, 1)

        @block.vector
        def _(dve):
            for t in range(TT):
                dve.wait_ge(out_products, t + 1)
                nc.vector.tensor_copy(core.delta[:, t], core.bank(4 + t)[:, 0:D]).then_inc(summed, 1)
            for e in range(E):
                for t in range(TT):
                    dve.wait_ge(out_products, TT * (e + 1) + t + 1)
                    dve.wait_ge(summed, TT * e + t + 1)
                    nc.vector.scalar_tensor_tensor(out=core.delta[:, t], in0=core.bank(4 + t)[:, 0:D], scalar=mix[:, t, e:e + 1],
                                                   in1=core.delta[:, t], op0=ALU.mult, op1=ALU.add).then_inc(summed, 1)


def l2_attn(core, w):
    nc = core.nc
    NS = w["L2_attn_B"].shape[0]
    K = 9
    TWO_PI_HI, TWO_PI_MID, TWO_PI_LO = 6.28125, 0.0019350051879882812, 3.0199159819567e-07
    with ExitStack() as ctx:
        sb = lambda name, shape: ctx.enter_context(nc.sbuf_tensor(core.named(name), shape, F32))
        cosT, sinT, drive, decay = (sb(n, [P, S]) for n in ("cosT", "sinT", "drive", "decay"))
        inT, outP, outQ = sb("inT", [P, DT, P]), sb("outP", [P, D]), sb("outQ", [P, D])
        skip = sb("skip", [P, D])
        with ExitStack() as early:
            eb = lambda name, shape: early.enter_context(nc.sbuf_tensor(core.named(name), shape, F32))
            lar, aim, ls = eb("lar", [P, 1]), eb("aim", [P, 1]), eb("ls", [P, 1])
            b_rows, c_rows, c_sorted = eb("b_rows", [NS, D]), eb("c_rows", [P, DT, NS, 2]), eb("c_sorted", [P, DT, 2, P])
            la, ai = w["L2_attn_log_A_real"].rearrange("(n o) -> n o", o=1), w["L2_attn_A_imag"].rearrange("(n o) -> n o", o=1)
            load_stage(core, [
                (lar[0:NS], la), (lar[NS:P], la), (aim[0:NS], ai), (aim[NS:P], ai), (ls[:], spread_over(w["L2_attn_log_step"])),
                (b_rows[:], w["L2_attn_B"]), (skip[:], spread_over(w["L2_attn_D"])),
                *[(c_rows[:, t], w["L2_attn_C"][t * P:(t + 1) * P]) for t in range(DT)]])
            dt_, are, r, angle, turns, half = eb("dt", [P, 1]), eb("are", [P, 1]), eb("r", [P, 1]), eb("angle", [P, K]), eb("turns", [P, K]), eb("half", [P, K])
            cosK, sinK = eb("cosK", [P, K]), eb("sinK", [P, K])
            nr, ni, den, cr, ci, t0, ga, gb = (eb(n, [P, 1]) for n in ("nr", "ni", "den", "cr", "ci", "t0", "ga", "gb"))
            tmp = eb("tmp", [P, S])
            with stage(nc, "dve_step", "act_step", "product_ready", "angle_ready", "sines_ready") as (
                    block, dve_step, act_step, product_ready, angle_ready, sines_ready):
                @block.scalar
                def _(act):
                    step = stepper(act, act_step)
                    step(nc.scalar.activation(dt_[:], ls[:], ACT.Exp))
                    step(nc.scalar.activation(are[:], lar[:], ACT.Exp))
                    act.wait_ge(product_ready, 1)
                    nc.scalar.activation(r[:], r[:], ACT.Exp).then_inc(sines_ready, 1)
                    act.wait_ge(angle_ready, 1)
                    nc.scalar.activation(sinK[:], angle[:], ACT.Sin).then_inc(sines_ready, 1)
                    nc.scalar.activation(half[:], half[:], ACT.Sin).then_inc(sines_ready, 1)

                @block.vector
                def _(dve):
                    v = nc.vector
                    step = stepper(dve, dve_step)
                    dve.wait_ge(act_step, 2)
                    step(v.tensor_scalar(are[:], are[:], -1.0, None, ALU.mult))
                    v.tensor_tensor(r[:], are[:], dt_[:], ALU.mult).then_inc(product_ready, 1)
                    step(v.tensor_tensor(angle[:, 0:1], aim[:], dt_[:], ALU.mult))
                    for k in range(1, K):
                        step(v.tensor_scalar(angle[:, k:k + 1], angle[:, k - 1:k], 2.0, None, ALU.mult))
                    step(v.tensor_scalar(turns[:], angle[:], 0.15915494309189535, None, ALU.mult))
                    step(v.tensor_scalar(turns[:], turns[:], ROUND, None, ALU.add))
                    step(v.tensor_scalar(turns[:], turns[:], ROUND, None, ALU.subtract))
                    for part in (TWO_PI_HI, TWO_PI_MID, TWO_PI_LO):
                        step(v.scalar_tensor_tensor(out=angle[:], in0=turns[:], scalar=-part, in1=angle[:], op0=ALU.mult, op1=ALU.add))
                    step(v.tensor_scalar(angle[:], angle[:], -3.1415925, 3.1415925, ALU.max, ALU.min))
                    v.tensor_scalar(half[:], angle[:], 0.5, None, ALU.mult).then_inc(angle_ready, 1)
                    dve.wait_ge(sines_ready, 3)
                    step(v.tensor_tensor(cosK[:], half[:], half[:], ALU.mult))
                    step(v.tensor_scalar(cosK[:], cosK[:], -2.0, 1.0, ALU.mult, ALU.add))
                    step(v.tensor_tensor(nr[:], r[:], cosK[:, 0:1], ALU.mult))
                    step(v.tensor_scalar(nr[:], nr[:], -1.0, None, ALU.add))
                    step(v.tensor_tensor(ni[:], r[:], sinK[:, 0:1], ALU.mult))
                    step(v.tensor_tensor(den[:], are[:], are[:], ALU.mult))
                    step(v.tensor_tensor(t0[:], aim[:], aim[:], ALU.mult))
                    step(v.tensor_tensor(den[:], den[:], t0[:], ALU.add))
                    step(v.reciprocal(den[:], den[:]))
                    step(v.tensor_tensor(cr[:], nr[:], are[:], ALU.mult))
                    step(v.scalar_tensor_tensor(out=cr[:], in0=ni[:], scalar=aim[:, 0:1], in1=cr[:], op0=ALU.mult, op1=ALU.add))
                    step(v.tensor_tensor(cr[:], cr[:], den[:], ALU.mult))
                    step(v.tensor_tensor(t0[:], nr[:], aim[:], ALU.mult))
                    step(v.scalar_tensor_tensor(out=ci[:], in0=ni[:], scalar=are[:, 0:1], in1=t0[:], op0=ALU.mult, op1=ALU.subtract))
                    step(v.tensor_tensor(ci[:], ci[:], den[:], ALU.mult))
                    step(v.memset(cosT[:, 0:1], 1.0))
                    step(v.memset(sinT[:, 0:1], 0.0))
                    for k in range(K):
                        n = 1 << k
                        for to, a, bb, op in ((cosT, cosT, sinT, ALU.subtract), (sinT, sinT, cosT, ALU.add)):
                            step(v.tensor_scalar(tmp[:, 0:n], bb[:, 0:n], sinK[:, k:k + 1], None, ALU.mult))
                            step(v.scalar_tensor_tensor(out=to[:, n:2 * n], in0=a[:, 0:n], scalar=cosK[:, k:k + 1], in1=tmp[:, 0:n],
                                                        op0=ALU.mult, op1=op))
                    step(v.tensor_copy(ga[0:NS], cr[0:NS]))
                    step(v.tensor_copy(ga[NS:P], ci[NS:P]))
                    step(v.tensor_copy(gb[0:NS], ci[0:NS]))
                    step(v.tensor_scalar(gb[NS:P], cr[NS:P], -1.0, None, ALU.mult))
                    step(v.tensor_scalar(tmp[:], sinT[:], gb[:, 0:1], None, ALU.mult))
                    step(v.scalar_tensor_tensor(out=drive[:], in0=cosT[:], scalar=ga[:, 0:1], in1=tmp[:], op0=ALU.mult, op1=ALU.add))
                    step(v.tensor_scalar(decay[:], core.ones[:], r[:, 0:1], None, ALU.mult))
                    for t in range(DT):
                        step(v.tensor_copy(c_sorted[:, t, 0, 0:NS], c_rows[:, t, :, 0]))
                        step(v.tensor_scalar(c_sorted[:, t, 0, NS:P], c_rows[:, t, :, 1], -1.0, None, ALU.mult))
                        step(v.tensor_scalar(c_sorted[:, t, 1, 0:NS], c_rows[:, t, :, 1], -1.0, None, ALU.mult))
                        step(v.tensor_scalar(c_sorted[:, t, 1, NS:P], c_rows[:, t, :, 0], -1.0, None, ALU.mult))

            def turn_b(bank):
                for f in range(DT):
                    for half_ in range(2):
                        last = nc.tensor.transpose(bank[:, f * P + half_ * NS:f * P + half_ * NS + NS], b_rows[:, f * P:(f + 1) * P], core.ident[0:NS, 0:NS])
                return last

            def turn_c(i):
                def multiply(bank):
                    for t in range(DT):
                        last = nc.tensor.transpose(bank[:, t * P:(t + 1) * P], c_sorted[:, t, i], core.ident[:])
                    return last
                return multiply

            product_stage(core, [Job(turn_b, "dve", out_of_bank(core, "dve", inT[:].rearrange("p k n -> p (k n)"))),
                                 Job(turn_c(0), "act", out_of_bank(core, "act", outP[:])), Job(turn_c(1), "dve", out_of_bank(core, "dve", outQ[:]))])
        z, zc, zs = sb("z", [P, S]), sb("zc", [P, S]), sb("zs", [P, S])
        with loop(nc, B) as b:
            take_turned_stage(core, b)
            with stage(nc, "drive_product", "dve_step", "state_ready", "out_products") as (
                    block, drive_product, dve_step, state_ready, out_products):
                @block.tensor
                def _(pe):
                    accumulate(nc, core.bank(0), [(inT[:, k], core.xT[:, k]) for k in range(DT)]).then_inc(drive_product, 1)
                    pe.wait_ge(state_ready, 1)
                    for t in range(TT):
                        cut = slice(t * P, (t + 1) * P)
                        accumulate(nc, core.bank(1 + t)[:, 0:D], [(zc[:, cut], outP[:]), (zs[:, cut], outQ[:])]).then_inc(out_products, 1)

                @block.vector
                def _(dve):
                    v = nc.vector
                    step = stepper(dve, dve_step)
                    dve.wait_ge(drive_product, 1)
                    step(v.tensor_tensor(zc[:], core.bank(0), drive[:], ALU.mult))
                    step(v.tensor_tensor_scan(z[:], decay[:], zc[:], 0.0, ALU.mult, ALU.add))
                    step(v.tensor_tensor(zc[:], z[:], cosT[:], ALU.mult))
                    v.tensor_tensor(zs[:], z[:], sinT[:], ALU.mult).then_inc(state_ready, 1)
                    for t in range(TT):
                        step(v.tensor_tensor(core.delta[:, t], core.x[:, t], skip[:], ALU.mult))
                    for t in range(TT):
                        dve.wait_ge(out_products, t + 1)
                        step(v.tensor_tensor(core.delta[:, t], core.bank(1 + t)[:, 0:D], core.delta[:, t], ALU.add))
            residual_norm(core, b)


def turn_square(core, source, to, rows_tiles, cols_tiles):
    nc = core.nc
    jobs = []
    for c in range(cols_tiles):
        def multiply(bank, c=c):
            for r in range(rows_tiles):
                last = nc.tensor.transpose(bank[:, r * P:(r + 1) * P], source[:, r, c * P:(c + 1) * P], core.ident[:])
            return last
        jobs.append(Job(multiply, "dve", out_of_bank(core, "dve", to[:, c, 0:rows_tiles * P])))
    return jobs


def l2_xattn(core, w, ctx_in):
    nc = core.nc
    with ExitStack() as ctx:
        sb = lambda name, shape: ctx.enter_context(nc.sbuf_tensor(core.named(name), shape, F32))
        wr, wT, bias = sb("wr", [P, DT, 2 * D]), sb("wT", [P, 2 * DT, D]), sb("bias", [1, D])
        load_stage(core, [(wr[:], matrix(w["L2_xattn_W"])), (bias[:], rowed(w["L2_xattn_b"]))])
        product_stage(core, turn_square(core, wr, wT, DT, 2 * DT))
        rows, mean, pooled = sb("rows", [P, MT, D]), sb("mean", [P, DT]), sb("pooled", [1, D])
        with loop(nc, B) as b:
            take_stage(core, b)
            context_load(core, ctx_in, b, rows)

            def sums(bank):
                for f in range(DT):
                    last = accumulate(nc, bank[:, f:f + 1], [(rows[0:kt_rows(M, t), t, f * P:(f + 1) * P], core.ones[0:kt_rows(M, t), 0:1]) for t in range(MT)])
                return last

            product_stage(core, [*turned(core, core.x, core.xT), Job(sums, "dve", lambda bank: nc.vector.tensor_scalar(
                mean[:], bank[:, 0:DT], 1.0 / M, None, ALU.mult))])
            product_stage(core, [Job(lambda bank: accumulate(nc, bank[0:1, 0:D], [(mean[:, k:k + 1], wT[:, DT + k]) for k in range(DT)]), "dve",
                                     lambda bank: nc.vector.tensor_tensor(pooled[:], bank[0:1, 0:D], bias[:], ALU.add))])
            product_stage(core, rows_out(core, core.xT, wT[:, 0:DT], S, D, into(core, core.delta), bias_row=pooled[:]))
            residual_norm(core, b)


def l2_ffn(core, w):
    nc = core.nc
    E, _, R = w["L2_ffn_down_W"].shape
    with ExitStack() as ctx:
        sb = lambda name, shape: ctx.enter_context(nc.sbuf_tensor(core.named(name), shape, F32))
        base, baseT, base_b = sb("base", [P, DT, D]), sb("baseT", [P, DT, D]), sb("base_b", [1, D])
        mu, iv, muiv, mu2iv = (sb(n, [P, DT, E]) for n in ("mu", "iv", "muiv", "mu2iv"))
        down, up, conv = sb("down", [P, E, DT, R]), sb("up", [R, E, D]), sb("conv", [P, E, DT, D])
        down_b, up_b, conv_b = sb("down_b", [E, R]), sb("up_b", [E, D]), sb("conv_b", [E, D])
        by_feature = lambda v: v.rearrange("e (k p) -> p k e", p=P)
        with nc.allow_non_contiguous_dma("small tables of the experts' statistics"):
            load_stage(core, [
                (base[:], matrix(w["L2_ffn_base_W"])), (base_b[:], rowed(w["L2_ffn_base_b"])),
                *[(mu[:, k], by_feature(w["L2_ffn_disc_mu"])[:, k]) for k in range(DT)],
                *[(iv[:, k], by_feature(w["L2_ffn_disc_sigma"])[:, k]) for k in range(DT)],
                *[(down[:, e], matrix(w["L2_ffn_down_W"][e])) for e in range(E)], (up[:], w["L2_ffn_up_W"].rearrange("e r d -> r e d")),
                *[(conv[:, e], matrix(w["L2_ffn_conv_W"][e])) for e in range(E)],
                (down_b[:], w["L2_ffn_down_b"]), (up_b[:], w["L2_ffn_up_b"]), (conv_b[:], w["L2_ffn_conv_b"])])
        with stage(nc, "dve_step") as (block, dve_step):
            @block.vector
            def _(dve):
                v = nc.vector
                step = stepper(dve, dve_step)
                step(v.tensor_tensor(iv[:], iv[:], iv[:], ALU.mult))
                step(v.reciprocal(iv[:], iv[:]))
                step(v.tensor_tensor(muiv[:], mu[:], iv[:], ALU.mult))
                step(v.tensor_tensor(mu2iv[:], mu[:], muiv[:], ALU.mult))
                step(v.tensor_scalar(muiv[:], muiv[:], -2.0, None, ALU.mult))
        product_stage(core, turn_square(core, base, baseT, DT, DT))
        m1, m2, square = sb("m1", [P, DT]), sb("m2", [P, DT]), sb("square", [P, DT, S])
        loss, least, ties, counted, pick = sb("loss", [1, 1, E]), sb("least", [1, 1]), sb("ties", [1, 1, E]), sb("counted", [1, 1, E]), sb("pick", [1, 1, E])
        everywhere, picked = sb("everywhere", [P, E]), sb("picked", [E, 1])
        wd, wu, wc, wcT = sb("wd", [P, DT, R]), sb("wu", [R, 1, D]), sb("wc", [P, DT, D]), sb("wcT", [P, DT, D])
        bd, bu, bc = sb("bd", [R, 1]), sb("bu", [P, DT]), sb("bc", [1, D])
        hT, aT = sb("hT", [R, 1, S]), sb("aT", [P, DT, S])
        with loop(nc, B) as b:
            take_turned_stage(core, b)
            with stage(nc, "dve_step", "act_step") as (block, dve_step, act_step):
                @block.vector
                def _(dve):
                    step = stepper(dve, dve_step)
                    step(nc.vector.reduce_sum(m1[:], core.xT[:], AX.X))
                    step(nc.vector.tensor_scalar(m1[:], m1[:], 1.0 / S, None, ALU.mult))
                    dve.wait_ge(act_step, DT)
                    step(nc.vector.tensor_scalar(m2[:], m2[:], 1.0 / S, None, ALU.mult))

                @block.scalar
                def _(act):
                    step = stepper(act, act_step)
                    for f in range(DT):
                        step(nc.scalar.activation(square[:, f], core.xT[:, f], ACT.Square, accum_out=m2[:, f:f + 1]))

            def losses(bank):
                terms = []
                for k in range(DT):
                    terms += [(m2[:, k:k + 1], iv[:, k]), (m1[:, k:k + 1], muiv[:, k]), (core.ones[:, 0:1], mu2iv[:, k])]
                return accumulate(nc, bank[0:1, 0:E], terms)

            product_stage(core, [Job(losses, "dve", lambda bank: nc.vector.tensor_scalar(loss[:, 0], bank[0:1, 0:E], -1.0 / D, None, ALU.mult))])
            with stage(nc, "dve_step") as (block, dve_step):
                @block.vector
                def _(dve):
                    step = stepper(dve, dve_step)
                    step(nc.vector.reduce_max(least[:], loss[:], AX.X))
                    first_of_equal(nc, step, pick[:], loss[:], least[:], ties[:], counted[:], core.ones[0:1, 0:E])
            product_stage(core, [
                Job(lambda bank: nc.tensor.matmul(bank[:, 0:E], core.ones[0:1, 0:P], pick[:, 0], start=True, stop=True), "dve",
                    out_of_bank(core, "dve", everywhere[:])),
                Job(lambda bank: nc.tensor.matmul(bank[0:E, 0:1], pick[:, 0], core.ones[0:1, 0:1], start=True, stop=True), "dve",
                    out_of_bank(core, "dve", picked[:]))])
            with stage(nc, "dve_step") as (block, dve_step):
                @block.vector
                def _(dve):
                    step = stepper(dve, dve_step)
                    for e in range(E):
                        for to, of, p in ((wd[:], down[:, e], P), (wu[:, 0], up[:, e], R), (wc[:], conv[:, e], P)):
                            if e == 0:
                                step(nc.vector.tensor_scalar(to, of, everywhere[0:p, 0:1], None, ALU.mult))
                            else:
                                step(nc.vector.scalar_tensor_tensor(out=to, in0=of, scalar=everywhere[0:p, e:e + 1], in1=to, op0=ALU.mult, op1=ALU.add))

            def column(bias, cut, rows):
                return lambda bank: nc.tensor.matmul(bank[0:rows, 0:1], bias[:, cut], picked[:], start=True, stop=True)

            product_stage(core, [
                *turn_square(core, wc, wcT, DT, DT),
                Job(column(down_b, slice(0, R), R), "dve", out_of_bank(core, "dve", bd[:])),
                *[Job(column(up_b, slice(f * P, (f + 1) * P), P), "dve", out_of_bank(core, "dve", bu[:, f:f + 1])) for f in range(DT)],
                Job(lambda bank: nc.tensor.matmul(bank[0:1, 0:D], picked[:], conv_b[:], start=True, stop=True), "dve", out_of_bank(core, "dve", bc[:]))])
            product_stage(core, columns_out(core, wd, core.xT, hT, S, m=R, bias=bd, func=ACT.Relu, engines=("act",)))
            product_stage(core, columns_out(core, wu, hT, aT, S, bias=bu))

            def both(t):
                cut = slice(t * P, (t + 1) * P)
                terms = [(core.xT[:, k, cut], baseT[:, k]) for k in range(DT)] + [(aT[:, k, cut], wcT[:, k]) for k in range(DT)]
                terms += [(core.ones[0:1, 0:P], base_b[:]), (core.ones[0:1, 0:P], bc[:])]
                return lambda bank: accumulate(nc, bank[:, 0:D], terms)

            product_stage(core, [Job(both(t), *into(core, core.delta)(t)) for t in range(TT)])
            residual_norm(core, b)


def l3_attn(core, w):
    nc = core.nc
    L, CH, HD = 64, S // 64, 16
    with ExitStack() as ctx:
        sb = lambda name, shape: ctx.enter_context(nc.sbuf_tensor(core.named(name), shape, F32))
        wq, wk, wv = sb("wq", [P, DT, D]), sb("wk", [P, DT, D]), sb("wv", [P, DT, D])
        bq, bk, bv = sb("bq", [P, DT]), sb("bk", [P, DT]), sb("bv", [1, D])
        rq, rk, rv = sb("rq", [P, DT, L]), sb("rk", [P, DT, L]), sb("rv", [P, DT, L])
        rbq, rbk, rbv = sb("rbq", [L, 1]), sb("rbk", [L, 1]), sb("rbv", [1, L])
        v, rvr = sb("v", [P, TT, HEADS, value_slot(HD)]), sb("rvr", [L, 1, L // HD, value_slot(HD)])
        q_parts, k_parts = scratch_for(core, "q_parts", D, S), scratch_for(core, "k_parts", D, S)
        rq_parts, rk_parts = scratch_for(core, "rq_parts", L, S), scratch_for(core, "rk_parts", L, L)
        rout, rout_b = sb("rout", [L, 1, D]), sb("rout_b", [1, D])
        wo, bo = sb("wo", [P, DT, D]), sb("bo", [1, D])
        gl, gr = sb("gl", [P, HD]), sb("gr", [P, HD])
        some_key, some_chunk = sb("some_key", [P, TT]), sb("some_chunk", [P, TT])
        sb16 = lambda name, shape: ctx.enter_context(nc.sbuf_tensor(core.named(name), shape, BF16))
        before16, after16, chunks16 = sb16("before16", [P, P]), sb16("after16", [P, P]), sb16("chunks16", [P, TT, L])
        beforeT16, afterT16, chunksT16 = sb16("beforeT16", [P, P]), sb16("afterT16", [P, P]), sb16("chunksT16", [L, TT, P])
        qkv, qkv_b = w["L3_attn_qkv_w"], w["L3_attn_qkv_b"]
        load_stage(core, [
            (wq[:], matrix(qkv[:, 0:D])), (wk[:], matrix(qkv[:, D:2 * D])), (wv[:], matrix(qkv[:, 2 * D:3 * D])),
            (bq[:], columned(qkv_b[0:D])), (bk[:], columned(qkv_b[D:2 * D])), (bv[:], rowed(qkv_b[2 * D:3 * D])),
            (rq[:], matrix(w["L3_attn_rq_w"])), (rk[:], matrix(w["L3_attn_rkv_w"][:, 0:L])), (rv[:], matrix(w["L3_attn_rkv_w"][:, L:2 * L])),
            (rbq[:], columned(w["L3_attn_rq_b"], L)), (rbk[:], columned(w["L3_attn_rkv_b"][0:L], L)), (rbv[:], rowed(w["L3_attn_rkv_b"][L:2 * L])),
            (rout[:], matrix(w["L3_attn_rout_w"], L)), (rout_b[:], rowed(w["L3_attn_rout_b"])),
            (wo[:], matrix(w["L3_attn_out_w"])), (bo[:], rowed(w["L3_attn_out_b"])),
            (gl[:], spread_over(w["L3_attn_gl_w"].rearrange("a b -> (a b)"))), (gr[:], spread_over(w["L3_attn_gr_w"].rearrange("a b -> (a b)"))),
        ], zeroed=[v[:, :, :, HD + 1:], rvr[:, :, :, HD + 1:]], ones=[v[:, :, :, HD], rvr[:, :, :, HD]])
        with ExitStack() as early:
            eb = lambda name, shape: early.enter_context(nc.sbuf_tensor(core.named(name), shape, F32))
            square, chunks, chunksT = eb("square", [P, 4, P]), eb("chunks", [P, TT, L]), eb("chunksT", [L, TT, P])
            with stage(nc, "filled") as (block, filled):
                @block.gpsimd
                def _(pool):
                    for t, value in ((some_key, 1.0), (some_chunk, 1.0), (square, 0.0), (chunks, 0.0), (chunksT, 0.0)):
                        pool.memset(t[:], value).then_inc(filled, 1)
                    pool.wait_ge(filled, 5)
                    triangle(pool, square[:, 0], ALU.is_gt, 1).then_inc(filled, 1)
                    triangle(pool, square[:, 1], ALU.is_ge, -1).then_inc(filled, 1)
                    triangle(pool, square[:, 2], ALU.is_gt, -1).then_inc(filled, 1)
                    triangle(pool, square[:, 3], ALU.is_ge, 1).then_inc(filled, 1)
                    for q in range(TT):
                        pool.affine_select(out=chunks[:, q], in_=chunks[:, q], compare_op=ALU.is_ge, fill=MASKED, base=q * P - CH, pattern=[[-CH, L]], channel_multiplier=1).then_inc(filled, 1)
                        pool.affine_select(out=chunksT[:, q], in_=chunksT[:, q], compare_op=ALU.is_ge, fill=MASKED, base=q * P - CH, pattern=[[1, P]], channel_multiplier=-CH).then_inc(filled, 1)
                    pool.affine_select(out=some_key[:, 0:1], in_=some_key[:, 0:1], compare_op=ALU.is_gt, fill=0.0, base=0, pattern=[[0, 1]], channel_multiplier=1).then_inc(filled, 1)
                    pool.affine_select(out=some_chunk[:, 0:1], in_=some_chunk[:, 0:1], compare_op=ALU.is_ge, fill=0.0, base=-CH, pattern=[[0, 1]], channel_multiplier=1).then_inc(filled, 1)
                    pool.wait_ge(filled, 11 + 2 * TT)
                    for to, of in ((before16, square[:, 0]), (after16, square[:, 1]), (beforeT16, square[:, 2]), (afterT16, square[:, 3]),
                                   (chunks16, chunks[:]), (chunksT16, chunksT[:])):
                        pool.tensor_copy(to[:], of).then_inc(filled, 1)
                    pool.wait_ge(filled, 17 + 2 * TT)

        def local_blocks(q):
            return ([(q - 1, after16[:], afterT16[:])] if q else []) + [(q, before16[:], beforeT16[:])]

        o, oT, pooledT = sb("o", [P, TT, D]), sb("oT", [P, DT, S]), sb("pooledT", [P, DT, L])
        lat, latT, remote = sb("lat", [P, TT, L]), sb("latT", [L, 1, S]), sb("remote", [P, TT, D])
        gated, gate, gate2 = sb("gated", [P, TT * 16, HD]), sb("gate", [P, TT * 16]), sb("gate2", [P, TT * 16])
        local = Heads(k_parts, q_parts, v, o, HEADS, HEADS, HD, S, 0.25, local_blocks, valid=some_key, lag=3.6)
        local_buffers = attention_buffers(core, ctx, local)
        remote_heads = Heads(rk_parts, rq_parts, rvr, lat, L // HD, 4, HD, L, 0.25, lambda q: [(0, chunks16[:, q], chunksT16[:, q])], valid=some_chunk, lag=3.6)
        remote_heads_buffers = attention_buffers(core, ctx, remote_heads)
        with loop(nc, B) as b:
            take_turned_stage(core, b)
            with stage(nc, "dve_step") as (block, dve_step):
                @block.vector
                def _(dve):
                    step = stepper(dve, dve_step)
                    for k in range(DT):
                        step(nc.vector.reduce_sum(pooledT[:, k], core.xT[:, k].rearrange("p (l c) -> p l c", c=CH), AX.X))
                    step(nc.vector.tensor_scalar(pooledT[:], pooledT[:], 1.0 / CH, None, ALU.mult))
            with ExitStack() as early:
                split = Split(core, early, q=(DT, S), k=(DT, S), rq=(1, S), rk=(1, L))
                product_stage(core, [
                    *columns_out(core, wq, core.xT, split.x["q"], S, bias=bq), *columns_out(core, wk, core.xT, split.x["k"], S, bias=bk),
                    *rows_out(core, core.xT, wv, S, D, values_into(core, v, HD), bias_row=bv[:]),
                    *columns_out(core, rq, core.xT, split.x["rq"], S, m=L, bias=rbq), *columns_out(core, rk, pooledT, split.x["rk"], L, m=L, bias=rbk),
                    *rows_out(core, pooledT, rv, L, L, values_into(core, rvr, HD), bias_row=rbv[:])])
                split.store(core, q=q_parts, k=k_parts, rq=rq_parts, rk=rk_parts)
            attention(core, local, local_buffers)
            attention(core, remote_heads, remote_heads_buffers)

            def turn_lat(bank):
                for t in range(TT):
                    last = nc.tensor.transpose(bank[0:L, t * P:(t + 1) * P], lat[:, t], core.ident[:])
                return last

            product_stage(core, [Job(turn_lat, "dve", out_of_bank(core, "dve", latT[:, 0]))])
            product_stage(core, rows_out(core, latT, rout, S, D, into(core, remote), bias_row=rout_b[:]))
            with stage(nc, "dve_step", "logit_ready", "gate_ready") as (block, dve_step, logit_ready, gate_ready):
                by_head = lambda t: t[:].rearrange("p t (h s) -> p (t h) s", s=HD)
                wide = lambda t: t[:].unsqueeze(1).to_broadcast([P, TT * 16, HD])

                @block.vector
                def _(dve):
                    v_ = nc.vector
                    step = stepper(dve, dve_step)
                    step(v_.tensor_tensor(gated[:], by_head(o), wide(gl), ALU.mult))
                    step(v_.reduce_sum(gate[:], gated[:], AX.X))
                    step(v_.tensor_tensor(gated[:], by_head(remote), wide(gr), ALU.mult))
                    step(v_.reduce_sum(gate2[:], gated[:], AX.X))
                    v_.tensor_tensor(gate[:], gate[:], gate2[:], ALU.add).then_inc(logit_ready, 1)
                    step(v_.tensor_tensor(gated[:], by_head(o), by_head(remote), ALU.subtract))
                    dve.wait_ge(gate_ready, 1)
                    step(v_.tensor_tensor(gated[:], gated[:], gate[:].unsqueeze(2).to_broadcast([P, TT * 16, HD]), ALU.mult))
                    step(v_.tensor_tensor(by_head(o), gated[:], by_head(remote), ALU.add))

                @block.scalar
                def _(act):
                    act.wait_ge(logit_ready, 1)
                    nc.scalar.activation(gate[:], gate[:], ACT.Sigmoid).then_inc(gate_ready, 1)
            product_stage(core, turned(core, o, oT))
            product_stage(core, rows_out(core, oT, wo, S, D, into(core, core.delta), bias_row=bo[:]))
            residual_norm(core, b)


def l3_xattn(core, w, ctx_in):
    nc = core.nc
    with ExitStack() as ctx:
        sb = lambda name, shape: ctx.enter_context(nc.sbuf_tensor(core.named(name), shape, F32))
        wq, wk, wv = sb("wq", [P, DT, D]), sb("wk", [P, DT, D]), sb("wv", [P, DT, D])
        bq, bk, bv = sb("bq", [P, DT]), sb("bk", [P, DT]), sb("bv", [1, D])
        wo, bo = sb("wo", [P, DT, D]), sb("bo", [1, D])
        v = sb("v", [P, MT, HEADS, value_slot(D // HEADS)])
        q_parts, k_parts = scratch_for(core, "q_parts", D, S), scratch_for(core, "k_parts", D, M)
        load_stage(core, [
            (wq[:], matrix(w["L3_xattn_Wq"])), (wk[:], matrix(w["L3_xattn_Wk"])), (wv[:], matrix(w["L3_xattn_Wv"])),
            (bq[:], columned(w["L3_xattn_bq"])), (bk[:], columned(w["L3_xattn_bk"])), (bv[:], rowed(w["L3_xattn_bv"])),
            (wo[:], matrix(w["L3_xattn_Wo"])), (bo[:], rowed(w["L3_xattn_bo"])),
        ], zeroed=[v[:, :, :, 17:]], ones=[v[:, :, :, 16]])
        o, oT = sb("o", [P, TT, D]), sb("oT", [P, DT, S])
        heads = Heads(k_parts, q_parts, v, o, HEADS, HEADS, 16, M, 0.25, all_blocks(M))
        heads_buffers = attention_buffers(core, ctx, heads)
        with loop(nc, B) as b:
            with ExitStack() as early:
                ctxT = early.enter_context(nc.sbuf_tensor(core.named("ctxT"), [P, DT, M], F32))
                with ExitStack() as first:
                    inputs_stage(core, b, ctx_in, first.enter_context(nc.sbuf_tensor(core.named("ctx_rows"), [P, MT, D], F32)), ctxT)
                split = Split(core, early, q=(DT, S), k=(DT, M))
                product_stage(core, [
                    *columns_out(core, wq, core.xT, split.x["q"], S, bias=bq), *columns_out(core, wk, ctxT, split.x["k"], M, bias=bk),
                    *rows_out(core, ctxT, wv, M, D, values_into(core, v, 16), bias_row=bv[:])])
                split.store(core, q=q_parts, k=k_parts)
            attention(core, heads, heads_buffers)
            product_stage(core, turned(core, o, oT))
            product_stage(core, rows_out(core, oT, wo, S, D, into(core, core.delta), bias_row=bo[:]))
            residual_norm(core, b)


def l3_ffn(core, w):
    nc = core.nc
    FF = w["L3_ffn_w1"].shape[1]
    with ExitStack() as ctx:
        sb = lambda name, shape: ctx.enter_context(nc.sbuf_tensor(core.named(name), shape, F32))
        w1, b1 = sb("w1", [P, DT, FF]), sb("b1", [P, FF // P])
        w2, b2 = sb("w2", [P, FF // P, D]), sb("b2", [1, D])
        load_stage(core, [(w1[:], matrix(w["L3_ffn_w1"])), (b1[:], columned(w["L3_ffn_b1"])),
                          (w2[:], matrix(w["L3_ffn_w2"])), (b2[:], rowed(w["L3_ffn_b2"]))])
        hT = sb("hT", [P, FF // P, S])
        with loop(nc, B) as b:
            take_turned_stage(core, b)
            product_stage(core, columns_out(core, w1, core.xT, hT, S, bias=b1, func=ACT.Gelu, engines=("act",)))
            product_stage(core, rows_out(core, hT, w2, S, D, into(core, core.delta), bias_row=b2[:]))
            residual_norm(core, b)


def decoder(nc, w, out, layers=range(12)):
    with ExitStack() as ctx:
        core = Core(nc, ctx)
        constants_stage(core, w["x"])
        context = w["ctx_1024"]
        sublayers = [lambda: l0_attn(core, w), lambda: l0_xattn(core, w, context), lambda: l0_ffn(core, w),
                     lambda: l1_attn(core, w), lambda: l1_xattn(core, w, context), lambda: l1_ffn(core, w),
                     lambda: l2_attn(core, w), lambda: l2_xattn(core, w, context), lambda: l2_ffn(core, w),
                     lambda: l3_attn(core, w), lambda: l3_xattn(core, w, context), lambda: l3_ffn(core, w)]
        for n in layers:
            core.sublayer = f"l{n // 3}_{n % 3}"
            sublayers[n]()
        with stage(nc, "stored") as (block, stored):
            @block.sync
            def _(sp):
                for b in range(B):
                    sp.dma_start(out[b].rearrange("(t p) d -> p t d", p=P), core.x_all[:, b]).then_inc(stored, 16)
                sp.wait_ge(stored, 16 * B)


def kernel(**inputs):
    import numpy as _np
    import concourse.bacc as _bacc
    from concourse import mybir as _mybir
    from concourse.bass_utils import run_bass_kernel_spmd as _run

    nc = _bacc.Bacc("TRN2", target_bir_lowering=False, num_devices=1)
    arrays, args = {}, {}
    for name, value in inputs.items():
        a = _np.ascontiguousarray(value)
        arrays[name + "_dram"] = a
        args[name] = nc.dram_tensor(name + "_dram", a.shape, _mybir.dt.from_np(a.dtype), kind="ExternalInput").ap()
    out = nc.dram_tensor("out_dram", (B, S, D), F32, kind="ExternalOutput").ap()
    decoder(nc, args, out)
    return _run(nc, [arrays], core_ids=[0]).results[0]["out_dram"]
```
